# Optimizing a Trainium2 kernel written in Bass

```python
import numpy as np
import jax
import jax.numpy as jnp

def _softmax(x, axis=-1):
    return jax.nn.softmax(x, axis=axis)

def _gelu(x):
    return jax.nn.gelu(x, approximate=True)

def _silu(x):
    return jax.nn.silu(x)

def _sigmoid(x):
    return jax.nn.sigmoid(x)

def _layernorm(x, axis=-1, eps=1e-05):
    m = jnp.mean(x, axis=axis, keepdims=True)
    v = jnp.var(x, axis=axis, keepdims=True)
    return (x - m) / jnp.sqrt(v + eps)

def _scatter_add(tgt, idx, src, axis=0):
    return tgt.at[idx].add(src)

def _segment_sum(src, seg, n):
    return jax.ops.segment_sum(src, seg, n)
kernel_name = 'mk_gnn_resnorm_d4_gnn_r8_0b44c6'

def setup_inputs(seed: int=0):
    np.random.seed(seed)
    _w = jnp.asarray

    def _rec_inputs():
        import jax
        import jax.numpy as jnp
        _gk = jax.random.key(seed)
        x = -0.000202 + 1 * jax.random.normal(jax.random.fold_in(_gk, 1), (12500, 128), jnp.float32)
        src = jax.random.randint(jax.random.fold_in(_gk, 2), (200000,), 0, 12500, jnp.int32)
        dst = jnp.minimum((12500 * jax.random.uniform(jax.random.fold_in(_gk, 3), (200000,)) ** 2.0).astype(jnp.int32), 99999)
        _o = jnp.argsort(dst, stable=True)
        src = src[_o]
        dst = dst[_o]
        edge_attr_4 = jax.random.uniform(jax.random.fold_in(_gk, 11), (200000, 4), jnp.float32, 0.0, 1)
        edge_type_8 = jax.random.randint(jax.random.fold_in(_gk, 13), (200000,), 0, 8, jnp.int32)
        return (x, src, dst, edge_attr_4, edge_type_8)
    x, src, dst, edge_attr_4, edge_type_8 = _rec_inputs()

    def _L0_gnn_setup():
        import jax, jax.numpy as jnp
        import numpy as np
        N_NODES = 6250
        N_EDGES = 100000
        IN_DIM = 128
        OUT_DIM = 128
        NEG_SLOPE = 0.2
        key = jax.random.key(seed)
        k1, k2, k3, k4, k5 = jax.random.split(key, 5)
        x = jax.random.normal(k1, (N_NODES, IN_DIM), dtype=jnp.float32)
        edge_index = jax.random.randint(k2, (2, N_EDGES), 0, N_NODES, dtype=jnp.int64)
        W = jax.random.normal(k3, (IN_DIM, OUT_DIM), dtype=jnp.float32) * (1.0 / np.sqrt(IN_DIM))
        a_src = jax.random.normal(k4, (OUT_DIM,), dtype=jnp.float32) * (1.0 / np.sqrt(OUT_DIM))
        a_dst = jax.random.normal(k5, (OUT_DIM,), dtype=jnp.float32) * (1.0 / np.sqrt(OUT_DIM))
        bias = jnp.zeros((OUT_DIM,), dtype=jnp.float32)
        return {'x': x, 'edge_index': edge_index, 'W': W, 'a_src': a_src, 'a_dst': a_dst, 'bias': bias}
    _L0_gnn_all = _L0_gnn_setup()
    _L0_gnn_in = {k: v for k, v in _L0_gnn_all.items() if k in ('W', 'a_src', 'a_dst', 'bias')}
    del _L0_gnn_all

    def _L1_gnn_setup():
        import jax, jax.numpy as jnp
        import numpy as np
        N_NODES = 6250
        N_EDGES = 100000
        IN_DIM = 128
        OUT_DIM = 128
        HEADS = 4
        HEAD_DIM = OUT_DIM // HEADS
        NEG_SLOPE = 0.2
        LN_EPS = 1e-05
        key = jax.random.key(seed)
        ks = jax.random.split(key, 8)
        x = jax.random.normal(ks[0], (N_NODES, IN_DIM), dtype=jnp.float32)
        edge_index = jax.random.randint(ks[1], (2, N_EDGES), 0, N_NODES, dtype=jnp.int64)
        W = jax.random.normal(ks[2], (IN_DIM, HEADS * HEAD_DIM), dtype=jnp.float32) / np.sqrt(IN_DIM)
        att_src = jax.random.normal(ks[3], (HEADS, HEAD_DIM), dtype=jnp.float32) / np.sqrt(HEAD_DIM)
        att_dst = jax.random.normal(ks[4], (HEADS, HEAD_DIM), dtype=jnp.float32) / np.sqrt(HEAD_DIM)
        bias = jnp.zeros((OUT_DIM,), dtype=jnp.float32)
        gamma = jnp.ones((OUT_DIM,), dtype=jnp.float32)
        beta = jnp.zeros((OUT_DIM,), dtype=jnp.float32)
        return {'x': x, 'edge_index': edge_index, 'W': W, 'att_src': att_src, 'att_dst': att_dst, 'bias': bias, 'gamma': gamma, 'beta': beta}
    _L1_gnn_all = _L1_gnn_setup()
    _L1_gnn_in = {k: v for k, v in _L1_gnn_all.items() if k in ('W', 'att_src', 'att_dst', 'bias', 'gamma', 'beta')}
    del _L1_gnn_all

    def _L2_gnn_setup():
        import jax, jax.numpy as jnp
        import numpy as np
        N_NODES = 12500
        N_EDGES = 200000
        HIDDEN = 128
        N_ETYPES = 4
        N_STEPS = 4

        def _gru_cell(x, h, W_ih, W_hh, b_ih, b_hh):
            gi = x @ W_ih.T + b_ih
            gh = h @ W_hh.T + b_hh
            ir, iz, inn = jnp.split(gi, 3, axis=1)
            hr, hz, hn = jnp.split(gh, 3, axis=1)
            r = jax.nn.sigmoid(ir + hr)
            z = jax.nn.sigmoid(iz + hz)
            n = jnp.tanh(inn + r * hn)
            return (1.0 - z) * n + z * h
        key = jax.random.key(seed)
        ks = jax.random.split(key, 10)
        s = 1.0 / np.sqrt(HIDDEN)
        node_feat = jax.random.normal(ks[0], (N_NODES, HIDDEN), dtype=jnp.float32)
        edge_index = jax.random.randint(ks[1], (2, N_EDGES), 0, N_NODES)
        edge_feat = jax.random.uniform(ks[2], (N_EDGES, N_ETYPES), dtype=jnp.float32)
        W_edge = jax.random.uniform(ks[3], (N_ETYPES, HIDDEN, HIDDEN), minval=-s, maxval=s, dtype=jnp.float32)
        b_edge = jax.random.uniform(ks[4], (N_ETYPES, HIDDEN), minval=-s, maxval=s, dtype=jnp.float32)
        W_ih = jax.random.uniform(ks[5], (3 * HIDDEN, HIDDEN), minval=-s, maxval=s, dtype=jnp.float32)
        W_hh = jax.random.uniform(ks[6], (3 * HIDDEN, HIDDEN), minval=-s, maxval=s, dtype=jnp.float32)
        b_ih = jax.random.uniform(ks[7], (3 * HIDDEN,), minval=-s, maxval=s, dtype=jnp.float32)
        b_hh = jax.random.uniform(ks[8], (3 * HIDDEN,), minval=-s, maxval=s, dtype=jnp.float32)
        return {'node_feat': node_feat, 'edge_index': edge_index, 'edge_feat': edge_feat, 'W_edge': W_edge, 'b_edge': b_edge, 'W_ih': W_ih, 'W_hh': W_hh, 'b_ih': b_ih, 'b_hh': b_hh}
    _L2_gnn_all = _L2_gnn_setup()
    _L2_gnn_in = {k: v for k, v in _L2_gnn_all.items() if k in ('W_edge', 'b_edge', 'W_ih', 'W_hh', 'b_ih', 'b_hh')}
    del _L2_gnn_all

    def _L3_gnn_setup():
        import jax, jax.numpy as jnp
        import numpy as np
        N, E = (6250, 100000)
        IN, OUT, R, B = (128, 128, 8, 4)
        LN_EPS = 1e-05
        key = jax.random.key(seed)
        ks = jax.random.split(key, 9)
        x = jax.random.normal(ks[0], (N, IN), dtype=jnp.float32)
        edge_index = jax.random.randint(ks[1], (2, E), 0, N, dtype=jnp.int64)
        edge_type = jax.random.randint(ks[2], (E,), 0, R, dtype=jnp.int64)
        weight = jax.random.normal(ks[3], (B, IN, OUT), dtype=jnp.float32) * (2.0 / (IN + OUT)) ** 0.5
        alpha = jax.random.normal(ks[4], (R, B), dtype=jnp.float32) * (2.0 / (R + B)) ** 0.5
        bias = jnp.zeros((OUT,), dtype=jnp.float32)
        weight_self_loop = jax.random.normal(ks[5], (IN, OUT), dtype=jnp.float32) * (2.0 / (IN + OUT)) ** 0.5
        ln_gamma = jnp.ones((OUT,), dtype=jnp.float32)
        ln_beta = jnp.zeros((OUT,), dtype=jnp.float32)
        return {'x': x, 'edge_index': edge_index, 'edge_type': edge_type, 'weight': weight, 'alpha': alpha, 'bias': bias, 'weight_self_loop': weight_self_loop, 'ln_gamma': ln_gamma, 'ln_beta': ln_beta}
    _L3_gnn_all = _L3_gnn_setup()
    _L3_gnn_in = {k: v for k, v in _L3_gnn_all.items() if k in ('weight', 'alpha', 'bias', 'weight_self_loop', 'ln_gamma', 'ln_beta')}
    del _L3_gnn_all
    return {'x': x, 'src': src, 'dst': dst, 'edge_attr_4': edge_attr_4, 'edge_type_8': edge_type_8, 'L0_gnn_W': _L0_gnn_in['W'], 'L0_gnn_a_src': _L0_gnn_in['a_src'], 'L0_gnn_a_dst': _L0_gnn_in['a_dst'], 'L0_gnn_bias': _L0_gnn_in['bias'], 'L1_gnn_W': _L1_gnn_in['W'], 'L1_gnn_att_src': _L1_gnn_in['att_src'], 'L1_gnn_att_dst': _L1_gnn_in['att_dst'], 'L1_gnn_bias': _L1_gnn_in['bias'], 'L1_gnn_gamma': _L1_gnn_in['gamma'], 'L1_gnn_beta': _L1_gnn_in['beta'], 'L2_gnn_W_edge': _L2_gnn_in['W_edge'], 'L2_gnn_b_edge': _L2_gnn_in['b_edge'], 'L2_gnn_W_ih': _L2_gnn_in['W_ih'], 'L2_gnn_W_hh': _L2_gnn_in['W_hh'], 'L2_gnn_b_ih': _L2_gnn_in['b_ih'], 'L2_gnn_b_hh': _L2_gnn_in['b_hh'], 'L3_gnn_weight': _L3_gnn_in['weight'], 'L3_gnn_alpha': _L3_gnn_in['alpha'], 'L3_gnn_bias': _L3_gnn_in['bias'], 'L3_gnn_weight_self_loop': _L3_gnn_in['weight_self_loop'], 'L3_gnn_ln_gamma': _L3_gnn_in['ln_gamma'], 'L3_gnn_ln_beta': _L3_gnn_in['ln_beta']}

def reference(x, src, dst, edge_attr_4, edge_type_8, L0_gnn_W, L0_gnn_a_src, L0_gnn_a_dst, L0_gnn_bias, L1_gnn_W, L1_gnn_att_src, L1_gnn_att_dst, L1_gnn_bias, L1_gnn_gamma, L1_gnn_beta, L2_gnn_W_edge, L2_gnn_b_edge, L2_gnn_W_ih, L2_gnn_W_hh, L2_gnn_b_ih, L2_gnn_b_hh, L3_gnn_weight, L3_gnn_alpha, L3_gnn_bias, L3_gnn_weight_self_loop, L3_gnn_ln_gamma, L3_gnn_ln_beta):
    import jax
    import jax.numpy as jnp

    def _L0_gnn_ref(x, edge_index, W, a_src, a_dst, bias):
        import jax, jax.numpy as jnp
        import numpy as np
        N_NODES = 6250
        N_EDGES = 100000
        IN_DIM = 128
        OUT_DIM = 128
        NEG_SLOPE = 0.2
        N = x.shape[0]
        h = x @ W
        src, dst = (edge_index[0], edge_index[1])
        e_src = h @ a_src
        e_dst = h @ a_dst
        raw = jax.nn.leaky_relu(e_src[src] + e_dst[dst], negative_slope=NEG_SLOPE)
        per_recv_max = jax.ops.segment_max(raw, dst, num_segments=N)
        per_recv_max = jnp.where(jnp.isfinite(per_recv_max), per_recv_max, jnp.zeros_like(per_recv_max))
        exp = jnp.exp(raw - per_recv_max[dst])
        denom = jnp.maximum(jax.ops.segment_sum(exp, dst, num_segments=N), 1e-15)
        alpha = exp / denom[dst]
        msg = h[src] * alpha[:, None]
        agg = jax.ops.segment_sum(msg, dst, num_segments=N)
        return jax.nn.elu(agg + bias)

    def _L1_gnn_ref(x, edge_index, W, att_src, att_dst, bias, gamma, beta):
        import jax, jax.numpy as jnp
        import numpy as np
        N_NODES = 6250
        N_EDGES = 100000
        IN_DIM = 128
        OUT_DIM = 128
        HEADS = 4
        HEAD_DIM = OUT_DIM // HEADS
        NEG_SLOPE = 0.2
        LN_EPS = 1e-05
        N = x.shape[0]
        loop = jnp.arange(N, dtype=edge_index.dtype)
        src = jnp.concatenate([edge_index[0], loop])
        dst = jnp.concatenate([edge_index[1], loop])
        h = (x @ W).reshape(N, HEADS, HEAD_DIM)
        a_s = jnp.einsum('nhd,hd->nh', h, att_src)
        a_d = jnp.einsum('nhd,hd->nh', h, att_dst)
        e = jax.nn.leaky_relu(a_s[src] + a_d[dst], NEG_SLOPE)
        e_max = jax.ops.segment_max(e, dst, num_segments=N)
        e_exp = jnp.exp(e - e_max[dst])
        denom = jax.ops.segment_sum(e_exp, dst, num_segments=N)
        alpha = e_exp / (denom[dst] + 1e-16)
        msg = h[src] * alpha[..., None]
        out = jax.ops.segment_sum(msg, dst, num_segments=N)
        out = out.reshape(N, HEADS * HEAD_DIM) + bias
        mu = out.mean(-1, keepdims=True)
        var = ((out - mu) ** 2).mean(-1, keepdims=True)
        out = (out - mu) * jax.lax.rsqrt(var + LN_EPS) * gamma + beta
        return jax.nn.gelu(out, approximate=False)

    def _L2_gnn_ref(node_feat, edge_index, edge_feat, W_edge, b_edge, W_ih, W_hh, b_ih, b_hh):
        import jax, jax.numpy as jnp
        import numpy as np
        N_NODES = 12500
        N_EDGES = 200000
        HIDDEN = 128
        N_ETYPES = 4
        N_STEPS = 4

        def _gru_cell(x, h, W_ih, W_hh, b_ih, b_hh):
            gi = x @ W_ih.T + b_ih
            gh = h @ W_hh.T + b_hh
            ir, iz, inn = jnp.split(gi, 3, axis=1)
            hr, hz, hn = jnp.split(gh, 3, axis=1)
            r = jax.nn.sigmoid(ir + hr)
            z = jax.nn.sigmoid(iz + hz)
            n = jnp.tanh(inn + r * hn)
            return (1.0 - z) * n + z * h
        etypes = jnp.argmax(edge_feat, axis=1)
        src, dst = (edge_index[0], edge_index[1])
        N = node_feat.shape[0]
        h = node_feat
        for _ in range(N_STEPS):
            trans = jnp.einsum('nd,tod->tno', h, W_edge) + b_edge[:, None, :]
            msg = trans[etypes, src]
            a = jax.ops.segment_sum(msg, dst, num_segments=N)
            h = _gru_cell(a, h, W_ih, W_hh, b_ih, b_hh)
        return h

    def _L3_gnn_ref(x, edge_index, edge_type, weight, alpha, bias, weight_self_loop, ln_gamma, ln_beta):
        import jax, jax.numpy as jnp
        import numpy as np
        N, E = (6250, 100000)
        IN, OUT, R, B = (128, 128, 8, 4)
        LN_EPS = 1e-05
        n = x.shape[0]
        row, col = (edge_index[0], edge_index[1])
        ones = jnp.ones((edge_type.shape[0],), dtype=x.dtype)
        deg = jax.ops.segment_sum(ones, row, num_segments=n)
        inv_deg = jnp.where(deg > 0, 1.0 / deg, 0.0)
        ew = inv_deg[row]
        W = jnp.einsum('rb,bio->rio', alpha, weight)
        h = jnp.einsum('ni,rio->rno', x, W)
        msg = ew[:, None] * h[edge_type, col]
        agg = jax.ops.segment_sum(msg, row, num_segments=n)
        mu = jnp.mean(agg, axis=-1, keepdims=True)
        var = jnp.var(agg, axis=-1, keepdims=True)
        out = (agg - mu) / jnp.sqrt(var + LN_EPS) * ln_gamma + ln_beta
        out = out + bias
        out = out + x @ weight_self_loop
        return out
    edge_index = jnp.stack([src, dst])
    x = _layernorm(x + _L0_gnn_ref(x, edge_index, L0_gnn_W, L0_gnn_a_src, L0_gnn_a_dst, L0_gnn_bias), axis=-1)
    x = _layernorm(x + _L1_gnn_ref(x, edge_index, L1_gnn_W, L1_gnn_att_src, L1_gnn_att_dst, L1_gnn_bias, L1_gnn_gamma, L1_gnn_beta), axis=-1)
    x = _layernorm(x + _L2_gnn_ref(x, edge_index, edge_attr_4, L2_gnn_W_edge, L2_gnn_b_edge, L2_gnn_W_ih, L2_gnn_W_hh, L2_gnn_b_ih, L2_gnn_b_hh), axis=-1)
    x = _layernorm(x + _L3_gnn_ref(x, edge_index, edge_type_8, L3_gnn_weight, L3_gnn_alpha, L3_gnn_bias, L3_gnn_weight_self_loop, L3_gnn_ln_gamma, L3_gnn_ln_beta), axis=-1)
    return x

_drawn_inputs = setup_inputs


def setup_inputs(seed=0):
    import zlib

    import numpy as np

    out = dict(_drawn_inputs(seed))
    spreads = {'L0_gnn_bias': (0.0, 0.1),
     'L1_gnn_bias': (0.0, 0.1),
     'L1_gnn_gamma': (1.0, 0.2),
     'L1_gnn_beta': (0.0, 0.1),
     'L3_gnn_bias': (0.0, 0.1),
     'L3_gnn_ln_gamma': (1.0, 0.2),
     'L3_gnn_ln_beta': (0.0, 0.1)}
    factors = {}
    for name, (base, spread) in spreads.items():
        noise = np.random.default_rng([zlib.crc32(name.encode()), seed]).standard_normal(out[name].shape)
        drawn = base * np.exp(spread * noise) if base else spread * noise
        out[name] = jnp.asarray(drawn.astype(out[name].dtype))
    for name, factor in factors.items():
        out[name] = (out[name] * factor).astype(out[name].dtype)
    return out
```

```python
import concourse.bass as bass
from concourse import mybir
from contextlib import ExitStack

F32 = mybir.dt.float32
BF16 = mybir.dt.bfloat16
I32 = mybir.dt.int32
U32 = mybir.dt.uint32
ALU = mybir.AluOpType
ACT = mybir.ActivationFunctionType
AX = mybir.AxisListType

P = 128
N = 12500
E = 200000
D = 128
NBLK = -(-N // P)
NPAD = NBLK * P
ECOL = -(-E // P)
ELAST = E - (P - 1) * ECOL
SCOL = 8
ECH = 4
C = -(-ECOL // (2 * SCOL)) * 2 * SCOL
CW = C // ECH
GRP = 4
RING = 4
BODY = GRP * RING
T = -(-((E + NBLK * (P - 1)) // P) // BODY) * BODY
NG = T // GRP
NI = T // BODY
H1 = 4
HD = D // H1
NET = 4
NREL = 8
NBASE = 4
STEPS = 4
NPB = 7
NPI = NBLK // NPB
TBI = NBLK // 2
GW = 256
GI = NPAD // GW
BIG = 1e30
DUMMY = N
WROW = D + H1
EPS = 1e-5
SLOPE = 0.2
MW = T // 4
SCI = C // (2 * SCOL)
ASK = [0, 3 * NPI, 9 * NPI, 11 * NPI]
assert NBLK % (2 * NPB) == 0 and C >= ECOL and MW <= 512 and NPAD % GW == 0


def wait(eng, sem, value):
    if isinstance(value, int) and value <= 0:
        return
    eng.wait_ge(sem, value)


def steps(eng, count, body, peel=False):
    if peel:
        body(0)
    with eng.Fori(1 if peel else 0, count) as i:
        body(i)


def following(i, q):
    return (i, q + 1) if q < RING - 1 else (i + 1, 0)


def before(i, q):
    return (i, q - 1) if q else (i - 1, RING - 1)


class Chain:

    def __init__(self, eng, sem):
        self.eng, self.sem, self.n = eng, sem, 0

    def done(self, ins):
        ins.then_inc(self.sem, 1)
        self.n += 1
        return ins

    def wait(self):
        wait(self.eng, self.sem, self.n)

    def restart(self):
        self.wait()
        if self.n:
            self.eng.sem_clear(self.sem)
        self.n = 0


def build(nc, x, src, dst, edge_attr_4, edge_type_8,
          L0_gnn_W, L0_gnn_a_src, L0_gnn_a_dst, L0_gnn_bias,
          L1_gnn_W, L1_gnn_att_src, L1_gnn_att_dst, L1_gnn_bias, L1_gnn_gamma, L1_gnn_beta,
          L2_gnn_W_edge, L2_gnn_b_edge, L2_gnn_W_ih, L2_gnn_W_hh, L2_gnn_b_ih, L2_gnn_b_hh,
          L3_gnn_weight, L3_gnn_alpha, L3_gnn_bias, L3_gnn_weight_self_loop, L3_gnn_ln_gamma, L3_gnn_ln_beta,
          out):
    ctx = ExitStack()
    with ctx:
        def sb(name, shape, dt=F32):
            return ctx.enter_context(nc.sbuf_tensor(name, shape, dt))

        def sem(name):
            return ctx.enter_context(nc.semaphore(name))

        def dram(name, shape, dt=F32):
            return nc.dram_tensor(name, shape, dt, kind="Internal").ap()

        rec_dst = dram("rec_dst", [P * T + P * C, 3], I32)
        rec_src = dram("rec_src", [P * T + P * C, 2], I32)
        tab0 = dram("tab0", [NPAD, D + 1])
        tab1 = dram("tab1", [NPAD, D + H1])
        tab2 = dram("tab2", [NPAD * NET, D])
        tab3 = dram("tab3", [NPAD * NREL, D])

        X = sb("X", [P, NBLK, D])
        HT = sb("HT", [P, NPAD])
        ACC = sb("ACC", [P, NBLK, WROW])
        ACCT = ACC[:, :, :].rearrange("p b w -> p (b w)")[:, 0:NPAD]
        G = sb("G", [P, BODY, WROW])
        STG = sb("STG", [P, 2, NREL * D])
        DOH = STG[:, :, :].rearrange("p a b -> p (a b)")[:, 0:BODY * P].rearrange("p (a b) -> p a b", b=P)
        node_tmp = sb("node_tmp", [P, NPB * (D + WROW)])
        T1 = node_tmp[:, 0:NPB * D].rearrange("p (a b) -> p a b", b=D)
        T2 = node_tmp[:, NPB * D:].rearrange("p (a b) -> p a b", b=WROW)
        DTS = node_tmp[:, 0:2 * GRP * P].rearrange("p (a b) -> p a b", a=2)
        NEG = node_tmp[:, 2 * GRP * P:3 * GRP * P].bitcast(BF16).rearrange("p (a j e) -> p a j e", a=2, j=GRP)
        by_layer = sb("by_layer", [P, (NREL + 1 + NET + 6 + NBASE) * D])

        def part(width):
            taken[0] += width
            return by_layer[:, taken[0] - width:taken[0]]
        taken = [0]
        LIM = part(T)
        ME = part(NBLK * H1).rearrange("p (b h) -> p b h", h=H1)
        ED = part(NBLK * H1).rearrange("p (b h) -> p b h", h=H1)
        taken[0] = 0
        wide_w = part((NREL + 1) * D)
        wide_b = part(NET * D)
        w_ih = part(3 * D)
        w_hh = part(3 * D)
        raw_w = part(NBASE * D)
        REC = sb("REC", [P, RING, GRP, 3], I32)
        ident = sb("ident", [P, P])
        identb = sb("identb", [P, P], BF16)
        ones = sb("ones", [P, P])
        lower = sb("lower", [P, P])
        iota = sb("iota", [P, P])
        iotai = sb("iotai", [P, P], I32)
        maskc = sb("maskc", [P, 1])
        tile_blocks = sb("tile_blocks", [33, T], I32)
        blk_d, blk_s = tile_blocks[0:1, :], tile_blocks[32:33, :]
        w_ext = sb("w_ext", [P, D + 2 * H1])
        w_t = sb("w_t", [P, D])
        att = sb("att", [P, 2 * H1])
        bias_b = sb("bias_b", [P, D])
        gamma_b = sb("gamma_b", [P, D])
        beta_b = sb("beta_b", [P, D])
        b_gru = sb("b_gru", [P, 6])
        b_rz = sb("b_rz", [P, 2])
        alpha_b = sb("alpha_b", [P, NREL * NBASE])
        XS = sb("XS", [P, 2, D])
        XT = sb("XT", [P, 2, D])
        SM = sb("SM", [P, 3, NPB])
        SA = sb("SA", [P, 3, NPB * H1])
        SC = sb("SC", [P, 3, NPB * H1])
        SD = sb("SD", [P, 2, NPB * H1])
        ESB = sb("ESB", [P, 2, GRP, H1], BF16)
        TMAX = sb("TMAX", [P, GRP, H1])
        NEW = sb("NEW", [P, GRP + 1, H1])
        NO = sb("NO", [P, 2, GRP, H1])
        NO2 = sb("NO2", [P, 2, GRP, H1])
        EDM = sb("EDM", [P, 2, GRP, 2, H1])
        FAC = sb("FAC", [P, 2, GRP, H1])
        FEX = sb("FEX", [P, 2, GRP, H1])
        SE = sb("SE", [P, GRP, H1])
        SE2 = sb("SE2", [P, GRP, H1])

        accf = ACC[:, :, :].rearrange("p b w -> p (b w)")
        xf = X[:, :, :].rearrange("p b w -> p (b w)")
        src_i = accf[:, 0 * C:1 * C].bitcast(I32)
        dst_i = accf[:, 1 * C:2 * C].bitcast(I32)
        typ_i = accf[:, 2 * C:3 * C].bitcast(I32)
        bkt = accf[:, 3 * C:4 * C]
        tmp_a = accf[:, 4 * C:5 * C]
        tmp_b = accf[:, 5 * C:6 * C]
        m_sel = accf[:, 6 * C:6 * C + T]
        attr = HT[:, 0:4 * C].rearrange("p (c f) -> p c f", f=4)
        rec1 = HT[:, 4 * C:8 * C].bitcast(I32).rearrange("p (c f) -> p c f", f=4)
        rec2 = HT[:, 0:3 * C].bitcast(I32).rearrange("p (c f) -> p c f", f=3)
        assert 8 * C <= NPAD and 6 * C + T <= NBLK * WROW
        iota_t = xf[:, 0:T]
        iota_ti = xf[:, T:2 * T].bitcast(I32)
        trash = xf[:, 2 * T:2 * T + C].bitcast(I32)
        zeros = xf[:, 2 * T + C:2 * T + 2 * C]
        eq = xf[:, 2 * T + 2 * C:2 * T + 3 * C]
        pre = xf[:, 2 * T + 3 * C:2 * T + 4 * C]
        emp = xf[:, 2 * T + 4 * C:2 * T + 4 * C + 3 * MW].bitcast(I32).rearrange("p (c f) -> p c f", f=3)
        small = xf[:, 2 * T + 4 * C + 3 * MW:]
        CNT, BAS = small[:, 0:NBLK], small[:, NBLK:2 * NBLK]
        TOT = small[:, 2 * NBLK:5 * NBLK].rearrange("p (k b) -> p k b", k=3)
        TIL = small[:, 5 * NBLK:6 * NBLK].bitcast(I32)
        ENDC = small[:, 6 * NBLK:6 * NBLK + 1]
        STGS = sb("STGS", [P, 2, SCOL, 4], I32)
        STG2 = sb("STG2", [P, 2, SCOL, 3], I32)

        PS = [ctx.enter_context(nc.psum_tensor(f"PS{i}", [P, 512], F32)) for i in range(8)]

        s_ints = sem("s_ints")
        s_const = sem("s_const")
        s_consts2 = sem("s_consts2")
        s_key = sem("s_key")
        s_empty = sem("s_empty")
        s_emp0 = sem("s_emp0")
        s_cnt = sem("s_cnt")
        s_pre = sem("s_pre")
        s_end = sem("s_end")
        s_endt = sem("s_endt")
        s_sel = sem("s_sel")
        s_blk = sem("s_blk")
        s_blkc = sem("s_blkc")
        s_pos = sem("s_pos")
        s_stage = [sem(f"s_stage{i}") for i in range(2)]
        s_scat = [sem(f"s_scat{i}") for i in range(2)]
        s_x = sem("s_x")
        s_xz = sem("s_xz")
        s_w = sem("s_w")
        s_wp = sem("s_wp")
        s_wa = sem("s_wa")
        s_wv = sem("s_wv")
        s_acc0 = sem("s_acc0")
        s_rec = [sem(f"s_rec{i}") for i in range(RING)]
        s_gath = [sem(f"s_gath{i}") for i in range(RING)]
        s_hot = sem("s_hot")
        s_neg = sem("s_neg")
        s_dt = sem("s_dt")
        s_dts = sem("s_dts")
        s_v = sem("s_v")
        s_red = sem("s_red")
        s_m = sem("s_m")
        s_fe = sem("s_fe")
        s_eb = sem("s_eb")
        s_se = sem("s_se")
        s_pe = sem("s_pe")
        s_msg = sem("s_msg")
        s_sum = sem("s_sum")
        s_add = sem("s_add")
        s_turn = sem("s_turn")
        s_xs = sem("s_xs")
        s_t = sem("s_t")
        s_xt = sem("s_xt")
        s_mm = sem("s_mm")
        s_ev = sem("s_ev")
        s_tab = [sem(f"s_tab{i}") for i in range(2)]
        s_np = sem("s_np")
        s_na = sem("s_na")
        s_hr = sem("s_hr")
        s_hru = sem("s_hru")
        s_xr = sem("s_xr")
        s_g = sem("s_g")
        s_gr = sem("s_gr")
        s_gt = sem("s_gt")
        s_gn = sem("s_gn")
        s_gh = sem("s_gh")
        s_on = sem("s_on")
        s_out = sem("s_out")
        s_cv = sem("s_cv")
        s_ca = sem("s_ca")
        s_cp = sem("s_cp")
        s_tb_all = sem("s_tb_all")
        s_ht = sem("s_ht")
        s_xa = sem("s_xa")

        block = ctx.enter_context(nc.Block())


        def bcast(ap, n):
            return ap.unsqueeze(2).to_broadcast([ap.shape[0], ap.shape[1], n])

        def row_of(vec):
            return vec.rearrange("(a n) -> a n", a=1).to_broadcast([P, vec.shape[0]])

        W0 = 4 * 16
        W1 = W0 + (4 + 2 * H1) * 16
        W2M = W1 + (NET + 6) * 16
        W2 = W2M + (6 + NET) * 16
        W3 = W2 + (NBASE + 5) * 16
        full = (P - 1) * ECOL
        full_b = N // P

        @block.sync
        def _(sp):
            sp.wait_ge(s_key, 1)
            for vec, tile in ((dst, dst_i), (src, src_i), (edge_type_8, typ_i)):
                sp.dma_start(tile[0:P - 1, 0:ECOL], vec[0:full].rearrange("(p c) -> p c", p=P - 1)).then_inc(s_ints, 16)
                sp.dma_start(tile[P - 1:P, 0:ELAST], vec[full:E].rearrange("(p c) -> p c", p=1)).then_inc(s_ints, 16)
            sp.dma_start(attr[0:P - 1, 0:ECOL, :],
                         edge_attr_4[0:full, :].rearrange("(p c) f -> p c f", p=P - 1)).then_inc(s_ints, 16)
            sp.dma_start(attr[P - 1:P, 0:ELAST, :],
                         edge_attr_4[full:E, :].rearrange("(p c) f -> p c f", p=1)).then_inc(s_ints, 16)

            def prefill(recs, words, ready):
                sp.wait_ge(s_emp0, ready)
                view = recs[0:P * T, :].rearrange("(p t) f -> p t f", p=P)
                for k in range(4):
                    sp.dma_start(view[:, k * MW:(k + 1) * MW, :], emp[:, :, words]).then_inc(s_empty, 16)

            prefill(rec_dst, slice(0, 3), 1)
            prefill(rec_src, slice(1, 3), 2)

            def load_w(pairs):
                for tile, ap in pairs:
                    sp.dma_start(tile, ap).then_inc(s_w, 16)

            load_w([(w_ext[:, 0:D], L0_gnn_W), (att[:, 0:1], L0_gnn_a_src.rearrange("(n a) -> n a", a=1)),
                    (att[:, 1:2], L0_gnn_a_dst.rearrange("(n a) -> n a", a=1)), (bias_b[:, :], row_of(L0_gnn_bias))])

            def stage_columns(key, recs, stage, width):
                flat = recs.rearrange("p c f -> p (c f)")

                def body(i):
                    for s in range(2):
                        wait(sp, s_scat[s], (i + key * SCI) * (16 * SCOL))
                        sp.dma_start(stage[:, s, :, :].rearrange("p c f -> p (c f)"),
                                     flat[:, bass.ds((i * 2 + s) * (SCOL * width), SCOL * width)]
                                     ).then_inc(s_stage[s], 16)
                steps(sp, SCI, body, peel=(key == 0))

            sp.wait_ge(s_pos, 1)
            stage_columns(0, rec1, STGS, 4)
            sp.wait_ge(s_pos, 2)
            sp.wait_ge(s_xz, 1)
            sp.dma_start(X[:, 0:full_b, :], x[0:full_b * P, :].rearrange("(b p) f -> p b f", p=P)).then_inc(s_x, 16)
            sp.dma_start(X[0:N - full_b * P, full_b, :], x[full_b * P:N, :]).then_inc(s_x, 16)
            stage_columns(1, rec2, STG2, 3)
            for s in range(2):
                sp.wait_ge(s_scat[s], 2 * SCI * SCOL * 16)

            def store_table(n, table, rows):
                width = table.shape[1] * rows

                def body(i):
                    for q in range(2):
                        sp.wait_ge(s_ev, i * 2 + (n * NBLK + (q + 1)))
                        sp.dma_start(table[bass.ds((i * 2 + q) * (P * rows), P * rows), :]
                                     .rearrange("(p r) f -> p (r f)", p=P), STG[:, q, 0:width]).then_inc(s_tab[q], 16)
                steps(sp, TBI, body)
                for q in range(2):
                    sp.wait_ge(s_tab[q], (n + 1) * (16 * TBI))
                    sp.sem_inc(s_turn, 1)
                sp.sem_inc(s_tb_all, 1)

            def load_records(n, recs, width):
                view = recs[0:P * T, :].rearrange("(p t) f -> p t f", p=P)

                def body(i):
                    for q in range(RING):
                        wait(sp, s_gath[q], (n * NI + i) * (16 * GRP))
                        sp.sem_inc(s_turn, 1)
                        wait(sp, s_hot, i * RING + (n * NG + (q + 1 - RING)))
                        sp.dma_start(REC[:, q, :, 3 - width:3],
                                     view[:, bass.ds(i * BODY + q * GRP, GRP), :]).then_inc(s_rec[q], 16)
                steps(sp, NI, body, peel=(isinstance(n, int) and n == 0))

            store_table(0, tab0, 1)
            load_records(0, rec_dst, 3)
            sp.wait_ge(s_xr, 1)
            load_w([(w_ext[:, 0:D], L1_gnn_W), (bias_b[:, :], row_of(L1_gnn_bias)),
                    (gamma_b[:, :], row_of(L1_gnn_gamma)), (beta_b[:, :], row_of(L1_gnn_beta))] +
                   [(att[h * HD:(h + 1) * HD, o + h:o + h + 1], a[h, :].rearrange("(n a) -> n a", a=1))
                    for o, a in ((0, L1_gnn_att_src), (H1, L1_gnn_att_dst)) for h in range(H1)])
            store_table(1, tab1, 1)
            load_records(1, rec_dst, 3)
            rows1 = tab1.rearrange("(b p) w -> p b w", p=P)

            def own_rows(i):
                sp.wait_ge(s_hru, i + 1)
                sp.dma_start(T2[:, :, :], rows1[:, bass.ds(i * NPB, NPB), :]).then_inc(s_hr, 16)
            steps(sp, NPI, own_rows)
            sp.wait_ge(s_xr, 2)
            raws = [L2_gnn_W_edge[t, :, :] for t in range(NET)] + \
                   [m[g * D:(g + 1) * D, :] for m in (L2_gnn_W_ih, L2_gnn_W_hh) for g in range(3)]
            for k, m in enumerate(raws):
                load_w([(raw_w[:, 0:D], m)])
                sp.wait_ge(s_wp, 2 + k + 1)
            load_w([(b_gru[:, 3 * k + g:3 * k + g + 1], b[g * D:(g + 1) * D].rearrange("(n a) -> n a", a=1))
                    for k, b in enumerate((L2_gnn_b_ih, L2_gnn_b_hh)) for g in range(3)] +
                   [(wide_b[:, t * D:(t + 1) * D], row_of(L2_gnn_b_edge[t, :])) for t in range(NET)])
            with sp.Fori(0, STEPS) as st:
                store_table(st + 2, tab2, NET)
                load_records(st + 2, rec_dst, 3)
            sp.wait_ge(s_xr, 3)
            load_w([(raw_w[:, b * D:(b + 1) * D], L3_gnn_weight[b, :, :]) for b in range(NBASE)] +
                   [(alpha_b[:, :], row_of(L3_gnn_alpha.rearrange("r b -> (r b)"))),
                    (wide_w[:, NREL * D:(NREL + 1) * D], L3_gnn_weight_self_loop),
                    (bias_b[:, :], row_of(L3_gnn_bias)), (gamma_b[:, :], row_of(L3_gnn_ln_gamma)),
                    (beta_b[:, :], row_of(L3_gnn_ln_beta))])
            store_table(6, tab3, NREL)
            load_records(6, rec_src, 2)
            sp.wait_ge(s_on, 1)
            sp.dma_start(out[0:full_b * P, :].rearrange("(b p) f -> p b f", p=P), X[:, 0:full_b, :]).then_inc(s_out, 16)
            sp.dma_start(out[full_b * P:N, :], X[0:N - full_b * P, full_b, :]).then_inc(s_out, 16)
            sp.wait_ge(s_out, 32)

        @block.gpsimd
        def _(pool):
            ch = Chain(pool, s_cp)
            ch.done(pool.memset(ident[:, :], 0.0))
            ch.done(pool.memset(lower[:, :], 1.0))
            ch.done(pool.memset(maskc[:, :], 1.0))
            ch.done(pool.memset(ones[:, :], 1.0))
            ch.wait()
            ch.done(pool.affine_select(out=ident[:, :], in_=ident[:, :], compare_op=ALU.not_equal, fill=1.0,
                                       base=0, pattern=[[-1, P]], channel_multiplier=1))
            ch.done(pool.affine_select(out=lower[:, :], in_=lower[:, :], compare_op=ALU.is_gt, fill=0.0,
                                       base=0, pattern=[[1, P]], channel_multiplier=-1))
            ch.done(pool.affine_select(out=maskc[:, :], in_=maskc[:, :], compare_op=ALU.is_gt, fill=0.0,
                                       base=N - (NBLK - 1) * P, pattern=[[0, 1]], channel_multiplier=-1))
            ch.done(pool.iota(iotai[:, :], pattern=[[1, P]], base=0, channel_multiplier=0))
            ch.done(pool.iota(iota_ti, pattern=[[1, T]], base=0, channel_multiplier=0))
            ch.done(pool.iota(trash, pattern=[[1, C]], base=P * T, channel_multiplier=C))
            ch.wait()
            pool.sem_inc(s_const, 1)

            def scatter(key, recs, stage, width):
                def body(i):
                    for s in range(2):
                        pool.wait_ge(s_stage[s], (i + (key * SCI + 1)) * 16)
                        pool.sem_inc(s_turn, 1)
                        for c in range(SCOL):
                            pool.indirect_dma_start(
                                recs, bass.IndirectOffsetOnAxis(stage[:, s, c, 0:1], 0),
                                stage[:, s, c, 1:width], None).then_inc(s_scat[s], 16)
                steps(pool, SCI, body)

            pool.wait_ge(s_empty, 8 * 16)
            scatter(0, rec_dst, STGS, 4)
            scatter(1, rec_src, STG2, 3)

            def gather(n, table, word):
                width = table.shape[1]
                pool.wait_ge(s_tb_all, n + 1)
                pool.sem_inc(s_turn, 1)

                def body(i):
                    for q in range(RING):
                        pool.wait_ge(s_rec[q], (n * NI + i + 1) * 16)
                        pool.sem_inc(s_turn, 1)
                        wait(pool, s_sum, i * RING + (n * NG + (q + 1 - RING)))
                        pool.sem_inc(s_turn, 1)
                        for j in range(GRP):
                            pool.indirect_dma_start(
                                G[:, q * GRP + j, 0:width], None, table,
                                bass.IndirectOffsetOnAxis(REC[:, q, j, word:word + 1], 0)).then_inc(s_gath[q], 16)
                steps(pool, NI, body, peel=(isinstance(n, int) and n == 0))

            gather(0, tab0, 0)
            gather(1, tab1, 0)
            with pool.Fori(0, STEPS) as st:
                gather(st + 2, tab2, 1)
            gather(6, tab3, 1)

        @block.tensor
        def _(pe):
            mm, tr = nc.tensor.matmul, nc.tensor.transpose
            pe.wait_ge(s_const, 1)
            for key in range(2):
                pe.wait_ge(s_cnt, key + 1)
                mm(PS[0][:, 0:NBLK], lower[:, :], CNT[:, :], start=True, stop=True)
                mm(PS[0][:, P:P + NBLK], ones[:, :], CNT[:, :], start=True, stop=True).then_inc(s_pre, 1)
                pe.wait_ge(s_end, key + 1)
                tr(PS[1][0:NBLK, 0:P], TOT[:, 1, :], ident[:, :]).then_inc(s_endt, 1)
                pe.wait_ge(s_sel, key + 1)
                for k in range(4):
                    wait(pe, s_blkc, key * 4 + k)
                    mm(PS[2][:, 0:MW], ones[0:NBLK, :], m_sel[0:NBLK, k * MW:(k + 1) * MW],
                       start=True, stop=True).then_inc(s_blk, 1)

            def attention_weights(n, heads, loaded):
                pe.wait_ge(s_w, loaded)
                tr(PS[3][:, 0:D], w_ext[:, 0:D], ident[:, :]).then_inc(s_wp, 1)
                pe.wait_ge(s_wv, 2 * n + 1)
                mm(PS[3][:, P:P + 2 * heads], w_t[:, :], att[:, 0:2 * heads], start=True, stop=True).then_inc(s_wa, 1)
                pe.wait_ge(s_wv, 2 * n + 2)

            def turn_block(turn, i, q):
                pe.wait_ge(s_xs, i * 2 + (turn * NBLK + q + 1))
                tr(PS[q][:, 0:D], XS[:, q, :], ident[:, :]).then_inc(s_t, 1)

            def table(n, turn, rhs, width):
                def body(i):
                    for q in range(2):
                        if turn is not None:
                            turn_block(turn, i, q)
                        pe.wait_ge(s_xt, i * 2 + (n * NBLK + (q + 1)))
                        wait(pe, s_ev, i * 2 + (n * NBLK + (q - 1)))
                        for k in range(-(-width // 512)):
                            w = min(512, width - 512 * k)
                            last = mm(PS[2 + 3 * q + k][:, 0:w], XT[:, q, :], rhs[:, 512 * k:512 * k + w],
                                      start=True, stop=True)
                        last.then_inc(s_mm, 1)
                steps(pe, TBI, body, peel=(isinstance(n, int) and n == 0))

            def attention(n, heads):
                def turn(i, q):
                    wait(pe, s_hot, i * RING + (n * NG + (q + 1)))
                    wait(pe, s_dts, i * RING + (n * NG + q))
                    for j in range(GRP):
                        last = tr(PS[4][:, j * P:(j + 1) * P], DOH[:, q * GRP + j, :], ident[:, :])
                    last.then_inc(s_dt, 1)

                def scores(i, q):
                    wait(pe, s_neg, i * RING + (n * NG + (q + 1)))
                    wait(pe, s_red, i * RING + (n * NG + q))
                    for j in range(GRP):
                        o = PS[j][:, 0:heads * P] if heads > 1 else PS[0][:, j * P:(j + 1) * P]
                        if heads > 1:
                            mm(o, NEG[:, q % 2, j, :], identb[:, :].unsqueeze(1).to_broadcast([P, heads, P]),
                               start=True, stop=False)
                        else:
                            mm(o, NEG[:, q % 2, j, :], identb[:, :], start=True, stop=False)
                        for h in range(heads):
                            last = mm(o[:, h * P:(h + 1) * P], ESB[:, q % 2, j, h:h + 1].to_broadcast([P, P]),
                                      identb[:, :], start=False, stop=(h == heads - 1))
                    last.then_inc(s_v, 1)

                def by_edge(i, q):
                    wait(pe, s_m, i * RING + (n * NG + (q + 1)))
                    wait(pe, s_dts, i * RING + (n * NG + (q + 1)))
                    for j in range(GRP):
                        c = (q % 2) * 64 + j * 2 * heads
                        last = mm(PS[5][:, c:c + 2 * heads], DTS[:, q % 2, j * P:(j + 1) * P],
                                  EDM[:, q % 2, j, :, 0:heads], start=True, stop=True)
                    last.then_inc(s_eb, 1)

                def sums(i, q):
                    wait(pe, s_msg, i * RING + (n * NG + (q + 1)))
                    wait(pe, s_add, i * RING + (n * NG + q))
                    for j in range(GRP):
                        c = (j % 2) * 256
                        last = mm(PS[6 + j // 2][:, c:c + D + heads], DOH[:, q * GRP + j, :],
                                  G[:, q * GRP + j, 0:D + heads], start=True, stop=True)
                    last.then_inc(s_sum, 1)

                def body(i, first=False, last=False):
                    for q in range(RING):
                        if not (last and q == RING - 1):
                            turn(*following(i, q))
                        if not (first and q == 0):
                            sums(*before(i, q))
                        if not (last and q == RING - 1):
                            scores(*following(i, q))
                        by_edge(i, q)

                turn(0, 0)
                scores(0, 0)
                body(0, first=True)
                with pe.Fori(1, NI - 1) as i:
                    body(i)
                body(NI - 1, last=True)
                sums(NI - 1, RING - 1)

            def plain(n, turned):
                def body(i):
                    for q in range(RING):
                        pe.wait_ge(s_hot, i * RING + (n * NG + (q + 1)))
                        pe.wait_ge(s_gath[q], (n * NI + i + 1) * (16 * GRP))
                        pe.wait_ge(s_add, i * RING + (n * NG + (q - 1)))
                        for j in range(GRP):
                            rows, hot = G[:, q * GRP + j, :], DOH[:, q * GRP + j, :]
                            if turned:
                                last = mm(PS[q % 2][:, j * P:(j + 1) * P], rows[:, 0:D], hot, start=True, stop=True)
                            else:
                                c = (j % 2) * 256
                                last = mm(PS[2 * (q % 2) + j // 2][:, c:c + D + 1], hot, rows[:, 0:D + 1],
                                          start=True, stop=True)
                        last.then_inc(s_sum, 1)
                steps(pe, NI, body)

            attention_weights(0, 1, W0)
            table(0, 0, w_ext, D + 2)
            attention(0, 1)
            attention_weights(1, H1, W1)
            table(1, 1, w_ext, D + 2 * H1)
            attention(1, H1)
            for k in range(NET + 6):
                pe.wait_ge(s_w, W1 + 16 * (k + 1))
                pe.wait_ge(s_wv, 4 + k)
                tr(PS[0][:, 0:D], raw_w[:, 0:D], ident[:, :]).then_inc(s_wp, 1)
            pe.wait_ge(s_wv, 4 + NET + 6)

            def into_state(i):
                for q in range(2):
                    turn_block(2, i, q)
            steps(pe, TBI, into_state)
            pe.wait_ge(s_wv, 4 + NET + 6 + 1)
            with pe.Fori(0, STEPS) as st:
                table(st + 2, None, wide_w, NET * D)
                plain(st + 2, True)

                def gru(i):
                    pe.wait_ge(s_add, (st + 3) * NG)
                    pe.wait_ge(s_gh, st * GI + (i + 1))
                    a, h = ACCT[:, bass.ds(i * GW, GW)], HT[:, bass.ds(i * GW, GW)]
                    for g in range(2):
                        o = PS[0][:, g * GW:(g + 1) * GW]
                        mm(o, w_ih[:, g * D:(g + 1) * D], a, start=True, stop=False)
                        mm(o, w_hh[:, g * D:(g + 1) * D], h, start=False, stop=True)
                    mm(PS[1][:, 0:GW], w_ih[:, 2 * D:3 * D], a, start=True, stop=True)
                    mm(PS[1][:, GW:2 * GW], w_hh[:, 2 * D:3 * D], h, start=True, stop=True).then_inc(s_g, 1)
                steps(pe, GI, gru)

            def out_of_state(i):
                for q in range(2):
                    turn_block(3, i, q)
            steps(pe, TBI, out_of_state)
            pe.wait_ge(s_wv, 4 + NET + 6 + 2)
            table(6, 4, wide_w, (NREL + 1) * D)
            plain(6, False)

        @block.scalar
        def _(act):
            def x_block(b):
                return X[:, bass.ds(b, 1), :].rearrange("p a f -> p (a f)")

            def h_block(b):
                return HT[:, bass.ds(b * P, P)]

            def turn_blocks(n, turn):
                def body(i):
                    for q in range(2):
                        wait(act, s_t, i * 2 + (turn * NBLK + (q - 1)))
                        act.sem_inc(s_turn, 1)
                        act.copy(XS[:, q, :], x_block(i * 2 + q)).then_inc(s_xs, 1)
                        act.wait_ge(s_t, i * 2 + (turn * NBLK + (q + 1)))
                        wait(act, s_mm, i * 2 + (n * NBLK + (q - 1)))
                        act.copy(XT[:, q, :], PS[q][:, 0:D]).then_inc(s_xt, 1)
                steps(act, TBI, body, peel=(n == 0))

            def attention(n, heads):
                def masks(i, q):
                    wait(act, s_hot, i * RING + (n * NG + (q + 1)))
                    wait(act, s_v, i * RING + (n * NG + (q - 1)))
                    act.activation(NEG[:, q % 2, :, :], DOH[:, q * GRP:(q + 1) * GRP, :], ACT.Copy,
                                   scale=BIG, bias=-BIG)
                    act.wait_ge(s_gath[q], (i + (n * NI + 1)) * (16 * GRP))
                    act.copy(ESB[:, q % 2, :, 0:heads],
                             G[:, q * GRP:(q + 1) * GRP, D:D + heads]).then_inc(s_neg, 1)

                def turned(i, q):
                    wait(act, s_dt, i * RING + (n * NG + (q + 1)))
                    wait(act, s_eb, i * RING + (n * NG + (q - 1)))
                    act.copy(DTS[:, q % 2, :], PS[4][:, :]).then_inc(s_dts, 1)

                def factors(i, q):
                    wait(act, s_m, i * RING + (n * NG + (q + 1)))
                    wait(act, s_add, i * RING + (n * NG + (q - 1)))
                    act.activation(FEX[:, q % 2, :, 0:heads], FAC[:, q % 2, :, 0:heads], ACT.Exp).then_inc(s_fe, 1)

                def weights(i, q):
                    wait(act, s_se, i * RING + (n * NG + (q + 1)))
                    act.activation(G[:, q * GRP:(q + 1) * GRP, D:D + heads], SE[:, :, 0:heads],
                                   ACT.Exp).then_inc(s_pe, 1)

                def body(i, first=False, last=False):
                    for q in range(RING):
                        if not (first and q == 0):
                            weights(*before(i, q))
                        if not (last and q == RING - 1):
                            masks(*following(i, q))
                            turned(*following(i, q))
                        factors(i, q)
                masks(0, 0)
                turned(0, 0)
                body(0, first=True)
                with act.Fori(1, NI - 1) as i:
                    body(i)
                body(NI - 1, last=True)
                weights(NI - 1, RING - 1)

            t1d, t2d = T1[:, :, :], T2[:, :, 0:D]

            def node_phase(base, requests):
                def body(i):
                    for k, (func, o, a) in enumerate(requests):
                        act.wait_ge(s_np, i * len(requests) + (base + k + 1))
                        act.activation(o, a, func).then_inc(s_na, 1)
                steps(act, NPI, body)

            act.wait_ge(s_x, 32)
            turn_blocks(0, 0)
            attention(0, 1)
            square, root = (ACT.Square, t2d, t1d), (ACT.Sqrt, SM[:, 1, :], SM[:, 1, :])
            node_phase(ASK[0], [(ACT.Exp, t2d, t2d), square, root])
            act.wait_ge(s_xr, 1)
            turn_blocks(1, 1)
            attention(1, H1)
            node_phase(ASK[1], [(ACT.Exp, SD[:, :, :], SD[:, :, :]), square, root, (ACT.Gelu, t2d, t1d),
                                  square, root])
            act.wait_ge(s_xr, 2)

            def into_state(i):
                for q in range(2):
                    act.wait_ge(s_t, i * 2 + (2 * NBLK + q - 1))
                    act.sem_inc(s_turn, 1)
                    act.copy(XS[:, q, :], x_block(i * 2 + q)).then_inc(s_xs, 1)
                    act.wait_ge(s_t, i * 2 + (2 * NBLK + q + 1))
                    act.sem_inc(s_turn, 1)
                    act.copy(h_block(i * 2 + q), PS[q][:, 0:D]).then_inc(s_ht, 1)
            steps(act, TBI, into_state)
            act.wait_ge(s_ht, NBLK)
            act.wait_ge(s_wv, 4 + NET + 6 + 1)
            with act.Fori(0, STEPS) as st:
                def state_blocks(i):
                    for q in range(2):
                        act.wait_ge(s_mm, i * 2 + ((st + 2) * NBLK + (q - 1)))
                        act.sem_inc(s_turn, 1)
                        act.copy(XT[:, q, :], h_block(i * 2 + q)).then_inc(s_xt, 1)
                steps(act, TBI, state_blocks)

                def gates(i):
                    act.wait_ge(s_g, st * GI + (i + 1))
                    act.activation(STG[:, 0, 0:GW], PS[0][:, 0:GW], ACT.Sigmoid, bias=b_rz[:, 0:1])
                    act.activation(STG[:, 0, GW:2 * GW], PS[0][:, GW:2 * GW], ACT.Sigmoid,
                                   bias=b_rz[:, 1:2]).then_inc(s_gr, 1)
                    act.wait_ge(s_gt, st * GI + (i + 1))
                    act.activation(STG[:, 1, GW:2 * GW], STG[:, 1, 0:GW], ACT.Tanh, bias=b_gru[:, 2:3]).then_inc(s_gn, 1)
                steps(act, GI, gates)
                act.wait_ge(s_gh, (st + 1) * GI + 1)
                act.sem_inc(s_turn, 1)

            def out_of_state(i):
                for q in range(2):
                    act.wait_ge(s_t, i * 2 + (3 * NBLK + q - 1))
                    act.sem_inc(s_turn, 1)
                    wait(act, s_xa, i * 2 + (q - 1))
                    act.sem_inc(s_turn, 1)
                    act.copy(XS[:, q, :], h_block(i * 2 + q)).then_inc(s_xs, 1)
            steps(act, TBI, out_of_state, peel=True)
            node_phase(ASK[2], [square, root])
            act.wait_ge(s_xr, 3)
            turn_blocks(6, 4)
            node_phase(ASK[3], [square, root, square, root])

        @block.vector
        def _(dve):
            v = nc.vector
            ch = Chain(dve, s_cv)
            ch.done(v.memset(accf[:, 0:3 * C].bitcast(I32), -1))
            ch.done(v.memset(HT[:, 0:4 * C], 0.0))
            ch.wait()
            dve.sem_inc(s_key, 1)
            ch.done(v.memset(zeros, 0.0))
            ch.done(v.memset(emp[:, :, 0:1], DUMMY))
            ch.done(v.memset(emp[:, :, 1:2], DUMMY * NET))
            ch.done(v.memset(emp[:, :, 2:3].bitcast(F32), -1.0))
            ch.wait()
            dve.sem_inc(s_emp0, 1)
            dve.wait_ge(s_const, 1)
            ch.done(v.tensor_copy(iota[:, :], iotai[:, :]))
            ch.done(v.tensor_copy(identb[:, :], ident[:, :]))
            ch.done(v.tensor_copy(iota_t, iota_ti))
            dve.wait_ge(s_empty, 4 * 16)
            ch.done(v.memset(emp[:, :, 1:2], DUMMY * NREL))
            ch.wait()
            dve.sem_inc(s_emp0, 1)

            dve.wait_ge(s_ints, 8 * 16)
            top, et = tmp_b, tmp_a
            ch.done(v.tensor_reduce(top, attr, AX.X, ALU.max))
            ch.wait()
            ch.done(v.tensor_tensor(et, attr[:, :, 0], top, ALU.is_lt))
            ch.done(v.tensor_tensor(eq, attr[:, :, 1], top, ALU.is_lt))
            ch.done(v.tensor_tensor(pre, attr[:, :, 2], top, ALU.is_lt))
            ch.wait()
            ch.done(v.tensor_tensor(eq, eq, et, ALU.mult))
            ch.wait()
            ch.done(v.tensor_tensor(pre, pre, eq, ALU.mult))
            ch.done(v.tensor_tensor(et, et, eq, ALU.add))
            ch.wait()
            ch.done(v.tensor_tensor(et, et, pre, ALU.add))
            ch.wait()
            ch.done(v.tensor_copy(rec1[:, :, 1], src_i))
            ch.done(v.scalar_tensor_tensor(rec1[:, :, 2], src_i, float(NET), et, ALU.mult, ALU.add))
            ch.done(v.scalar_tensor_tensor(rec2[:, :, 1], dst_i, float(NREL), typ_i, ALU.mult, ALU.add))
            ch.wait()
            tmp_i = tmp_b.bitcast(I32)
            shift = P.bit_length() - 1
            tile_blk = xf[:, 2 * T + 2 * C:2 * T + 2 * C + T]

            def rank(key, key_i, recs, node_word):
                ch.done(v.tensor_scalar(tmp_i, key_i, P - 1, None, ALU.bitwise_and))
                ch.wait()
                ch.done(v.tensor_copy(recs[:, :, node_word].bitcast(F32), tmp_i))
                ch.wait()
                ch.done(v.tensor_scalar(tmp_i, key_i, shift, None, ALU.arith_shift_right))
                ch.wait()
                ch.done(v.tensor_copy(bkt, tmp_i))
                ch.restart()
                with dve.Fori(0, NBLK) as b:
                    ch.done(v.tensor_scalar(eq, bkt, iota[:, bass.ds(b, 1)], 0.0, ALU.is_equal, ALU.add,
                                            accum_out=CNT[:, bass.ds(b, 1)]))
                    ch.restart()
                dve.sem_inc(s_cnt, 1)
                dve.wait_ge(s_pre, key + 1)
                ch.done(v.tensor_scalar(TIL[:, :], PS[0][:, P:P + NBLK], float(P - 1), None, ALU.add))
                ch.wait()
                ch.done(v.tensor_scalar(TIL[:, :], TIL[:, :], shift, None, ALU.arith_shift_right))
                ch.wait()
                ch.done(v.tensor_copy(TOT[:, 0, :], TIL[:, :]))
                ch.wait()
                ch.done(v.tensor_tensor_scan(TOT[:, 1, :], TOT[:, 0, :], zeros[:, 0:NBLK], 0.0, ALU.add, ALU.add))
                ch.wait()
                dve.sem_inc(s_end, 1)
                ch.done(v.tensor_tensor(TOT[:, 2, :], TOT[:, 1, :], TOT[:, 0, :], ALU.subtract))
                ch.wait()
                ch.done(v.scalar_tensor_tensor(BAS[:, :], TOT[:, 2, :], float(P), PS[0][:, 0:NBLK],
                                               ALU.mult, ALU.add))
                dve.wait_ge(s_endt, key + 1)
                ch.done(v.tensor_copy(ENDC[0:NBLK, :], PS[1][0:NBLK, 0:1]))
                ch.wait()
                ch.done(v.tensor_scalar(m_sel[0:NBLK, :], iota_t[0:NBLK, :], ENDC[0:NBLK, :], None, ALU.is_ge))
                ch.wait()
                dve.sem_inc(s_sel, 1)
                for k in range(4):
                    part = slice(k * MW, (k + 1) * MW)
                    dve.wait_ge(s_blk, key * 4 + k + 1)
                    ch.done(v.tensor_scalar((blk_d, blk_s)[key][:, part],
                                            PS[2][32 * key:32 * key + 1, 0:MW], float(NBLK - 1),
                                            None, ALU.min))
                    ch.done(v.tensor_scalar(tile_blk[:, part], PS[2][:, 0:MW], float(NBLK - 1), None, ALU.min))
                    ch.wait()
                    dve.sem_inc(s_blkc, 1)
                if key == 0:
                    ch.done(v.tensor_tensor(LIM[:, 1:T], tile_blk[:, 1:T], tile_blk[:, 0:T - 1], ALU.is_equal))
                    ch.done(v.memset(LIM[:, 0:1], 0.0))
                    ch.wait()
                    ch.done(v.tensor_scalar(LIM[:, :], LIM[:, :], 2 * BIG, -BIG, ALU.mult, ALU.add))
                    ch.wait()
                for k in range(ECH):
                    cols = slice(k * CW, (k + 1) * CW)
                    same, seen, pos = eq[:, 0:CW], pre[:, 0:CW], pre[:, CW:2 * CW]
                    ch.done(v.memset(pos, 1.0))
                    ch.restart()
                    with dve.Fori(0, NBLK) as b:
                        one = bass.ds(b, 1)
                        ch.done(v.tensor_scalar(same, bkt[:, cols], iota[:, one], None, ALU.is_equal))
                        ch.wait()
                        ch.done(v.tensor_tensor_scan(seen, same, zeros[:, 0:CW], BAS[:, one], ALU.add, ALU.add))
                        ch.wait()
                        ch.done(v.tensor_copy(BAS[:, one], seen[:, CW - 1:CW]))
                        ch.done(v.copy_predicated(pos, same.bitcast(U32), seen))
                        ch.restart()
                    pos_i, low, high = same.bitcast(I32), seen.bitcast(I32), pos.bitcast(I32)
                    ch.done(v.tensor_scalar(pos_i, pos, -1.0, None, ALU.add))
                    ch.wait()
                    ch.done(v.tensor_scalar(low, pos_i, P - 1, None, ALU.bitwise_and))
                    ch.done(v.tensor_scalar(high, pos_i, shift, None, ALU.arith_shift_right))
                    ch.wait()
                    ch.done(v.scalar_tensor_tensor(recs[:, cols, 0], low, float(T), high, ALU.mult, ALU.add))
                    ch.done(v.tensor_scalar(same, bkt[:, cols], 0.0, None, ALU.is_lt))
                    ch.wait()
                    ch.done(v.copy_predicated(recs[:, cols, 0], same.bitcast(U32), trash[:, cols]))
                    ch.wait()
                dve.sem_inc(s_pos, 1)

            dve.wait_ge(s_empty, 8 * 16)
            rank(0, dst_i, rec1, 3)
            rank(1, src_i, rec2, 2)
            ch.done(v.memset(X[:, NBLK - 1, :], 0.0))
            ch.wait()
            dve.sem_inc(s_xz, 1)

            def attention_weights(n, heads):
                dve.wait_ge(s_wp, n + 1)
                ch.done(v.tensor_copy(w_t[:, :], PS[3][:, 0:D]))
                ch.wait()
                dve.sem_inc(s_wv, 1)
                dve.wait_ge(s_wa, n + 1)
                ch.done(v.tensor_copy(w_ext[:, D:D + 2 * heads], PS[3][:, P:P + 2 * heads]))
                ch.wait()
                dve.sem_inc(s_wv, 1)

            def x_block(b):
                return X[:, bass.ds(b, 1), :].rearrange("p a f -> p (a f)")

            def evacuate(n, width, heads=0, bias=None, self_loop=False):
                def body(i):
                    for q in range(2):
                        b = i * 2 + q
                        dve.wait_ge(s_mm, i * 2 + (n * NBLK + (q + 1)))
                        wait(dve, s_tab[q], (n * TBI + i) * 16)
                        for k in range(-(-width // 512)):
                            w = min(512, width - 512 * k)
                            o, p = STG[:, q, 512 * k:512 * k + w], PS[2 + 3 * q + k][:, 0:w]
                            last = v.tensor_copy(o, p) if bias is None else v.tensor_tensor(o, p, bias, ALU.add)
                        if heads:
                            ch.done(last)
                            last = v.tensor_copy(ED[:, bass.ds(b, 1), 0:heads].rearrange("p a f -> p (a f)"),
                                                 PS[2 + 3 * q][:, D + heads:D + 2 * heads])
                        if self_loop:
                            ch.done(last)
                            last = v.tensor_tensor(x_block(b), x_block(b), PS[4 + 3 * q][:, 0:D], ALU.add)
                        last.then_inc(s_ev, 1)
                    ch.restart()
                ch.restart()
                steps(dve, TBI, body, peel=(isinstance(n, int) and n == 0))

            def clear_sums():
                ch.done(v.memset(accf, 0.0))
                ch.restart()

            def hot_rows(n, i, q):
                dve.wait_ge(s_rec[q], (i + (n * NI + 1)) * 16)
                v.tensor_tensor(DOH[:, q * GRP:(q + 1) * GRP, :],
                                iota[:, :].unsqueeze(1).to_broadcast([P, GRP, P]),
                                bcast(REC[:, q, :, 2].bitcast(F32), P), ALU.is_equal).then_inc(s_hot, 1)

            regs = [dve.alloc_register(f"blk{j}") for j in range(GRP)]

            def blocks(tile_blocks, g):
                dve.load(regs, tile_blocks[0:1, bass.ds(g * GRP, GRP)])
                return [dve.snap(r, min_val=0, max_val=NBLK - 1) for r in regs]

            def attention(n, heads):
                hs = slice(0, heads)

                def edge_scores(i, q):
                    g = i * RING + q
                    wait(dve, s_eb, g + (n * NG + 1))
                    wait(dve, s_gath[q], (i + (n * NI + 1)) * (16 * GRP))
                    eb = PS[5][:, (q % 2) * 64:(q % 2) * 64 + GRP * 2 * heads].rearrange(
                        "p (j k h) -> p j k h", j=GRP, k=2)
                    ch.done(v.tensor_tensor(SE[:, :, hs], G[:, q * GRP:(q + 1) * GRP, D:D + heads], eb[:, :, 0, :],
                                            ALU.add))
                    ch.wait()
                    ch.done(v.scalar_tensor_tensor(SE2[:, :, hs], SE[:, :, hs], SLOPE, SE[:, :, hs],
                                                   ALU.mult, ALU.max))
                    ch.wait()
                    v.tensor_tensor(SE[:, :, hs], SE2[:, :, hs], eb[:, :, 1, :], ALU.subtract).then_inc(s_se, 1)

                def weigh(i, q):
                    wait(dve, s_pe, i * RING + (n * NG + (q + 1)))
                    rows = G[:, q * GRP:(q + 1) * GRP, :]
                    r4 = rows[:, :, 0:D].rearrange("p j (h d) -> p j h d", h=heads)
                    v.tensor_tensor(r4, r4, rows[:, :, D:D + heads].unsqueeze(3)
                                    .to_broadcast([P, GRP, heads, D // heads]), ALU.mult).then_inc(s_msg, 1)

                def maxima(i, q):
                    g = i * RING + q
                    blk = blocks(blk_d, g)
                    for j in range(GRP):
                        ch.done(v.tensor_copy(EDM[:, q % 2, j, 0, hs],
                                              ED[:, bass.ds(blk[j], 1), hs].rearrange("p a h -> p (a h)")))
                    ch.done(v.tensor_copy(NEW[:, 0, hs], NEW[:, GRP, hs]))
                    wait(dve, s_v, g + (n * NG + 1))
                    if heads == 1:
                        v.tensor_reduce(TMAX[:, :, 0], PS[0][:, :].rearrange("p (j e) -> p j e", j=GRP), AX.X,
                                        ALU.max).then_inc(s_red, 1)
                    else:
                        for j in range(GRP):
                            last = v.tensor_reduce(TMAX[:, j, :], PS[j][:, :].rearrange("p (h e) -> p h e", h=heads),
                                                   AX.X, ALU.max)
                        last.then_inc(s_red, 1)
                    wait(dve, s_red, g + (n * NG + 1))
                    ch.wait()
                    for j in range(GRP):
                        ch.done(v.scalar_tensor_tensor(NEW[:, j + 1, hs], NEW[:, j, hs],
                                                       LIM[:, bass.ds(g * GRP + j, 1)], TMAX[:, j, hs],
                                                       ALU.min, ALU.max))
                        ch.wait()
                        if heads > 1:
                            ch.done(v.tensor_copy(ME[:, bass.ds(blk[j], 1), hs].rearrange("p a h -> p (a h)"),
                                                  NEW[:, j + 1, hs]))
                    lim = bcast(LIM[:, bass.ds(g * GRP, GRP)], heads)
                    ch.done(v.tensor_tensor(NO[:, 1, :, hs], NEW[:, 0:GRP, hs], lim, ALU.min))
                    ed = EDM[:, q % 2, :, 0, hs]
                    ch.done(v.tensor_tensor(NO[:, 0, :, hs], NEW[:, 1:GRP + 1, hs], ed, ALU.add))
                    ch.wait()
                    ch.done(v.tensor_tensor(NO[:, 1, :, hs], NO[:, 1, :, hs], ed, ALU.add))
                    ch.done(v.scalar_tensor_tensor(EDM[:, q % 2, :, 1, hs], NO[:, 0, :, hs], SLOPE, NO[:, 0, :, hs],
                                                   ALU.mult, ALU.max))
                    ch.wait()
                    ch.done(v.scalar_tensor_tensor(NO2[:, 1, :, hs], NO[:, 1, :, hs], SLOPE, NO[:, 1, :, hs],
                                                   ALU.mult, ALU.max))
                    ch.wait()
                    v.tensor_tensor(FAC[:, q % 2, :, hs], NO2[:, 1, :, hs], EDM[:, q % 2, :, 1, hs],
                                    ALU.subtract).then_inc(s_m, 1)

                def add_sums(i, q):
                    g = i * RING + q
                    blk = blocks(blk_d, g)
                    wait(dve, s_sum, g + (n * NG + 1))
                    wait(dve, s_fe, g + (n * NG + 1))
                    for j in range(GRP):
                        s = PS[6 + j // 2][:, (j % 2) * 256:(j % 2) * 256 + D + heads]
                        f = FEX[:, q % 2, j, hs]
                        a = ACC[:, bass.ds(blk[j], 1), 0:D + heads].rearrange("p a f -> p (a f)")
                        if heads == 1:
                            last = v.scalar_tensor_tensor(a, a, f, s, ALU.mult, ALU.add)
                        else:
                            a3 = ACC[:, bass.ds(blk[j], 1), 0:D].rearrange("p a (h d) -> p (a h) d", h=heads)
                            ch.done(v.tensor_tensor(a3, a3, bcast(f, D // heads), ALU.mult))
                            ae = ACC[:, bass.ds(blk[j], 1), D:D + heads].rearrange("p a f -> p (a f)")
                            ch.done(v.tensor_tensor(ae, ae, f, ALU.mult))
                            ch.wait()
                            last = v.tensor_tensor(a, a, s, ALU.add)
                        if j < GRP - 1:
                            ch.done(last)
                            ch.wait()
                    last.then_inc(s_add, 1)

                def body(i, first=False, last=False):
                    for q in range(RING):
                        if not (first and q == 0):
                            edge_scores(*before(i, q))
                        if not (last and q == RING - 1):
                            hot_rows(n, *following(i, q))
                        if not (first and q == 0):
                            weigh(*before(i, q))
                        maxima(i, q)
                        if not (first and q == 0):
                            add_sums(*before(i, q))
                    ch.restart()

                ch.done(v.memset(NEW[:, GRP, :], -BIG))
                ch.done(v.memset(ME[:, :, :], -BIG))
                clear_sums()
                hot_rows(n, 0, 0)
                body(0, first=True)
                with dve.Fori(1, NI - 1) as i:
                    body(i)
                body(NI - 1, last=True)
                edge_scores(NI - 1, RING - 1)
                weigh(NI - 1, RING - 1)
                add_sums(NI - 1, RING - 1)
                dve.wait_ge(s_add, (n + 1) * NG)

            def plain(n, turned, tile_blocks):
                def add(i, q):
                    g = i * RING + q
                    blk = blocks(tile_blocks, g)
                    dve.wait_ge(s_sum, g + (n * NG + 1))
                    dve.wait_ge(s_add, g + n * NG)
                    for j in range(GRP):
                        if turned:
                            a = ACCT[:, bass.ds(blk[j] * P, P)]
                            s = PS[q % 2][:, j * P:(j + 1) * P]
                        else:
                            a = ACC[:, bass.ds(blk[j], 1), 0:D + 1].rearrange("p a f -> p (a f)")
                            s = PS[2 * (q % 2) + j // 2][:, (j % 2) * 256:(j % 2) * 256 + D + 1]
                        last = v.tensor_tensor(a, a, s, ALU.add)
                        if j < GRP - 1:
                            ch.done(last)
                            ch.wait()
                    last.then_inc(s_add, 1)

                def body(i, first=False):
                    for q in range(RING):
                        hot_rows(n, i, q)
                        if not (first and q == 0):
                            add(*before(i, q))
                    ch.restart()
                clear_sums()
                body(0, first=True)
                with dve.Fori(1, NI) as i:
                    body(i)
                add(NI - 1, RING - 1)
                ch.restart()
                dve.wait_ge(s_add, (n + 1) * NG)
                dve.sem_inc(s_turn, 1)

            sm = [SM[:, k, :] for k in range(3)]
            t1d, t2d = T1[:, :, :], T2[:, :, 0:D]

            def rows(tile):
                return tile[:, :].unsqueeze(1).to_broadcast([P, NPB, D])

            def tt(o, a, b, op):
                ch.done(v.tensor_tensor(o, a, b, op))
                ch.wait()

            def ts(o, a, s1, s2, op0, op1=ALU.bypass):
                if s2 is None:
                    ch.done(v.tensor_scalar(o, a, s1, None, op0))
                else:
                    ch.done(v.tensor_scalar(o, a, s1, s2, op0, op1))
                ch.wait()

            def stt(o, a, s, b, op0, op1):
                ch.done(v.scalar_tensor_tensor(o, a, s, b, op0, op1))
                ch.wait()

            def node_phase(base, per, body):
                def step(i):
                    asked = [0]

                    def ask():
                        asked[0] += 1
                        ch.wait()
                        dve.sem_inc(s_np, 1)
                        dve.wait_ge(s_na, i * per + (base + asked[0]))
                    body(i, ask)
                    assert asked[0] == per
                    ch.restart()
                ch.restart()
                steps(dve, NPI, step)

            def normalize(dest, ask):
                ch.done(v.tensor_reduce(sm[0], t1d, AX.X, ALU.add))
                ch.wait()
                ts(sm[0], sm[0], 1.0 / D, None, ALU.mult)
                tt(t1d, t1d, bcast(sm[0], D), ALU.subtract)
                ask()
                ch.done(v.tensor_reduce(sm[1], t2d, AX.X, ALU.add))
                ch.wait()
                ts(sm[1], sm[1], 1.0 / D, EPS, ALU.mult, ALU.add)
                ask()
                ch.done(v.reciprocal(sm[1], sm[1]))
                ch.wait()
                tt(dest, t1d, bcast(sm[1], D), ALU.mult)

            def new_x_complete():
                ch.done(v.tensor_scalar(X[:, NBLK - 1, :], X[:, NBLK - 1, :], maskc[:, :], None, ALU.mult))
                ch.wait()
                dve.sem_inc(s_xr, 1)

            dve.wait_ge(s_x, 32)
            attention_weights(0, 1)
            evacuate(0, D + 1, heads=1)
            attention(0, 1)

            def nodes0(i, ask):
                bs = bass.ds(i * NPB, NPB)
                ts(sm[2], ACC[:, bs, D], 1e-15, None, ALU.max)
                ch.done(v.reciprocal(sm[2], sm[2]))
                ch.wait()
                tt(t1d, ACC[:, bs, 0:D], bcast(sm[2], D), ALU.mult)
                tt(t1d, t1d, rows(bias_b), ALU.add)
                ts(t2d, t1d, 0.0, None, ALU.min)
                ask()
                stt(t1d, t1d, 0.0, t2d, ALU.max, ALU.add)
                stt(t1d, t1d, -1.0, X[:, bs, :], ALU.add, ALU.add)
                normalize(X[:, bs, :], ask)
            node_phase(ASK[0], 3, nodes0)
            ch.done(v.memset(att[:, :], 0.0))
            new_x_complete()

            attention_weights(1, H1)
            evacuate(1, D + H1, heads=H1)
            attention(1, H1)

            def nodes1(i, ask):
                bs = bass.ds(i * NPB, NPB)
                dve.sem_inc(s_hru, 1)
                dve.wait_ge(s_hr, (i + 1) * 16)

                def heads_of(ap):
                    return ap.rearrange("p b (h d) -> p b h d", h=H1)

                def per_row(ap):
                    return ap.rearrange("p (b h) -> p b h", h=H1).unsqueeze(3).to_broadcast([P, NPB, H1, HD])

                def small(ap):
                    return ap.rearrange("p (b h) -> p b h", h=H1)
                tt(small(SA[:, 0, :]), ME[:, bs, :], ED[:, bs, :], ALU.add)
                tt(small(SA[:, 2, :]), T2[:, :, D:D + H1], ED[:, bs, :], ALU.add)
                tt(SA[:, 1, :], SA[:, 0, :], SA[:, 2, :], ALU.max)
                stt(SC[:, :, :], SA[:, :, :], SLOPE, SA[:, :, :], ALU.mult, ALU.max)
                tt(SD[:, 0, :], SC[:, 0, :], SC[:, 1, :], ALU.subtract)
                tt(SD[:, 1, :], SC[:, 2, :], SC[:, 1, :], ALU.subtract)
                ask()
                tt(heads_of(t1d), heads_of(ACC[:, bs, 0:D]), per_row(SD[:, 0, :]), ALU.mult)
                tt(heads_of(t2d), heads_of(t2d), per_row(SD[:, 1, :]), ALU.mult)
                tt(t1d, t1d, t2d, ALU.add)
                tt(small(SA[:, 0, :]), ACC[:, bs, D:D + H1], small(SD[:, 0, :]), ALU.mult)
                stt(SA[:, 0, :], SA[:, 0, :], 1e-16, SD[:, 1, :], ALU.add, ALU.add)
                ch.done(v.reciprocal(SA[:, 1, :], SA[:, 0, :]))
                ch.wait()
                tt(heads_of(t1d), heads_of(t1d), per_row(SA[:, 1, :]), ALU.mult)
                tt(t1d, t1d, rows(bias_b), ALU.add)
                normalize(t1d, ask)
                tt(t1d, t1d, rows(gamma_b), ALU.mult)
                tt(t1d, t1d, rows(beta_b), ALU.add)
                ask()
                tt(t1d, t2d, X[:, bs, :], ALU.add)
                normalize(X[:, bs, :], ask)
            node_phase(ASK[1], 6, nodes1)
            new_x_complete()

            for k in range(NET + 6):
                dve.wait_ge(s_wp, 2 + k + 1)
                g = k - NET
                o = wide_w[:, k * D:(k + 1) * D] if k < NET else (w_ih, w_hh)[g // 3][:, (g % 3) * D:(g % 3 + 1) * D]
                ch.done(v.tensor_copy(o, PS[0][:, 0:D]))
                ch.wait()
                dve.sem_inc(s_wv, 1)
            dve.wait_ge(s_w, W2)
            tt(b_rz[:, :], b_gru[:, 0:2], b_gru[:, 3:5], ALU.add)
            dve.wait_ge(s_ht, NBLK)
            dve.sem_inc(s_wv, 1)
            dve.sem_inc(s_gh, 1)
            ch.restart()
            with dve.Fori(0, STEPS) as st:
                evacuate(st + 2, NET * D, bias=wide_b[:, :])
                plain(st + 2, True, blk_d)

                def gru(i):
                    h = HT[:, bass.ds(i * GW, GW)]
                    r, z = STG[:, 0, 0:GW], STG[:, 0, GW:2 * GW]
                    t, n = STG[:, 1, 0:GW], STG[:, 1, GW:2 * GW]
                    dve.wait_ge(s_gr, st * GI + (i + 1))
                    ch.done(v.scalar_tensor_tensor(t, PS[1][:, GW:2 * GW], b_gru[:, 5:6], r, ALU.add, ALU.mult))
                    ch.wait()
                    v.tensor_tensor(t, t, PS[1][:, 0:GW], ALU.add).then_inc(s_gt, 1)
                    dve.wait_ge(s_gn, st * GI + (i + 1))
                    tt(h, h, n, ALU.subtract)
                    tt(h, h, z, ALU.mult)
                    v.tensor_tensor(h, h, n, ALU.add).then_inc(s_gh, 1)
                    ch.restart()
                steps(dve, GI, gru)
                dve.wait_ge(s_gh, (st + 1) * GI + 1)
                dve.sem_inc(s_turn, 1)

            def add_state(i):
                for q in range(2):
                    dve.wait_ge(s_t, i * 2 + (3 * NBLK + q + 1))
                    b = i * 2 + q
                    v.tensor_tensor(x_block(b), x_block(b), PS[q][:, 0:D], ALU.add).then_inc(s_xa, 1)
            steps(dve, TBI, add_state)
            dve.wait_ge(s_xa, NBLK)

            def nodes2(i, ask):
                bs = bass.ds(i * NPB, NPB)
                ch.done(v.tensor_copy(t1d, X[:, bs, :]))
                ch.wait()
                normalize(X[:, bs, :], ask)
            node_phase(ASK[2], 2, nodes2)
            new_x_complete()

            dve.wait_ge(s_w, W3)
            for r in range(NREL):
                w_r = wide_w[:, r * D:(r + 1) * D]
                ts(w_r, raw_w[:, 0:D], alpha_b[:, r * NBASE:r * NBASE + 1], None, ALU.mult)
                for b in range(1, NBASE):
                    stt(w_r, raw_w[:, b * D:(b + 1) * D], alpha_b[:, r * NBASE + b:r * NBASE + b + 1], w_r,
                        ALU.mult, ALU.add)
            tt(beta_b[:, :], beta_b[:, :], bias_b[:, :], ALU.add)
            ch.done(v.memset(G[:, :, D:D + 1], 1.0))
            ch.wait()
            dve.sem_inc(s_wv, 1)
            evacuate(6, NREL * D, self_loop=True)
            plain(6, False, blk_s)

            def nodes3(i, ask):
                bs = bass.ds(i * NPB, NPB)
                ts(sm[2], ACC[:, bs, D], 1.0, None, ALU.max)
                ch.done(v.reciprocal(sm[2], sm[2]))
                ch.wait()
                tt(t1d, ACC[:, bs, 0:D], bcast(sm[2], D), ALU.mult)
                normalize(t1d, ask)
                tt(t1d, t1d, rows(gamma_b), ALU.mult)
                tt(t1d, t1d, rows(beta_b), ALU.add)
                tt(t1d, t1d, X[:, bs, :], ALU.add)
                normalize(X[:, bs, :], ask)
            node_phase(ASK[3], 4, nodes3)
            dve.sem_inc(s_on, 1)


_INS = ['x', 'src', 'dst', 'edge_attr_4', 'edge_type_8',
        'L0_gnn_W', 'L0_gnn_a_src', 'L0_gnn_a_dst', 'L0_gnn_bias',
        'L1_gnn_W', 'L1_gnn_att_src', 'L1_gnn_att_dst', 'L1_gnn_bias', 'L1_gnn_gamma', 'L1_gnn_beta',
        'L2_gnn_W_edge', 'L2_gnn_b_edge', 'L2_gnn_W_ih', 'L2_gnn_W_hh', 'L2_gnn_b_ih', 'L2_gnn_b_hh',
        'L3_gnn_weight', 'L3_gnn_alpha', 'L3_gnn_bias', 'L3_gnn_weight_self_loop', 'L3_gnn_ln_gamma',
        'L3_gnn_ln_beta']


def kernel(**inputs):
    import numpy as _np
    import concourse.bacc as _bacc
    from concourse import mybir as _mybir
    from concourse.bass_utils import run_bass_kernel_spmd as _run

    nc = _bacc.Bacc("TRN2", target_bir_lowering=False, num_devices=1)
    arrays, args = {}, []
    for name in _INS:
        a = _np.ascontiguousarray(inputs[name])
        arrays[f"in_{name}"] = a
        args.append(nc.dram_tensor(f"in_{name}", a.shape, _mybir.dt.from_np(a.dtype), kind="ExternalInput").ap())
    args.append(nc.dram_tensor("out_x", (N, D), F32, kind="ExternalOutput").ap())
    build(nc, *args)
    r = _run(nc, [arrays], core_ids=[0])
    return r.results[0]["out_x"]
```

```python
import concourse.bass as bass
from concourse import mybir
from contextlib import ExitStack

F32 = mybir.dt.float32
BF16 = mybir.dt.bfloat16
I32 = mybir.dt.int32
U32 = mybir.dt.uint32
ALU = mybir.AluOpType
ACT = mybir.ActivationFunctionType
AX = mybir.AxisListType

P = 128
N = 12500
E = 200000
D = 128
NBLK = -(-N // P)
NPAD = NBLK * P
ECOL = -(-E // P)
ELAST = E - (P - 1) * ECOL
SCOL = 4
ECH = 7
C = -(-ECOL // (2 * SCOL)) * 2 * SCOL
CW = C // ECH
GRP = 4
RING = 4
BODY = GRP * RING
T = -(-((E + NBLK * (P - 1)) // P) // BODY) * BODY
NG = T // GRP
NI = T // BODY
H1 = 4
HD = D // H1
NET = 4
NREL = 8
NBASE = 4
STEPS = 4
NPB = 7
NPI = NBLK // NPB
TBI = NBLK // 2
GW = 256
GI = NPAD // GW
BIG = 1e30
DUMMY = N
WROW = D + H1
EPS = 1e-5
SLOPE = 0.2
MW = T // 4
SCI = C // (2 * SCOL)
SCK = CW // (2 * SCOL)
SC_A, SC_B, SC_L1 = SCK, 36, NI
SC_C = SCI - SC_A - SC_B - SC_L1
assert SC_C % NPI == 0
assert C % ECH == 0 and CW % (2 * SCOL) == 0 and SC_C > 0 and GI % 2 == 1 and NBLK == 2 * GI
ASK = [0, 3 * NPI, 9 * NPI, 11 * NPI]
assert NBLK % (2 * NPB) == 0 and C >= ECOL and MW <= 512 and NPAD % GW == 0


def wait(eng, sem, value):
    if isinstance(value, int) and value <= 0:
        return
    eng.wait_ge(sem, value)


def steps(eng, count, body, peel=False):
    if peel:
        body(0)
    with eng.Fori(1 if peel else 0, count) as i:
        body(i)


def following(i, q):
    return (i, q + 1) if q < RING - 1 else (i + 1, 0)


def before(i, q):
    return (i, q - 1) if q else (i - 1, RING - 1)


class Chain:

    def __init__(self, eng, sem):
        self.eng, self.sem, self.n = eng, sem, 0

    def done(self, ins):
        ins.then_inc(self.sem, 1)
        self.n += 1
        return self.n

    def wait(self, n=None):
        wait(self.eng, self.sem, self.n if n is None else n)

    def restart(self):
        self.wait()
        if self.n:
            self.eng.sem_clear(self.sem)
        self.n = 0


def build(nc, x, src, dst, edge_attr_4, edge_type_8,
          L0_gnn_W, L0_gnn_a_src, L0_gnn_a_dst, L0_gnn_bias,
          L1_gnn_W, L1_gnn_att_src, L1_gnn_att_dst, L1_gnn_bias, L1_gnn_gamma, L1_gnn_beta,
          L2_gnn_W_edge, L2_gnn_b_edge, L2_gnn_W_ih, L2_gnn_W_hh, L2_gnn_b_ih, L2_gnn_b_hh,
          L3_gnn_weight, L3_gnn_alpha, L3_gnn_bias, L3_gnn_weight_self_loop, L3_gnn_ln_gamma, L3_gnn_ln_beta,
          out):
    ctx = ExitStack()
    with ctx:
        def sb(name, shape, dt=F32):
            return ctx.enter_context(nc.sbuf_tensor(name, shape, dt))

        def sem(name):
            return ctx.enter_context(nc.semaphore(name))

        def dram(name, shape, dt=F32):
            return nc.dram_tensor(name, shape, dt, kind="Internal").ap()

        rec_dst = dram("rec_dst", [P * T + P * C, 3], I32)
        rec_src = dram("rec_src", [P * T + P * C, 2], I32)
        tab0 = dram("tab0", [NPAD, D + 1])
        tab1 = dram("tab1", [NPAD, D + H1])
        tab2 = dram("tab2", [NPAD * NET, D])
        tab3 = dram("tab3", [NPAD * NREL, D])

        X = sb("X", [P, NBLK, D])
        HT = sb("HT", [P, NPAD])
        ACC = sb("ACC", [P, NBLK, WROW])
        ACCT = ACC[:, :, :].rearrange("p b w -> p (b w)")[:, 0:NPAD]
        G = sb("G", [P, BODY, WROW])
        STG = sb("STG", [P, 2, NREL * D])
        DOH = STG[:, :, :].rearrange("p a b -> p (a b)")[:, 0:BODY * P].rearrange("p (a b) -> p a b", b=P)
        node_tmp = sb("node_tmp", [P, NPB * (D + WROW)])
        GATE_T = node_tmp[:, 0:4 * GW].rearrange("p (a b) -> p a b", a=2)
        T1 = node_tmp[:, 0:NPB * D].rearrange("p (a b) -> p a b", b=D)
        T2 = node_tmp[:, NPB * D:].rearrange("p (a b) -> p a b", b=WROW)
        DTS = node_tmp[:, 0:2 * GRP * P].rearrange("p (a b) -> p a b", a=2)
        NEG = node_tmp[:, 2 * GRP * P:3 * GRP * P].bitcast(BF16).rearrange("p (a j e) -> p a j e", a=2, j=GRP)
        by_layer = sb("by_layer", [P, (NREL + 1 + NET + 6 + NBASE) * D])

        def part(width):
            taken[0] += width
            return by_layer[:, taken[0] - width:taken[0]]
        taken = [0]
        LIM = part(T)
        ME = part(NBLK * H1).rearrange("p (b h) -> p b h", h=H1)
        ED = part(NBLK * H1).rearrange("p (b h) -> p b h", h=H1)
        taken[0] = 0
        wide_w = part((NREL + 1) * D)
        wide_b = part(NET * D)
        w_ih = part(3 * D)
        w_hh = part(3 * D)
        raw_w = part(NBASE * D)
        REC = sb("REC", [P, RING, GRP, 3], I32)
        ident = sb("ident", [P, P])
        identb = sb("identb", [P, P], BF16)
        ones = sb("ones", [P, P])
        lower = sb("lower", [P, P])
        iota = sb("iota", [P, P])
        iotai = sb("iotai", [P, P], I32)
        maskc = sb("maskc", [P, 1])
        tile_blocks = sb("tile_blocks", [33, T], I32)
        blk_d, blk_s = tile_blocks[0:1, :], tile_blocks[32:33, :]
        w_ext = sb("w_ext", [P, D + 2 * H1])
        w_t = sb("w_t", [P, D])
        att = sb("att", [P, 2 * H1])
        bias_b = sb("bias_b", [P, D])
        gamma_b = sb("gamma_b", [P, D])
        beta_b = sb("beta_b", [P, D])
        b_gru = sb("b_gru", [P, 6])
        b_rz = sb("b_rz", [P, 2])
        alpha_b = sb("alpha_b", [P, NREL * NBASE])
        XS = sb("XS", [P, 2, D])
        XT = sb("XT", [P, 2, D])
        SM = sb("SM", [P, 3, NPB])
        SA = sb("SA", [P, 3, NPB * H1])
        SC = sb("SC", [P, 3, NPB * H1])
        SD = sb("SD", [P, 2, NPB * H1])
        ESB = sb("ESB", [P, 2, GRP, H1], BF16)
        TMAX = sb("TMAX", [P, GRP, H1])
        NEW = sb("NEW", [P, 2 * GRP + 1, H1])
        NO = sb("NO", [P, 2, GRP, H1])
        EDM = sb("EDM", [P, 2, 3, GRP, H1])
        FAC = sb("FAC", [P, 2, GRP, H1])
        FEX = sb("FEX", [P, 2, GRP, H1])
        SE = sb("SE", [P, GRP, H1])
        SE2 = sb("SE2", [P, GRP, H1])

        accf = ACC[:, :, :].rearrange("p b w -> p (b w)")
        xf = X[:, :, :].rearrange("p b w -> p (b w)")
        src_i = accf[:, 0 * C:1 * C].bitcast(I32)
        dst_i = accf[:, 1 * C:2 * C].bitcast(I32)
        typ_i = accf[:, 2 * C:3 * C].bitcast(I32)
        bkt = accf[:, 3 * C:4 * C]
        tmp_a = accf[:, 4 * C:5 * C]
        tmp_b = accf[:, 5 * C:6 * C]
        m_sel = accf[:, 6 * C:6 * C + T]
        attr = HT[:, 4 * C:8 * C].rearrange("p (c f) -> p c f", f=4)
        rec1 = HT[:, 0:4 * C].bitcast(I32).rearrange("p (c f) -> p c f", f=4)
        rec2 = HT[:, 5 * C:8 * C].bitcast(I32).rearrange("p (c f) -> p c f", f=3)
        DIST = HT[:, 0:GRP * P]
        assert 8 * C <= NPAD and 6 * C + T <= NBLK * WROW
        iota_t = xf[:, 0:T]
        iota_ti = xf[:, T:2 * T].bitcast(I32)
        trash = xf[:, 2 * T:2 * T + C].bitcast(I32)
        zeros = xf[:, 2 * T + C:2 * T + 2 * C]
        eq = xf[:, 2 * T + 2 * C:2 * T + 3 * C]
        pre = xf[:, 2 * T + 3 * C:2 * T + 4 * C]
        emp = xf[:, 2 * T + 4 * C:2 * T + 4 * C + 3 * MW].bitcast(I32).rearrange("p (c f) -> p c f", f=3)
        small = xf[:, 2 * T + 4 * C + 3 * MW:]
        CNT, BAS = small[:, 0:NBLK], small[:, NBLK:2 * NBLK]
        TOT = small[:, 2 * NBLK:5 * NBLK].rearrange("p (k b) -> p k b", k=3)
        TIL = small[:, 5 * NBLK:6 * NBLK].bitcast(I32)
        ENDC = small[:, 6 * NBLK:6 * NBLK + 1]
        STGS = sb("STGS", [P, 2, SCOL, 4], I32)
        STG2 = sb("STG2", [P, 2, SCOL, 3], I32)

        PS = [ctx.enter_context(nc.psum_tensor(f"PS{i}", [P, 512], F32)) for i in range(8)]

        s_ints = sem("s_ints")
        s_const = sem("s_const")
        s_consts2 = sem("s_consts2")
        s_key = sem("s_key")
        s_empty = sem("s_empty")
        s_emp0 = sem("s_emp0")
        s_cnt = sem("s_cnt")
        s_pre = sem("s_pre")
        s_end = sem("s_end")
        s_endt = sem("s_endt")
        s_sel = sem("s_sel")
        s_blk = sem("s_blk")
        s_blkc = sem("s_blkc")
        s_pos = sem("s_pos")
        s_stage = [sem(f"s_stage{i}") for i in range(2)]
        s_scat = [sem(f"s_scat{i}") for i in range(2)]
        s_x = sem("s_x")
        s_xz = sem("s_xz")
        s_w = sem("s_w")
        s_wp = sem("s_wp")
        s_wa = sem("s_wa")
        s_wv = sem("s_wv")
        s_acc0 = sem("s_acc0")
        s_rec = [sem(f"s_rec{i}") for i in range(RING)]
        s_gath = [sem(f"s_gath{i}") for i in range(RING)]
        s_hot = sem("s_hot")
        s_neg = sem("s_neg")
        s_dt = sem("s_dt")
        s_dts = sem("s_dts")
        s_v = sem("s_v")
        s_red = sem("s_red")
        s_m = sem("s_m")
        s_fe = sem("s_fe")
        s_eb = sem("s_eb")
        s_se = sem("s_se")
        s_pe = sem("s_pe")
        s_msg = sem("s_msg")
        s_sum = sem("s_sum")
        s_add = sem("s_add")
        s_turn = sem("s_turn")
        s_xs = sem("s_xs")
        s_t = sem("s_t")
        s_xt = sem("s_xt")
        s_mm = sem("s_mm")
        s_ev = sem("s_ev")
        s_tab = [sem(f"s_tab{i}") for i in range(2)]
        s_np = sem("s_np")
        s_na = sem("s_na")
        s_hr = sem("s_hr")
        s_hru = sem("s_hru")
        s_xr = sem("s_xr")
        s_g = sem("s_g")
        s_gr = sem("s_gr")
        s_gt = sem("s_gt")
        s_gn = sem("s_gn")
        s_gh = sem("s_gh")
        s_on = sem("s_on")
        s_out = sem("s_out")
        s_cv = sem("s_cv")
        s_ca = sem("s_ca")
        s_cp = sem("s_cp")
        s_tb_all = sem("s_tb_all")
        s_ht = sem("s_ht")
        s_xa = sem("s_xa")

        block = ctx.enter_context(nc.Block())


        def bcast(ap, n):
            return ap.unsqueeze(2).to_broadcast([ap.shape[0], ap.shape[1], n])

        def row_of(vec):
            return vec.rearrange("(a n) -> a n", a=1).to_broadcast([P, vec.shape[0]])

        W0 = 4 * 16
        W1 = W0 + (4 + 2 * H1) * 16
        W2M = W1 + (NET + 6) * 16
        W2 = W2M + (6 + NET) * 16
        W3 = W2 + (NBASE + 5) * 16
        full = (P - 1) * ECOL
        full_b = N // P

        @block.sync
        def _(sp):
            sp.wait_ge(s_key, 1)
            for vec, tile in ((dst, dst_i), (src, src_i), (edge_type_8, typ_i)):
                sp.dma_start(tile[0:P - 1, 0:ECOL], vec[0:full].rearrange("(p c) -> p c", p=P - 1)).then_inc(s_ints, 16)
                sp.dma_start(tile[P - 1:P, 0:ELAST], vec[full:E].rearrange("(p c) -> p c", p=1)).then_inc(s_ints, 16)
            sp.dma_start(attr[0:P - 1, 0:ECOL, :],
                         edge_attr_4[0:full, :].rearrange("(p c) f -> p c f", p=P - 1)).then_inc(s_ints, 16)
            sp.dma_start(attr[P - 1:P, 0:ELAST, :],
                         edge_attr_4[full:E, :].rearrange("(p c) f -> p c f", p=1)).then_inc(s_ints, 16)

            def prefill(recs, words, ready):
                sp.wait_ge(s_emp0, ready)
                view = recs[0:P * T, :].rearrange("(p t) f -> p t f", p=P)
                for k in range(4):
                    sp.dma_start(view[:, k * MW:(k + 1) * MW, :], emp[:, :, words]).then_inc(s_empty, 16)

            prefill(rec_dst, slice(0, 3), 1)
            prefill(rec_src, slice(1, 3), 2)

            def load_w(pairs):
                for tile, ap in pairs:
                    sp.dma_start(tile, ap).then_inc(s_w, 16)

            load_w([(w_t[:, :], L0_gnn_W), (att[:, 0:1], L0_gnn_a_src.rearrange("(n a) -> n a", a=1)),
                    (att[:, 1:2], L0_gnn_a_dst.rearrange("(n a) -> n a", a=1)), (bias_b[:, :], row_of(L0_gnn_bias))])

            def stage_columns(key, s, i, first=0):
                recs, stage, width = ((rec1, STGS, 4), (rec2, STG2, 3))[key]
                wait(sp, s_scat[s], (i + (key * SCI + first)) * (16 * SCOL))
                sp.dma_start(stage[:, s, :, :].rearrange("p c f -> p (c f)"),
                             recs.rearrange("p c f -> p (c f)")[:, bass.ds((i * 2 + (first * 2 + s)) * (SCOL * width),
                                                                          SCOL * width)]).then_inc(s_stage[s], 16)

            def stage_steps(key, first, count):
                def body(i):
                    for s in range(2):
                        stage_columns(key, s, i, first)
                steps(sp, count, body, peel=(key == 0 and first == 0))

            for k in range(ECH):
                sp.wait_ge(s_pos, k + 1)
                stage_steps(0, k * SCK, SCK)
            sp.wait_ge(s_pos, ECH + 1)
            stage_steps(1, 0, SC_A)

            def store_table(n, table, rows):
                width = table.shape[1] * rows

                def body(i):
                    for q in range(2):
                        sp.wait_ge(s_ev, i * 2 + (n * NBLK + (q + 1)))
                        sp.dma_start(table[bass.ds((i * 2 + q) * (P * rows), P * rows), :]
                                     .rearrange("(p r) f -> p (r f)", p=P), STG[:, q, 0:width]).then_inc(s_tab[q], 16)
                steps(sp, TBI, body)
                for q in range(2):
                    sp.wait_ge(s_tab[q], (n + 1) * (16 * TBI))
                    sp.sem_inc(s_turn, 1)
                sp.sem_inc(s_tb_all, 1)

            def load_records(n, recs, width, staging=False):
                view = recs[0:P * T, :].rearrange("(p t) f -> p t f", p=P)

                def body(i):
                    for q in range(RING):
                        wait(sp, s_gath[q], (n * NI + i) * (16 * GRP))
                        sp.sem_inc(s_turn, 1)
                        wait(sp, s_hot, i * RING + (n * NG + (q + 1 - RING)))
                        sp.dma_start(REC[:, q, :, 3 - width:3],
                                     view[:, bass.ds(i * BODY + q * GRP, GRP), :]).then_inc(s_rec[q], 16)
                        if staging and q % 2:
                            stage_columns(1, q // 2, i, SC_A + SC_B)
                steps(sp, NI, body, peel=(isinstance(n, int) and n == 0))

            store_table(0, tab0, 1)
            for s in range(2):
                sp.wait_ge(s_scat[s], (SCI + SC_A) * SCOL * 16)
            load_records(0, rec_dst, 3)
            sp.wait_ge(s_pos, 2 * ECH)
            stage_steps(1, SC_A, SC_B)
            sp.wait_ge(s_xr, 1)
            load_w([(w_t[:, :], L1_gnn_W), (bias_b[:, :], row_of(L1_gnn_bias)),
                    (gamma_b[:, :], row_of(L1_gnn_gamma)), (beta_b[:, :], row_of(L1_gnn_beta))] +
                   [(att[h * HD:(h + 1) * HD, o + h:o + h + 1], a[h, :].rearrange("(n a) -> n a", a=1))
                    for o, a in ((0, L1_gnn_att_src), (H1, L1_gnn_att_dst)) for h in range(H1)])
            store_table(1, tab1, 1)
            load_records(1, rec_dst, 3, staging=True)
            rows1 = tab1.rearrange("(b p) w -> p b w", p=P)

            def own_rows(i):
                sp.wait_ge(s_hru, i + 1)
                sp.dma_start(T2[:, :, :], rows1[:, bass.ds(i * NPB, NPB), :]).then_inc(s_hr, 16)
                for k in range(SC_C // NPI):
                    for s in range(2):
                        stage_columns(1, s, i * (SC_C // NPI) + k, SC_A + SC_B + SC_L1)
            steps(sp, NPI, own_rows)
            sp.wait_ge(s_xr, 2)
            raws = [L2_gnn_W_edge[t, :, :] for t in range(NET)] + \
                   [m[g * D:(g + 1) * D, :] for m in (L2_gnn_W_ih, L2_gnn_W_hh) for g in range(3)]
            for k, m in enumerate(raws):
                load_w([(raw_w[:, 0:D], m)])
                sp.wait_ge(s_wp, 2 + k + 1)
            load_w([(b_gru[:, 3 * k + g:3 * k + g + 1], b[g * D:(g + 1) * D].rearrange("(n a) -> n a", a=1))
                    for k, b in enumerate((L2_gnn_b_ih, L2_gnn_b_hh)) for g in range(3)] +
                   [(wide_b[:, t * D:(t + 1) * D], row_of(L2_gnn_b_edge[t, :])) for t in range(NET)])
            store_table(2, tab2, NET)
            with sp.Fori(0, STEPS - 1) as st:
                load_records(st + 2, rec_dst, 3)
                store_table(st + 3, tab2, NET)
            load_records(STEPS + 1, rec_dst, 3)
            sp.wait_ge(s_xr, 3)
            load_w([(raw_w[:, b * D:(b + 1) * D], L3_gnn_weight[b, :, :]) for b in range(NBASE)] +
                   [(alpha_b[:, :], row_of(L3_gnn_alpha.rearrange("r b -> (r b)"))),
                    (wide_w[:, NREL * D:(NREL + 1) * D], L3_gnn_weight_self_loop),
                    (bias_b[:, :], row_of(L3_gnn_bias)), (gamma_b[:, :], row_of(L3_gnn_ln_gamma)),
                    (beta_b[:, :], row_of(L3_gnn_ln_beta))])
            store_table(6, tab3, NREL)
            for s in range(2):
                sp.wait_ge(s_scat[s], 2 * SCI * SCOL * 16)
            load_records(6, rec_src, 2)
            sp.wait_ge(s_on, 1)
            sp.dma_start(out[0:full_b * P, :].rearrange("(b p) f -> p b f", p=P), X[:, 0:full_b, :]).then_inc(s_out, 16)
            sp.dma_start(out[full_b * P:N, :], X[0:N - full_b * P, full_b, :]).then_inc(s_out, 16)
            sp.wait_ge(s_out, 32)

        @block.gpsimd
        def _(pool):
            ch = Chain(pool, s_cp)
            ch.done(pool.memset(ident[:, :], 0.0))
            ch.done(pool.memset(lower[:, :], 1.0))
            ch.done(pool.memset(maskc[:, :], 1.0))
            ch.done(pool.memset(ones[:, :], 1.0))
            ch.wait()
            ch.done(pool.affine_select(out=ident[:, :], in_=ident[:, :], compare_op=ALU.not_equal, fill=1.0,
                                       base=0, pattern=[[-1, P]], channel_multiplier=1))
            ch.done(pool.affine_select(out=lower[:, :], in_=lower[:, :], compare_op=ALU.is_gt, fill=0.0,
                                       base=0, pattern=[[1, P]], channel_multiplier=-1))
            ch.done(pool.affine_select(out=maskc[:, :], in_=maskc[:, :], compare_op=ALU.is_gt, fill=0.0,
                                       base=N - (NBLK - 1) * P, pattern=[[0, 1]], channel_multiplier=-1))
            ch.done(pool.iota(iotai[:, :], pattern=[[1, P]], base=0, channel_multiplier=0))
            ch.done(pool.iota(iota_ti, pattern=[[1, T]], base=0, channel_multiplier=0))
            ch.done(pool.iota(trash, pattern=[[1, C]], base=P * T, channel_multiplier=C))
            ch.wait()
            pool.sem_inc(s_const, 1)

            def scatter_columns(key, s, i, first=0):
                recs, stage, width = ((rec_dst, STGS, 4), (rec_src, STG2, 3))[key]
                pool.wait_ge(s_stage[s], (i + (key * SCI + first + 1)) * 16)
                pool.sem_inc(s_turn, 1)
                for c in range(SCOL):
                    pool.indirect_dma_start(recs, bass.IndirectOffsetOnAxis(stage[:, s, c, 0:1], 0),
                                            stage[:, s, c, 1:width], None).then_inc(s_scat[s], 16)

            def scatter_steps(key, first, count):
                def body(i):
                    for s in range(2):
                        scatter_columns(key, s, i, first)
                steps(pool, count, body)

            pool.wait_ge(s_empty, 8 * 16)
            scatter_steps(0, 0, SCI)
            scatter_steps(1, 0, SC_A)

            def gather(n, table, word, scattering=False):
                width = table.shape[1]
                pool.wait_ge(s_tb_all, n + 1)
                pool.sem_inc(s_turn, 1)

                def body(i):
                    for q in range(RING):
                        pool.wait_ge(s_rec[q], (n * NI + i + 1) * 16)
                        pool.sem_inc(s_turn, 1)
                        wait(pool, s_sum, i * RING + (n * NG + (q + 1 - RING)))
                        pool.sem_inc(s_turn, 1)
                        for j in range(GRP):
                            pool.indirect_dma_start(
                                G[:, q * GRP + j, 0:width], None, table,
                                bass.IndirectOffsetOnAxis(REC[:, q, j, word:word + 1], 0)).then_inc(s_gath[q], 16)
                        if scattering and q % 2:
                            scatter_columns(1, q // 2, i, SC_A + SC_B)
                steps(pool, NI, body, peel=(isinstance(n, int) and n == 0))

            gather(0, tab0, 0)
            scatter_steps(1, SC_A, SC_B)
            gather(1, tab1, 0, scattering=True)
            scatter_steps(1, SC_A + SC_B + SC_L1, SC_C)
            with pool.Fori(0, STEPS) as st:
                gather(st + 2, tab2, 1)
            gather(6, tab3, 1)

        @block.tensor
        def _(pe):
            mm, tr = nc.tensor.matmul, nc.tensor.transpose
            pe.wait_ge(s_const, 1)
            for key in range(2):
                pe.wait_ge(s_cnt, key + 1)
                mm(PS[0][:, 0:NBLK], lower[:, :], CNT[:, :], start=True, stop=True)
                mm(PS[0][:, P:P + NBLK], ones[:, :], CNT[:, :], start=True, stop=True).then_inc(s_pre, 1)
                pe.wait_ge(s_end, key + 1)
                tr(PS[1][0:NBLK, 0:P], TOT[:, 1, :], ident[:, :]).then_inc(s_endt, 1)
                pe.wait_ge(s_sel, key + 1)
                for k in range(4):
                    wait(pe, s_blkc, key * 4 + k)
                    mm(PS[2][:, 0:MW], ones[0:NBLK, :], m_sel[0:NBLK, k * MW:(k + 1) * MW],
                       start=True, stop=True).then_inc(s_blk, 1)

            def attention_weights(n, heads, loaded):
                pe.wait_ge(s_w, loaded)
                tr(PS[3][:, 0:D], w_t[:, :], ident[:, :]).then_inc(s_wp, 1)
                pe.wait_ge(s_wv, 2 * n + 1)
                mm(PS[3][:, P:P + 2 * heads], w_t[:, :], att[:, 0:2 * heads], start=True, stop=True).then_inc(s_wa, 1)
                pe.wait_ge(s_wv, 2 * n + 2)

            def turn_block(turn, i, q):
                pe.wait_ge(s_xs, i * 2 + (turn * NBLK + q + 1))
                tr(PS[q][:, 0:D], XS[:, q, :], ident[:, :]).then_inc(s_t, 1)

            def table(n, turn, rhs, width):
                def body(i):
                    for q in range(2):
                        if turn is not None:
                            turn_block(turn, i, q)
                        pe.wait_ge(s_xt, i * 2 + (n * NBLK + (q + 1)))
                        wait(pe, s_ev, i * 2 + (n * NBLK + (q - 1)))
                        for k in range(-(-width // 512)):
                            w = min(512, width - 512 * k)
                            last = mm(PS[2 + 3 * q + k][:, 0:w], XT[:, q, :], rhs[:, 512 * k:512 * k + w],
                                      start=True, stop=True)
                        last.then_inc(s_mm, 1)
                steps(pe, TBI, body, peel=(isinstance(n, int) and n == 0))

            def attention(n, heads):
                def turn(i, q):
                    wait(pe, s_hot, i * RING + (n * NG + (q + 1)))
                    wait(pe, s_dts, i * RING + (n * NG + q))
                    for j in range(GRP):
                        last = tr(PS[4][:, j * P:(j + 1) * P], DOH[:, q * GRP + j, :], ident[:, :])
                    last.then_inc(s_dt, 1)

                def scores(i, q):
                    wait(pe, s_neg, i * RING + (n * NG + (q + 1)))
                    wait(pe, s_red, i * RING + (n * NG + q))
                    for j in range(GRP):
                        o = PS[j][:, 0:heads * P] if heads > 1 else PS[0][:, j * P:(j + 1) * P]
                        if heads > 1:
                            mm(o, NEG[:, q % 2, j, :], identb[:, :].unsqueeze(1).to_broadcast([P, heads, P]),
                               start=True, stop=False)
                        else:
                            mm(o, NEG[:, q % 2, j, :], identb[:, :], start=True, stop=False)
                        for h in range(heads):
                            last = mm(o[:, h * P:(h + 1) * P], ESB[:, q % 2, j, h:h + 1].to_broadcast([P, P]),
                                      identb[:, :], start=False, stop=(h == heads - 1))
                    last.then_inc(s_v, 1)

                def by_edge(i, q):
                    wait(pe, s_m, i * RING + (n * NG + (q + 1)))
                    wait(pe, s_dts, i * RING + (n * NG + (q + 1)))
                    for j in range(GRP):
                        c = (q % 2) * 64 + j * 2 * heads
                        last = mm(PS[5][:, c:c + 2 * heads], DTS[:, q % 2, j * P:(j + 1) * P],
                                  EDM[:, q % 2, 0:2, j, 0:heads], start=True, stop=True)
                    last.then_inc(s_eb, 1)

                def sums(i, q):
                    wait(pe, s_msg, i * RING + (n * NG + (q + 1)))
                    wait(pe, s_add, i * RING + (n * NG + q))
                    for j in range(GRP):
                        c = (j % 2) * 256
                        last = mm(PS[6 + j // 2][:, c:c + D + heads], DOH[:, q * GRP + j, :],
                                  G[:, q * GRP + j, 0:D + heads], start=True, stop=True)
                    last.then_inc(s_sum, 1)

                def body(i, first=False, last=False):
                    for q in range(RING):
                        if not (last and q == RING - 1):
                            turn(*following(i, q))
                        if not (first and q == 0):
                            sums(*before(i, q))
                        if not (last and q == RING - 1):
                            scores(*following(i, q))
                        by_edge(i, q)

                turn(0, 0)
                scores(0, 0)
                body(0, first=True)
                with pe.Fori(1, NI - 1) as i:
                    body(i)
                body(NI - 1, last=True)
                sums(NI - 1, RING - 1)

            def plain(n, turned):
                def body(i):
                    for q in range(RING):
                        pe.wait_ge(s_hot, i * RING + (n * NG + (q + 1)))
                        pe.wait_ge(s_gath[q], (n * NI + i + 1) * (16 * GRP))
                        pe.wait_ge(s_add, i * RING + (n * NG + (q - 1)))
                        for j in range(GRP):
                            rows, hot = G[:, q * GRP + j, :], DOH[:, q * GRP + j, :]
                            if turned:
                                last = mm(PS[q % 2][:, j * P:(j + 1) * P], rows[:, 0:D], hot, start=True, stop=True)
                            else:
                                c = (j % 2) * 256
                                last = mm(PS[2 * (q % 2) + j // 2][:, c:c + D + 1], hot, rows[:, 0:D + 1],
                                          start=True, stop=True)
                        last.then_inc(s_sum, 1)
                steps(pe, NI, body)

            attention_weights(0, 1, W0)
            table(0, 0, w_ext, D + 2)
            attention(0, 1)
            attention_weights(1, H1, W1)
            table(1, 1, w_ext, D + 2 * H1)
            attention(1, H1)
            for k in range(NET + 6):
                pe.wait_ge(s_w, W1 + 16 * (k + 1))
                pe.wait_ge(s_wv, 4 + k)
                tr(PS[0][:, 0:D], raw_w[:, 0:D], ident[:, :]).then_inc(s_wp, 1)
            pe.wait_ge(s_wv, 4 + NET + 6 + 1)
            table(2, 2, wide_w, NET * D)
            pe.wait_ge(s_ht, NBLK)

            def gates(step, i, q):
                if not (isinstance(i, int) and i < 2):
                    pe.wait_ge(s_gt, step * GI + (i - 1))
                a, h = ACCT[:, bass.ds(i * GW, GW)], HT[:, bass.ds(i * GW, GW)]
                for g in range(2):
                    o = PS[2 * q][:, g * GW:(g + 1) * GW]
                    mm(o, w_ih[:, g * D:(g + 1) * D], a, start=True, stop=False)
                    mm(o, w_hh[:, g * D:(g + 1) * D], h, start=False, stop=True)
                mm(PS[2 * q + 1][:, 0:GW], w_ih[:, 2 * D:3 * D], a, start=True, stop=True)
                mm(PS[2 * q + 1][:, GW:2 * GW], w_hh[:, 2 * D:3 * D], h, start=True, stop=True).then_inc(s_g, 1)

            def next_rows(n, i):
                for u in range(2):
                    pe.wait_ge(s_xt, i * 2 + (n * NBLK + (u + 1)))
                    pe.wait_ge(s_ev, i * 2 + (n * NBLK + (u - 1)))
                    mm(PS[4 + u][:, :], XT[:, u, :], wide_w[:, 0:NET * D], start=True, stop=True).then_inc(s_mm, 1)

            def state_step(step, with_table):
                pe.wait_ge(s_add, (step + 3) * NG)
                pe.sem_inc(s_turn, 1)

                def body(i, q):
                    gates(step, i, q)
                    if with_table and not (isinstance(i, int) and i < 2):
                        next_rows(step + 3, i - 2)
                for i in range(3):
                    body(i, i % 2)
                with pe.Fori(0, GI // 2 - 1) as k:
                    for u in range(2):
                        body(k * 2 + (3 + u), (3 + u) % 2)
                if with_table:
                    next_rows(step + 3, GI - 2)
                    next_rows(step + 3, GI - 1)

            with pe.Fori(0, STEPS - 1) as st:
                plain(st + 2, True)
                state_step(st, True)
            plain(STEPS + 1, True)
            state_step(STEPS - 1, False)

            def out_of_state(i):
                for q in range(2):
                    turn_block(3, i, q)
            steps(pe, TBI, out_of_state)
            pe.wait_ge(s_wv, 4 + NET + 6 + 2)
            table(6, 4, wide_w, (NREL + 1) * D)
            plain(6, False)

        @block.scalar
        def _(act):
            def x_block(b):
                return X[:, bass.ds(b, 1), :].rearrange("p a f -> p (a f)")

            def h_block(b):
                return HT[:, bass.ds(b * P, P)]

            def turn_blocks(n, turn, state=False):
                def body(i):
                    for q in range(2):
                        wait(act, s_t, i * 2 + (turn * NBLK + (q - 1)))
                        act.sem_inc(s_turn, 1)
                        act.copy(XS[:, q, :], x_block(i * 2 + q)).then_inc(s_xs, 1)
                        act.wait_ge(s_t, i * 2 + (turn * NBLK + (q + 1)))
                        wait(act, s_mm, i * 2 + (n * NBLK + (q - 1)))
                        if state:
                            act.sem_inc(s_turn, 1)
                            act.copy(h_block(i * 2 + q), PS[q][:, 0:D]).then_inc(s_ht, 1)
                        act.copy(XT[:, q, :], PS[q][:, 0:D]).then_inc(s_xt, 1)
                steps(act, TBI, body, peel=(n == 0))

            def attention(n, heads):
                own = D // heads + 1

                def hot_rows(i, q):
                    act.wait_ge(s_rec[q], (i + (n * NI + 1)) * 16)
                    act.sem_inc(s_turn, 1)
                    for j in range(GRP):
                        ch.done(act.activation(DIST[:, j * P:(j + 1) * P], iota[:, :], ACT.Square, scale=-1.0,
                                               bias=REC[:, q, j, 2:3].bitcast(F32)))
                    ch.wait()
                    act.activation(DOH[:, q * GRP:(q + 1) * GRP, :].rearrange("p a b -> p (a b)"), DIST, ACT.Relu,
                                   scale=-1.0, bias=ones[:, 0:1]).then_inc(s_hot, 1)
                    wait(act, s_v, i * RING + (n * NG + (q - 1)))
                    ch.done(act.activation(NEG[:, q % 2, :, :].rearrange("p a b -> p (a b)"), DIST, ACT.Copy,
                                           scale=-BIG))
                    act.wait_ge(s_gath[q], (i + (n * NI + 1)) * (16 * GRP))
                    act.copy(ESB[:, q % 2, :, 0:heads], G[:, q * GRP:(q + 1) * GRP, own - 1:D + heads:own]
                             ).then_inc(s_neg, 1)
                    ch.restart()

                def turned(i, q):
                    wait(act, s_dt, i * RING + (n * NG + (q + 1)))
                    wait(act, s_eb, i * RING + (n * NG + (q - 1)))
                    act.copy(DTS[:, q % 2, :], PS[4][:, :]).then_inc(s_dts, 1)

                def factors(i, q):
                    wait(act, s_m, i * RING + (n * NG + (q + 1)))
                    wait(act, s_add, i * RING + (n * NG + (q - 1)))
                    act.activation(FEX[:, q % 2, :, 0:heads], FAC[:, q % 2, :, 0:heads], ACT.Exp).then_inc(s_fe, 1)

                def weights(i, q):
                    wait(act, s_se, i * RING + (n * NG + (q + 1)))
                    act.activation(G[:, q * GRP:(q + 1) * GRP, own - 1:D + heads:own], SE[:, :, 0:heads],
                                   ACT.Exp).then_inc(s_pe, 1)

                def body(i, first=False, last=False):
                    for q in range(RING):
                        if not (first and q == 0):
                            weights(*before(i, q))
                        if not (last and q == RING - 1):
                            hot_rows(*following(i, q))
                            turned(*following(i, q))
                        factors(i, q)
                hot_rows(0, 0)
                turned(0, 0)
                body(0, first=True)
                with act.Fori(1, NI - 1) as i:
                    body(i)
                body(NI - 1, last=True)
                weights(NI - 1, RING - 1)

            t1d, t2d = T1[:, :, :], T2[:, :, 0:D]

            def node_phase(base, requests):
                def body(i):
                    for k, (func, o, a) in enumerate(requests):
                        act.wait_ge(s_np, i * len(requests) + (base + k + 1))
                        act.activation(o, a, func).then_inc(s_na, 1)
                steps(act, NPI, body)

            ch = Chain(act, s_ca)
            act.wait_ge(s_xz, 1)
            act.dma_start(X[:, 0:full_b, :], x[0:full_b * P, :].rearrange("(b p) f -> p b f", p=P)).then_inc(s_x, 16)
            act.dma_start(X[0:N - full_b * P, full_b, :], x[full_b * P:N, :]).then_inc(s_x, 16)
            act.wait_ge(s_x, 32)
            turn_blocks(0, 0)
            attention(0, 1)
            square, root = (ACT.Square, t2d, t1d), (ACT.Sqrt, SM[:, 1, :], SM[:, 1, :])
            node_phase(ASK[0], [(ACT.Exp, t2d, t2d), square, root])
            act.wait_ge(s_xr, 1)
            turn_blocks(1, 1)
            attention(1, H1)
            node_phase(ASK[1], [(ACT.Exp, SD[:, :, :], SD[:, :, :]), square, root, (ACT.Gelu, t2d, t1d),
                                  square, root])
            act.wait_ge(s_xr, 2)

            for s in range(2):
                act.wait_ge(s_scat[s], 2 * SCI * SCOL * 16)
            turn_blocks(2, 2, state=True)

            def next_blocks(step, i):
                for u in range(2):
                    act.wait_ge(s_gh, step * GI + (i + 1))
                    act.sem_inc(s_turn, 1)
                    act.wait_ge(s_mm, i * 2 + ((step + 3) * NBLK + (u - 1)))
                    act.sem_inc(s_turn, 1)
                    act.copy(XT[:, u, :], HT[:, bass.ds(i * GW + u * P, P)]).then_inc(s_xt, 1)

            def state_step(step, with_table):
                def body(i, q):
                    act.wait_ge(s_g, step * GI + (i + 1))
                    act.sem_inc(s_turn, 1)
                    if not (isinstance(i, int) and i < 2):
                        act.wait_ge(s_gh, step * GI + (i - 1))
                    for g in range(2):
                        last = act.activation(STG[:, q, 2 * GW + g * GW:2 * GW + (g + 1) * GW],
                                              PS[2 * q][:, g * GW:(g + 1) * GW], ACT.Sigmoid, bias=b_rz[:, g:g + 1])
                    last.then_inc(s_gr, 1)
                    if with_table and not (isinstance(i, int) and i < 2):
                        next_blocks(step, i - 2)
                    act.wait_ge(s_gt, step * GI + (i + 1))
                    act.activation(GATE_T[:, q, GW:2 * GW], GATE_T[:, q, 0:GW], ACT.Tanh,
                                   bias=b_gru[:, 2:3]).then_inc(s_gn, 1)
                for i in range(3):
                    body(i, i % 2)
                with act.Fori(0, GI // 2 - 1) as k:
                    for u in range(2):
                        body(k * 2 + (3 + u), (3 + u) % 2)
                if with_table:
                    next_blocks(step, GI - 2)
                    next_blocks(step, GI - 1)

            with act.Fori(0, STEPS - 1) as st:
                state_step(st, True)
            state_step(STEPS - 1, False)
            act.wait_ge(s_gh, STEPS * GI)

            def out_of_state(i):
                for q in range(2):
                    act.wait_ge(s_t, i * 2 + (3 * NBLK + q - 1))
                    act.sem_inc(s_turn, 1)
                    wait(act, s_xa, i * 2 + (q - 1))
                    act.sem_inc(s_turn, 1)
                    act.copy(XS[:, q, :], h_block(i * 2 + q)).then_inc(s_xs, 1)
            steps(act, TBI, out_of_state, peel=True)
            node_phase(ASK[2], [square, root])
            act.wait_ge(s_xr, 3)
            turn_blocks(6, 4)
            node_phase(ASK[3], [square, root, square, root])

        @block.vector
        def _(dve):
            v = nc.vector
            ch = Chain(dve, s_cv)
            ch.done(v.memset(accf[:, 0:3 * C].bitcast(I32), -1))
            ch.done(v.memset(HT[:, 4 * C:8 * C], 0.0))
            ch.wait()
            dve.sem_inc(s_key, 1)
            ch.done(v.memset(zeros, 0.0))
            ch.done(v.memset(emp[:, :, 0:1], DUMMY))
            ch.done(v.memset(emp[:, :, 1:2], DUMMY * NET))
            ch.done(v.memset(emp[:, :, 2:3].bitcast(F32), -1.0))
            ch.wait()
            dve.sem_inc(s_emp0, 1)
            dve.wait_ge(s_const, 1)
            ch.done(v.tensor_copy(iota[:, :], iotai[:, :]))
            ch.done(v.tensor_copy(identb[:, :], ident[:, :]))
            ch.done(v.tensor_copy(iota_t, iota_ti))
            dve.wait_ge(s_empty, 4 * 16)
            ch.done(v.memset(emp[:, :, 1:2], DUMMY * NREL))
            ch.wait()
            dve.sem_inc(s_emp0, 1)

            dve.wait_ge(s_ints, 8 * 16)
            top, et = tmp_b, tmp_a
            ch.done(v.tensor_reduce(top, attr, AX.X, ALU.max))
            ch.wait()
            ch.done(v.tensor_tensor(et, attr[:, :, 0], top, ALU.is_lt))
            ch.done(v.tensor_tensor(eq, attr[:, :, 1], top, ALU.is_lt))
            ch.done(v.tensor_tensor(pre, attr[:, :, 2], top, ALU.is_lt))
            ch.wait()
            ch.done(v.tensor_tensor(eq, eq, et, ALU.mult))
            ch.wait()
            ch.done(v.tensor_tensor(pre, pre, eq, ALU.mult))
            ch.done(v.tensor_tensor(et, et, eq, ALU.add))
            ch.wait()
            ch.done(v.tensor_tensor(et, et, pre, ALU.add))
            ch.wait()
            ch.done(v.tensor_copy(rec1[:, :, 1], src_i))
            ch.done(v.scalar_tensor_tensor(rec1[:, :, 2], src_i, float(NET), et, ALU.mult, ALU.add))
            ch.done(v.scalar_tensor_tensor(rec2[:, :, 1], dst_i, float(NREL), typ_i, ALU.mult, ALU.add))
            ch.wait()
            tmp_i = tmp_b.bitcast(I32)
            shift = P.bit_length() - 1
            tile_blk = xf[:, 2 * T + 2 * C:2 * T + 2 * C + T]

            def rank(key, key_i, recs, node_word):
                ch.done(v.tensor_scalar(tmp_i, key_i, P - 1, None, ALU.bitwise_and))
                ch.wait()
                ch.done(v.tensor_copy(recs[:, :, node_word].bitcast(F32), tmp_i))
                ch.wait()
                ch.done(v.tensor_scalar(tmp_i, key_i, shift, None, ALU.arith_shift_right))
                ch.wait()
                ch.done(v.tensor_copy(bkt, tmp_i))
                ch.restart()
                with dve.Fori(0, NBLK // 2) as b:
                    for u in range(2):
                        one = bass.ds(b * 2 + u, 1)
                        ch.done(v.tensor_scalar((eq, pre)[u], bkt, iota[:, one], 0.0, ALU.is_equal, ALU.add,
                                                accum_out=CNT[:, one]))
                    ch.restart()
                dve.sem_inc(s_cnt, 1)
                dve.wait_ge(s_pre, key + 1)
                ch.done(v.tensor_scalar(TIL[:, :], PS[0][:, P:P + NBLK], float(P - 1), None, ALU.add))
                ch.wait()
                ch.done(v.tensor_scalar(TIL[:, :], TIL[:, :], shift, None, ALU.arith_shift_right))
                ch.wait()
                ch.done(v.tensor_copy(TOT[:, 0, :], TIL[:, :]))
                ch.wait()
                ch.done(v.tensor_tensor_scan(TOT[:, 1, :], TOT[:, 0, :], zeros[:, 0:NBLK], 0.0, ALU.add, ALU.add))
                ch.wait()
                dve.sem_inc(s_end, 1)
                ch.done(v.tensor_tensor(TOT[:, 2, :], TOT[:, 1, :], TOT[:, 0, :], ALU.subtract))
                ch.wait()
                ch.done(v.scalar_tensor_tensor(BAS[:, :], TOT[:, 2, :], float(P), PS[0][:, 0:NBLK],
                                               ALU.mult, ALU.add))
                dve.wait_ge(s_endt, key + 1)
                ch.done(v.tensor_copy(ENDC[0:NBLK, :], PS[1][0:NBLK, 0:1]))
                ch.wait()
                ch.done(v.tensor_scalar(m_sel[0:NBLK, :], iota_t[0:NBLK, :], ENDC[0:NBLK, :], None, ALU.is_ge))
                ch.wait()
                dve.sem_inc(s_sel, 1)
                for k in range(4):
                    part = slice(k * MW, (k + 1) * MW)
                    dve.wait_ge(s_blk, key * 4 + k + 1)
                    ch.done(v.tensor_scalar((blk_d, blk_s)[key][:, part],
                                            PS[2][32 * key:32 * key + 1, 0:MW], float(NBLK - 1),
                                            None, ALU.min))
                    ch.done(v.tensor_scalar(tile_blk[:, part], PS[2][:, 0:MW], float(NBLK - 1), None, ALU.min))
                    ch.wait()
                    dve.sem_inc(s_blkc, 1)
                if key == 0:
                    ch.done(v.tensor_tensor(LIM[:, 1:T], tile_blk[:, 1:T], tile_blk[:, 0:T - 1], ALU.is_equal))
                    ch.done(v.memset(LIM[:, 0:1], 0.0))
                    ch.wait()
                    ch.done(v.tensor_scalar(LIM[:, :], LIM[:, :], 2 * BIG, -BIG, ALU.mult, ALU.add))
                    ch.wait()
                for k in range(ECH):
                    cols = slice(k * CW, (k + 1) * CW)
                    same = [eq[:, u * CW:(u + 1) * CW] for u in range(2)]
                    seen = [pre[:, u * CW:(u + 1) * CW] for u in range(2)]
                    pos = pre[:, 2 * CW:3 * CW]
                    ch.done(v.memset(pos, 1.0))
                    ch.restart()
                    with dve.Fori(0, NBLK // 2) as b:
                        one = [bass.ds(b * 2 + u, 1) for u in range(2)]
                        is_same = [ch.done(v.tensor_scalar(same[u], bkt[:, cols], iota[:, one[u]], None,
                                                           ALU.is_equal)) for u in range(2)]
                        counted = []
                        for u in range(2):
                            ch.wait(is_same[u])
                            counted.append(ch.done(v.tensor_tensor_scan(seen[u], same[u], zeros[:, 0:CW],
                                                                        BAS[:, one[u]], ALU.add, ALU.add)))
                        for u in range(2):
                            ch.wait(counted[u])
                            if u:
                                ch.wait(placed)
                            placed = ch.done(v.copy_predicated(pos, same[u].bitcast(U32), seen[u]))
                            ch.done(v.tensor_copy(BAS[:, one[u]], seen[u][:, CW - 1:CW]))
                        ch.restart()
                    pos_i, low, high = same[0].bitcast(I32), seen[0].bitcast(I32), pos.bitcast(I32)
                    ch.done(v.tensor_scalar(pos_i, pos, -1.0, None, ALU.add))
                    ch.wait()
                    ch.done(v.tensor_scalar(low, pos_i, P - 1, None, ALU.bitwise_and))
                    ch.done(v.tensor_scalar(high, pos_i, shift, None, ALU.arith_shift_right))
                    ch.wait()
                    ch.done(v.scalar_tensor_tensor(recs[:, cols, 0], low, float(T), high, ALU.mult, ALU.add))
                    ch.done(v.tensor_scalar(same[1], bkt[:, cols], 0.0, None, ALU.is_lt))
                    ch.wait()
                    ch.done(v.copy_predicated(recs[:, cols, 0], same[1].bitcast(U32), trash[:, cols]))
                    ch.wait()
                    dve.sem_inc(s_pos, 1)

            dve.wait_ge(s_empty, 8 * 16)
            rank(0, dst_i, rec1, 3)
            rank(1, src_i, rec2, 2)
            ch.done(v.memset(X[:, NBLK - 1, :], 0.0))
            ch.wait()
            dve.sem_inc(s_xz, 1)

            def attention_weights(n, heads):
                dve.wait_ge(s_wp, n + 1)
                by_head = w_ext[:, 0:D + heads].rearrange("p (h e) -> p h e", h=heads)
                ch.done(v.tensor_copy(by_head[:, :, 0:D // heads], w_t[:, :].rearrange("p (h d) -> p h d", h=heads)))
                ch.wait()
                ch.done(v.tensor_copy(w_t[:, :], PS[3][:, 0:D]))
                ch.wait()
                dve.sem_inc(s_wv, 1)
                dve.wait_ge(s_wa, n + 1)
                ch.done(v.tensor_copy(by_head[:, :, D // heads], PS[3][:, P:P + heads]))
                ch.done(v.tensor_copy(w_ext[:, D + heads:D + 2 * heads], PS[3][:, P + heads:P + 2 * heads]))
                ch.wait()
                dve.sem_inc(s_wv, 1)

            def x_block(b):
                return X[:, bass.ds(b, 1), :].rearrange("p a f -> p (a f)")

            def evacuate(n, width, heads=0, bias=None, self_loop=False):
                def body(i):
                    for q in range(2):
                        b = i * 2 + q
                        dve.wait_ge(s_mm, i * 2 + (n * NBLK + (q + 1)))
                        wait(dve, s_tab[q], (n * TBI + i) * 16)
                        for k in range(-(-width // 512)):
                            w = min(512, width - 512 * k)
                            o, p = STG[:, q, 512 * k:512 * k + w], PS[2 + 3 * q + k][:, 0:w]
                            last = v.tensor_copy(o, p) if bias is None else v.tensor_tensor(o, p, bias, ALU.add)
                        if heads:
                            ch.done(last)
                            last = v.tensor_copy(ED[:, bass.ds(b, 1), 0:heads].rearrange("p a f -> p (a f)"),
                                                 PS[2 + 3 * q][:, D + heads:D + 2 * heads])
                        if self_loop:
                            ch.done(last)
                            last = v.tensor_tensor(x_block(b), x_block(b), PS[4 + 3 * q][:, 0:D], ALU.add)
                        last.then_inc(s_ev, 1)
                    ch.restart()
                ch.restart()
                steps(dve, TBI, body, peel=(isinstance(n, int) and n == 0))

            def clear_sums():
                ch.done(v.memset(accf, 0.0))
                ch.restart()

            def hot_rows(n, i, q):
                dve.wait_ge(s_rec[q], (i + (n * NI + 1)) * 16)
                v.tensor_tensor(DOH[:, q * GRP:(q + 1) * GRP, :],
                                iota[:, :].unsqueeze(1).to_broadcast([P, GRP, P]),
                                bcast(REC[:, q, :, 2].bitcast(F32), P), ALU.is_equal).then_inc(s_hot, 1)

            regs = [[dve.alloc_register(f"blk{k}_{j}") for j in range(GRP)] for k in range(2)]

            def blocks(tile_blocks, g, regs=regs[0]):
                dve.load(regs, tile_blocks[0:1, bass.ds(g * GRP, GRP)])
                return [dve.snap(r, min_val=0, max_val=NBLK - 1) for r in regs]

            def attention(n, heads):
                hs = slice(0, heads)
                own = D // heads + 1

                def step(i, q, prev=True):
                    g = i * RING + q
                    pi, pq = before(i, q)
                    pg = g - 1
                    ed = EDM[:, q % 2, 0, :, hs]
                    blk = blocks(blk_d, g, regs[0])
                    if prev:
                        dve.wait_ge(s_eb, g + n * NG)
                        wait(dve, s_gath[pq], (pi + (n * NI + 1)) * (16 * GRP))
                        eb = PS[5][:, (pq % 2) * 64:(pq % 2) * 64 + GRP * 2 * heads].rearrange(
                            "p (j k h) -> p j k h", j=GRP, k=2)
                        rows = G[:, pq * GRP:(pq + 1) * GRP, 0:D + heads].rearrange("p j (h e) -> p j h e", h=heads)
                        scored = ch.done(v.tensor_tensor(SE[:, :, hs], rows[:, :, :, own - 1], eb[:, :, 0, :], ALU.add))
                    for j in range(2):
                        ch.done(v.tensor_copy(ed[:, j, :], ED[:, bass.ds(blk[j], 1), hs].rearrange("p a h -> p (a h)")))
                    if prev:
                        ch.wait(scored)
                        scored = ch.done(v.scalar_tensor_tensor(SE2[:, :, hs], SE[:, :, hs], SLOPE, SE[:, :, hs],
                                                                ALU.mult, ALU.max))
                    for j in range(2, GRP):
                        ch.done(v.tensor_copy(ed[:, j, :], ED[:, bass.ds(blk[j], 1), hs].rearrange("p a h -> p (a h)")))
                    carried = ch.done(v.tensor_copy(NEW[:, 0, hs], NEW[:, GRP, hs]))
                    if prev:
                        ch.wait(scored)
                        v.tensor_tensor(SE[:, :, hs], SE2[:, :, hs], eb[:, :, 1, :], ALU.subtract).then_inc(s_se, 1)

                    def weigh():
                        dve.wait_ge(s_pe, g + n * NG)
                        v.tensor_tensor(rows[:, :, :, 0:own - 1], rows[:, :, :, 0:own - 1],
                                        rows[:, :, :, own - 1:own].to_broadcast([P, GRP, heads, own - 1]),
                                        ALU.mult).then_inc(s_msg, 1)

                    dve.wait_ge(s_v, g + (n * NG + 1))
                    if heads == 1:
                        v.tensor_reduce(TMAX[:, :, 0], PS[0][:, :].rearrange("p (j e) -> p j e", j=GRP), AX.X,
                                        ALU.max).then_inc(s_red, 1)
                        if prev:
                            weigh()
                    else:
                        for j in range(GRP):
                            if j == GRP // 2 and prev:
                                weigh()
                            last = v.tensor_reduce(TMAX[:, j, :], PS[j][:, :].rearrange("p (h e) -> p h e", h=heads),
                                                   AX.X, ALU.max)
                            if j < GRP - 1:
                                ch.done(last)
                        last.then_inc(s_red, 1)
                    if prev:
                        pblk = blocks(blk_d, pg, regs[1])
                        dve.wait_ge(s_sum, g + n * NG)
                        dve.wait_ge(s_fe, g + n * NG)
                        wait(dve, s_add, g + (n * NG - 1))
                    added = []

                    def add_sums(count):
                        for _ in range(count if prev else 0):
                            j, h = divmod(len(added), heads)
                            if j:
                                ch.wait(added[-heads])
                            cols = slice(h * own, (h + 1) * own)
                            a = ACC[:, bass.ds(pblk[j], 1), cols].rearrange("p a f -> p (a f)")
                            c = (j % 2) * 256
                            ins = v.scalar_tensor_tensor(a, a, FEX[:, pq % 2, j, h:h + 1],
                                                         PS[6 + j // 2][:, c + h * own:c + (h + 1) * own],
                                                         ALU.mult, ALU.add)
                            if len(added) < heads * GRP - 1:
                                added.append(ch.done(ins))
                            else:
                                ins.then_inc(s_add, 1)
                                added.append(None)

                    share = [k * heads // 2 - (k - 1) * heads // 2 if heads > 1 else k % 2 for k in range(1, 9)]
                    dve.wait_ge(s_red, g + (n * NG + 1))
                    ch.wait(carried)
                    for j in range(GRP):
                        last = ch.done(v.scalar_tensor_tensor(NEW[:, j + 1, hs], NEW[:, j, hs],
                                                              LIM[:, bass.ds(g * GRP + j, 1)], TMAX[:, j, hs],
                                                              ALU.min, ALU.max))
                        add_sums(share[j])
                        ch.wait(last)
                        if heads > 1:
                            ch.done(v.tensor_copy(ME[:, bass.ds(blk[j], 1), hs].rearrange("p a h -> p (a h)"),
                                                  NEW[:, j + 1, hs]))
                    last = ch.done(v.tensor_tensor(NEW[:, GRP + 1:2 * GRP + 1, hs], NEW[:, 0:GRP, hs],
                                                   bcast(LIM[:, bass.ds(g * GRP, GRP)], heads), ALU.min))
                    add_sums(share[4])
                    ch.wait(last)
                    last = ch.done(v.tensor_tensor(NO[:, :, :, hs],
                                                   NEW[:, 1:2 * GRP + 1, hs].rearrange("p (k j) h -> p k j h", k=2),
                                                   ed.unsqueeze(1).to_broadcast([P, 2, GRP, heads]), ALU.add))
                    add_sums(share[5])
                    ch.wait(last)
                    last = ch.done(v.scalar_tensor_tensor(EDM[:, q % 2, 1:3, :, hs].rearrange("p k j h -> p (k j) h"),
                                                          NO[:, :, :, hs].rearrange("p k j h -> p (k j) h"), SLOPE,
                                                          NO[:, :, :, hs].rearrange("p k j h -> p (k j) h"),
                                                          ALU.mult, ALU.max))
                    add_sums(share[6])
                    ch.wait(last)
                    v.tensor_tensor(FAC[:, q % 2, :, hs], EDM[:, q % 2, 2, :, hs], EDM[:, q % 2, 1, :, hs],
                                    ALU.subtract).then_inc(s_m, 1)
                    add_sums(share[7])
                    assert not prev or len(added) == heads * GRP

                def last_sums():
                    g = NG
                    pq = RING - 1
                    dve.wait_ge(s_eb, g + n * NG)
                    dve.wait_ge(s_gath[pq], (n + 1) * NI * 16 * GRP)
                    eb = PS[5][:, 64:64 + GRP * 2 * heads].rearrange("p (j k h) -> p j k h", j=GRP, k=2)
                    rows = G[:, pq * GRP:(pq + 1) * GRP, 0:D + heads].rearrange("p j (h e) -> p j h e", h=heads)
                    ch.done(v.tensor_tensor(SE[:, :, hs], rows[:, :, :, own - 1], eb[:, :, 0, :], ALU.add))
                    ch.wait()
                    ch.done(v.scalar_tensor_tensor(SE2[:, :, hs], SE[:, :, hs], SLOPE, SE[:, :, hs],
                                                   ALU.mult, ALU.max))
                    ch.wait()
                    v.tensor_tensor(SE[:, :, hs], SE2[:, :, hs], eb[:, :, 1, :], ALU.subtract).then_inc(s_se, 1)
                    dve.wait_ge(s_pe, g + n * NG)
                    v.tensor_tensor(rows[:, :, :, 0:own - 1], rows[:, :, :, 0:own - 1],
                                    rows[:, :, :, own - 1:own].to_broadcast([P, GRP, heads, own - 1]),
                                    ALU.mult).then_inc(s_msg, 1)
                    blk = blocks(blk_d, NG - 1)
                    dve.wait_ge(s_sum, g + n * NG)
                    dve.wait_ge(s_fe, g + n * NG)
                    dve.wait_ge(s_add, g + n * NG - 1)
                    for j in range(GRP):
                        c = (j % 2) * 256
                        for h in range(heads):
                            a = ACC[:, bass.ds(blk[j], 1), h * own:(h + 1) * own].rearrange("p a f -> p (a f)")
                            last = v.scalar_tensor_tensor(a, a, FEX[:, pq % 2, j, h:h + 1],
                                                          PS[6 + j // 2][:, c + h * own:c + (h + 1) * own],
                                                          ALU.mult, ALU.add)
                            if (j, h) != (GRP - 1, heads - 1):
                                ch.done(last)
                        ch.wait()
                    last.then_inc(s_add, 1)
                    dve.wait_ge(s_add, (n + 1) * NG)

                def body(i, first=False):
                    for q in range(RING):
                        step(i, q, prev=not (first and q == 0))
                    ch.restart()

                ch.done(v.memset(NEW[:, GRP, :], -BIG))
                ch.done(v.memset(ME[:, :, :], -BIG))
                clear_sums()
                body(0, first=True)
                with dve.Fori(1, NI) as i:
                    body(i)
                last_sums()

            def plain(n, turned, tile_blocks):
                def add(i, q):
                    g = i * RING + q
                    blk = blocks(tile_blocks, g)
                    dve.wait_ge(s_sum, g + (n * NG + 1))
                    dve.wait_ge(s_add, g + n * NG)
                    for j in range(GRP):
                        if turned:
                            a = ACCT[:, bass.ds(blk[j] * P, P)]
                            s = PS[q % 2][:, j * P:(j + 1) * P]
                        else:
                            a = ACC[:, bass.ds(blk[j], 1), 0:D + 1].rearrange("p a f -> p (a f)")
                            s = PS[2 * (q % 2) + j // 2][:, (j % 2) * 256:(j % 2) * 256 + D + 1]
                        last = v.tensor_tensor(a, a, s, ALU.add)
                        if j < GRP - 1:
                            ch.done(last)
                            ch.wait()
                    last.then_inc(s_add, 1)

                def body(i, first=False):
                    for q in range(RING):
                        hot_rows(n, i, q)
                        if not (first and q == 0):
                            add(*before(i, q))
                    ch.restart()
                clear_sums()
                body(0, first=True)
                with dve.Fori(1, NI) as i:
                    body(i)
                add(NI - 1, RING - 1)
                ch.restart()
                dve.wait_ge(s_add, (n + 1) * NG)
                dve.sem_inc(s_turn, 1)

            sm = [SM[:, k, :] for k in range(3)]
            t1d, t2d = T1[:, :, :], T2[:, :, 0:D]

            def rows(tile):
                return tile[:, :].unsqueeze(1).to_broadcast([P, NPB, D])

            def tt(o, a, b, op):
                ch.done(v.tensor_tensor(o, a, b, op))
                ch.wait()

            def ts(o, a, s1, s2, op0, op1=ALU.bypass):
                if s2 is None:
                    ch.done(v.tensor_scalar(o, a, s1, None, op0))
                else:
                    ch.done(v.tensor_scalar(o, a, s1, s2, op0, op1))
                ch.wait()

            def stt(o, a, s, b, op0, op1):
                ch.done(v.scalar_tensor_tensor(o, a, s, b, op0, op1))
                ch.wait()

            def node_phase(base, per, body):
                def step(i):
                    asked = [0]

                    def ask():
                        asked[0] += 1
                        ch.wait()
                        dve.sem_inc(s_np, 1)
                        dve.wait_ge(s_na, i * per + (base + asked[0]))
                    body(i, ask)
                    assert asked[0] == per
                    ch.restart()
                ch.restart()
                steps(dve, NPI, step)

            def normalize(dest, ask):
                ch.done(v.tensor_reduce(sm[0], t1d, AX.X, ALU.add))
                ch.wait()
                ts(sm[0], sm[0], 1.0 / D, None, ALU.mult)
                tt(t1d, t1d, bcast(sm[0], D), ALU.subtract)
                ask()
                ch.done(v.tensor_reduce(sm[1], t2d, AX.X, ALU.add))
                ch.wait()
                ts(sm[1], sm[1], 1.0 / D, EPS, ALU.mult, ALU.add)
                ask()
                ch.done(v.reciprocal(sm[1], sm[1]))
                ch.wait()
                tt(dest, t1d, bcast(sm[1], D), ALU.mult)

            def new_x_complete():
                ch.done(v.tensor_scalar(X[:, NBLK - 1, :], X[:, NBLK - 1, :], maskc[:, :], None, ALU.mult))
                ch.wait()
                dve.sem_inc(s_xr, 1)

            dve.wait_ge(s_x, 32)
            attention_weights(0, 1)
            evacuate(0, D + 1, heads=1)
            attention(0, 1)

            def nodes0(i, ask):
                bs = bass.ds(i * NPB, NPB)
                ts(sm[2], ACC[:, bs, D], 1e-15, None, ALU.max)
                ch.done(v.reciprocal(sm[2], sm[2]))
                ch.wait()
                tt(t1d, ACC[:, bs, 0:D], bcast(sm[2], D), ALU.mult)
                tt(t1d, t1d, rows(bias_b), ALU.add)
                ts(t2d, t1d, 0.0, None, ALU.min)
                ask()
                stt(t1d, t1d, 0.0, t2d, ALU.max, ALU.add)
                stt(t1d, t1d, -1.0, X[:, bs, :], ALU.add, ALU.add)
                normalize(X[:, bs, :], ask)
            node_phase(ASK[0], 3, nodes0)
            ch.done(v.memset(att[:, :], 0.0))
            new_x_complete()

            attention_weights(1, H1)
            evacuate(1, D + H1, heads=H1)
            attention(1, H1)

            def nodes1(i, ask):
                bs = bass.ds(i * NPB, NPB)
                dve.sem_inc(s_hru, 1)
                dve.wait_ge(s_hr, (i + 1) * 16)

                def heads_of(ap):
                    return ap.rearrange("p b (h d) -> p b h d", h=H1)

                acc_h, own_h = heads_of(ACC[:, bs, :]), heads_of(T2[:, :, :])

                def per_row(ap):
                    return ap.rearrange("p (b h) -> p b h", h=H1).unsqueeze(3).to_broadcast([P, NPB, H1, HD])

                def small(ap):
                    return ap.rearrange("p (b h) -> p b h", h=H1)
                tt(small(SA[:, 0, :]), ME[:, bs, :], ED[:, bs, :], ALU.add)
                tt(small(SA[:, 2, :]), own_h[:, :, :, HD], ED[:, bs, :], ALU.add)
                tt(SA[:, 1, :], SA[:, 0, :], SA[:, 2, :], ALU.max)
                stt(SC[:, :, :], SA[:, :, :], SLOPE, SA[:, :, :], ALU.mult, ALU.max)
                tt(SD[:, 0, :], SC[:, 0, :], SC[:, 1, :], ALU.subtract)
                tt(SD[:, 1, :], SC[:, 2, :], SC[:, 1, :], ALU.subtract)
                ask()
                tt(heads_of(t1d), acc_h[:, :, :, 0:HD], per_row(SD[:, 0, :]), ALU.mult)
                tt(own_h[:, :, :, 0:HD], own_h[:, :, :, 0:HD], per_row(SD[:, 1, :]), ALU.mult)
                tt(heads_of(t1d), heads_of(t1d), own_h[:, :, :, 0:HD], ALU.add)
                tt(small(SA[:, 0, :]), acc_h[:, :, :, HD], small(SD[:, 0, :]), ALU.mult)
                stt(SA[:, 0, :], SA[:, 0, :], 1e-16, SD[:, 1, :], ALU.add, ALU.add)
                ch.done(v.reciprocal(SA[:, 1, :], SA[:, 0, :]))
                ch.wait()
                tt(heads_of(t1d), heads_of(t1d), per_row(SA[:, 1, :]), ALU.mult)
                tt(t1d, t1d, rows(bias_b), ALU.add)
                normalize(t1d, ask)
                tt(t1d, t1d, rows(gamma_b), ALU.mult)
                tt(t1d, t1d, rows(beta_b), ALU.add)
                ask()
                tt(t1d, t2d, X[:, bs, :], ALU.add)
                normalize(X[:, bs, :], ask)
            node_phase(ASK[1], 6, nodes1)
            new_x_complete()

            for k in range(NET + 6):
                dve.wait_ge(s_wp, 2 + k + 1)
                g = k - NET
                o = wide_w[:, k * D:(k + 1) * D] if k < NET else (w_ih, w_hh)[g // 3][:, (g % 3) * D:(g % 3 + 1) * D]
                ch.done(v.tensor_copy(o, PS[0][:, 0:D]))
                ch.wait()
                dve.sem_inc(s_wv, 1)
            dve.wait_ge(s_w, W2)
            tt(b_rz[:, :], b_gru[:, 0:2], b_gru[:, 3:5], ALU.add)
            dve.sem_inc(s_wv, 1)
            evacuate(2, NET * D, bias=wide_b[:, :])
            dve.wait_ge(s_ht, NBLK)
            ch.restart()

            def next_rows(n, i, u):
                dve.wait_ge(s_mm, i * 2 + (n * NBLK + (u + 1)))
                dve.sem_inc(s_turn, 1)
                dve.wait_ge(s_tab[u], (n * TBI + i) * 16)
                v.tensor_tensor(STG[:, u, 0:NET * D], PS[4 + u][:, :], wide_b[:, :], ALU.add).then_inc(s_ev, 1)

            def state_step(step, with_table):
                def body(i, q):
                    rows_too = with_table and not (isinstance(i, int) and i < 3)
                    h = HT[:, bass.ds(i * GW, GW)]
                    r, z = STG[:, q, 2 * GW:3 * GW], STG[:, q, 3 * GW:4 * GW]
                    t, n = GATE_T[:, q, 0:GW], GATE_T[:, q, GW:2 * GW]
                    dve.wait_ge(s_gr, step * GI + (i + 1))
                    ch.done(v.scalar_tensor_tensor(t, PS[2 * q + 1][:, GW:2 * GW], b_gru[:, 5:6], r, ALU.add, ALU.mult))
                    ch.wait()
                    v.tensor_tensor(t, t, PS[2 * q + 1][:, 0:GW], ALU.add).then_inc(s_gt, 1)
                    if rows_too:
                        next_rows(step + 3, i - 3, 0)
                    dve.wait_ge(s_gn, step * GI + (i + 1))
                    dve.sem_inc(s_turn, 1)
                    last = ch.done(v.tensor_tensor(h, h, n, ALU.subtract))
                    if rows_too:
                        next_rows(step + 3, i - 3, 1)
                    ch.wait(last)
                    ch.done(v.tensor_tensor(h, h, z, ALU.mult))
                    ch.wait()
                    v.tensor_tensor(h, h, n, ALU.add).then_inc(s_gh, 1)
                for i in range(3):
                    body(i, i % 2)
                ch.restart()
                with dve.Fori(0, GI // 2 - 1) as k:
                    for u in range(2):
                        body(k * 2 + (3 + u), (3 + u) % 2)
                    ch.restart()
                if with_table:
                    for i in range(GI - 3, GI):
                        for u in range(2):
                            next_rows(step + 3, i, u)
                dve.wait_ge(s_gh, (step + 1) * GI)
                dve.sem_inc(s_turn, 1)

            with dve.Fori(0, STEPS - 1) as st:
                plain(st + 2, True, blk_d)
                state_step(st, True)
            plain(STEPS + 1, True, blk_d)
            state_step(STEPS - 1, False)

            def add_state(i):
                for q in range(2):
                    dve.wait_ge(s_t, i * 2 + (3 * NBLK + q + 1))
                    b = i * 2 + q
                    v.tensor_tensor(x_block(b), x_block(b), PS[q][:, 0:D], ALU.add).then_inc(s_xa, 1)
            steps(dve, TBI, add_state)
            dve.wait_ge(s_xa, NBLK)

            def nodes2(i, ask):
                bs = bass.ds(i * NPB, NPB)
                ch.done(v.tensor_copy(t1d, X[:, bs, :]))
                ch.wait()
                normalize(X[:, bs, :], ask)
            node_phase(ASK[2], 2, nodes2)
            new_x_complete()

            dve.wait_ge(s_w, W3)
            for r in range(NREL):
                w_r = wide_w[:, r * D:(r + 1) * D]
                ts(w_r, raw_w[:, 0:D], alpha_b[:, r * NBASE:r * NBASE + 1], None, ALU.mult)
                for b in range(1, NBASE):
                    stt(w_r, raw_w[:, b * D:(b + 1) * D], alpha_b[:, r * NBASE + b:r * NBASE + b + 1], w_r,
                        ALU.mult, ALU.add)
            tt(beta_b[:, :], beta_b[:, :], bias_b[:, :], ALU.add)
            ch.done(v.memset(G[:, :, D:D + 1], 1.0))
            ch.wait()
            dve.sem_inc(s_wv, 1)
            evacuate(6, NREL * D, self_loop=True)
            plain(6, False, blk_s)

            def nodes3(i, ask):
                bs = bass.ds(i * NPB, NPB)
                ts(sm[2], ACC[:, bs, D], 1.0, None, ALU.max)
                ch.done(v.reciprocal(sm[2], sm[2]))
                ch.wait()
                tt(t1d, ACC[:, bs, 0:D], bcast(sm[2], D), ALU.mult)
                normalize(t1d, ask)
                tt(t1d, t1d, rows(gamma_b), ALU.mult)
                tt(t1d, t1d, rows(beta_b), ALU.add)
                tt(t1d, t1d, X[:, bs, :], ALU.add)
                normalize(X[:, bs, :], ask)
            node_phase(ASK[3], 4, nodes3)
            dve.sem_inc(s_on, 1)


_INS = ['x', 'src', 'dst', 'edge_attr_4', 'edge_type_8',
        'L0_gnn_W', 'L0_gnn_a_src', 'L0_gnn_a_dst', 'L0_gnn_bias',
        'L1_gnn_W', 'L1_gnn_att_src', 'L1_gnn_att_dst', 'L1_gnn_bias', 'L1_gnn_gamma', 'L1_gnn_beta',
        'L2_gnn_W_edge', 'L2_gnn_b_edge', 'L2_gnn_W_ih', 'L2_gnn_W_hh', 'L2_gnn_b_ih', 'L2_gnn_b_hh',
        'L3_gnn_weight', 'L3_gnn_alpha', 'L3_gnn_bias', 'L3_gnn_weight_self_loop', 'L3_gnn_ln_gamma',
        'L3_gnn_ln_beta']


def kernel(**inputs):
    import numpy as _np
    import concourse.bacc as _bacc
    from concourse import mybir as _mybir
    from concourse.bass_utils import run_bass_kernel_spmd as _run

    nc = _bacc.Bacc("TRN2", target_bir_lowering=False, num_devices=1)
    arrays, args = {}, []
    for name in _INS:
        a = _np.ascontiguousarray(inputs[name])
        arrays[f"in_{name}"] = a
        args.append(nc.dram_tensor(f"in_{name}", a.shape, _mybir.dt.from_np(a.dtype), kind="ExternalInput").ap())
    args.append(nc.dram_tensor("out_x", (N, D), F32, kind="ExternalOutput").ap())
    build(nc, *args)
    r = _run(nc, [arrays], core_ids=[0])
    return r.results[0]["out_x"]
```

```python
import concourse.bass as bass
from concourse import mybir
from contextlib import ExitStack

F32 = mybir.dt.float32
BF16 = mybir.dt.bfloat16
I32 = mybir.dt.int32
U32 = mybir.dt.uint32
ALU = mybir.AluOpType
ACT = mybir.ActivationFunctionType
AX = mybir.AxisListType

P = 128
N = 12500
E = 200000
D = 128
NBLK = -(-N // P)
NPAD = NBLK * P
ECOL = -(-E // P)
ELAST = E - (P - 1) * ECOL
SCOL = 4
ECH = 7
C = -(-ECOL // (2 * SCOL)) * 2 * SCOL
CW = C // ECH
GRP = 4
RING = 4
BODY = GRP * RING
AR = 2 * RING
T = -(-((E + NBLK * (P - 1)) // P) // BODY) * BODY
NG = T // GRP
NI = T // BODY
NIA = NG // AR
H1 = 4
HD = D // H1
NET = 4
NREL = 8
NBASE = 4
STEPS = 4
NPB = 7
NPI = NBLK // NPB
TBI = NBLK // 2
GW = 256
GI = NPAD // GW
BIG = 1e30
DUMMY = N
WROW = D + H1
EPS = 1e-5
SLOPE = 0.2
MW = T // 4
SCI = C // (2 * SCOL)
SCK = CW // (2 * SCOL)
SC_A, SC_B, SC_L1 = SCK, 36, NI
SC_C = SCI - SC_A - SC_B - SC_L1
assert SC_C % NPI == 0
assert C % ECH == 0 and CW % (2 * SCOL) == 0 and SC_C > 0 and GI % 2 == 1 and NBLK == 2 * GI
ASK = [0, 3 * NPI, 9 * NPI, 11 * NPI]
assert NI % 2 == 0 and NBLK % (2 * NPB) == 0 and C >= ECOL and MW <= 512 and NPAD % GW == 0


def wait(eng, sem, value):
    if isinstance(value, int) and value <= 0:
        return
    eng.wait_ge(sem, value)


def steps(eng, count, body, peel=False):
    if peel:
        body(0)
    with eng.Fori(1 if peel else 0, count) as i:
        body(i)


def off(i, q, ring, by):
    return i + (q + by) // ring, (q + by) % ring


class Chain:

    def __init__(self, eng, sem):
        self.eng, self.sem, self.n = eng, sem, 0

    def done(self, ins):
        ins.then_inc(self.sem, 1)
        self.n += 1
        return self.n

    def wait(self, n=None):
        wait(self.eng, self.sem, self.n if n is None else n)

    def restart(self):
        self.wait()
        if self.n:
            self.eng.sem_clear(self.sem)
        self.n = 0


def build(nc, x, src, dst, edge_attr_4, edge_type_8,
          L0_gnn_W, L0_gnn_a_src, L0_gnn_a_dst, L0_gnn_bias,
          L1_gnn_W, L1_gnn_att_src, L1_gnn_att_dst, L1_gnn_bias, L1_gnn_gamma, L1_gnn_beta,
          L2_gnn_W_edge, L2_gnn_b_edge, L2_gnn_W_ih, L2_gnn_W_hh, L2_gnn_b_ih, L2_gnn_b_hh,
          L3_gnn_weight, L3_gnn_alpha, L3_gnn_bias, L3_gnn_weight_self_loop, L3_gnn_ln_gamma, L3_gnn_ln_beta,
          out):
    ctx = ExitStack()
    with ctx:
        def sb(name, shape, dt=F32):
            return ctx.enter_context(nc.sbuf_tensor(name, shape, dt))

        def sem(name):
            return ctx.enter_context(nc.semaphore(name))

        def dram(name, shape, dt=F32):
            return nc.dram_tensor(name, shape, dt, kind="Internal").ap()

        rec_dst = dram("rec_dst", [P * T + P * C, 3], I32)
        rec_src = dram("rec_src", [P * T + P * C, 2], I32)
        tab0 = dram("tab0", [NPAD, D + 1])
        tab1 = dram("tab1", [NPAD, D + H1])
        tab2 = dram("tab2", [NPAD * NET, D])
        tab3 = dram("tab3", [NPAD * NREL, D])

        X = sb("X", [P, NBLK, D])
        HT = sb("HT", [P, NPAD])
        ACC = sb("ACC", [P, NBLK, WROW])
        ACCT = ACC[:, :, :].rearrange("p b w -> p (b w)")[:, 0:NPAD]
        G = sb("G", [P, BODY, WROW])
        STG = sb("STG", [P, 2, NREL * D])
        DOH = STG[:, :, :].rearrange("p a b -> p (a b)")[:, 0:BODY * P].rearrange("p (a b) -> p a b", b=P)
        node_tmp = sb("node_tmp", [P, NPB * (D + WROW)])
        GATE_T = node_tmp[:, 0:4 * GW].rearrange("p (a b) -> p a b", a=2)
        T1 = node_tmp[:, 0:NPB * D].rearrange("p (a b) -> p a b", b=D)
        T2 = node_tmp[:, NPB * D:].rearrange("p (a b) -> p a b", b=WROW)
        DTS = node_tmp[:, 0:2 * GRP * P].rearrange("p (a b) -> p a b", a=2)
        NEG = node_tmp[:, 2 * GRP * P:3 * GRP * P].bitcast(BF16).rearrange("p (a j e) -> p a j e", a=2, j=GRP)
        by_layer = sb("by_layer", [P, (NREL + 1 + NET + 6 + NBASE) * D])

        def part(width):
            taken[0] += width
            return by_layer[:, taken[0] - width:taken[0]]
        taken = [0]
        LIM = part(T)
        ME = part(NBLK * H1).rearrange("p (b h) -> p b h", h=H1)
        ED = part(NBLK * H1).rearrange("p (b h) -> p b h", h=H1)
        taken[0] = 0
        wide_w = part((NREL + 1) * D)
        wide_b = part(NET * D)
        w_ih = part(3 * D)
        w_hh = part(3 * D)
        raw_w = part(NBASE * D)
        REC = sb("REC", [P, AR, GRP, 3], I32)
        ident = sb("ident", [P, P])
        identb = sb("identb", [P, P], BF16)
        ones = sb("ones", [P, P])
        lower = sb("lower", [P, P])
        iota = sb("iota", [P, P])
        iotai = sb("iotai", [P, P], I32)
        maskc = sb("maskc", [P, 1])
        tile_blocks = sb("tile_blocks", [33, T], I32)
        blk_d, blk_s = tile_blocks[0:1, :], tile_blocks[32:33, :]
        w_ext = sb("w_ext", [P, D + 2 * H1])
        w_t = sb("w_t", [P, D])
        att = sb("att", [P, 2 * H1])
        bias_b = sb("bias_b", [P, D])
        gamma_b = sb("gamma_b", [P, D])
        beta_b = sb("beta_b", [P, D])
        b_gru = sb("b_gru", [P, 6])
        b_rz = sb("b_rz", [P, 2])
        alpha_b = sb("alpha_b", [P, NREL * NBASE])
        XS = sb("XS", [P, 2, D])
        XT = sb("XT", [P, 2, D])
        SM = sb("SM", [P, 3, NPB])
        SA = sb("SA", [P, 3, NPB * H1])
        SC = sb("SC", [P, 3, NPB * H1])
        SD = sb("SD", [P, 2, NPB * H1])
        ESB = sb("ESB", [P, 2, GRP, H1], BF16)
        TMAX = sb("TMAX", [P, GRP, H1])
        NEW = sb("NEW", [P, 2 * GRP + 1, H1])
        NO = sb("NO", [P, 2, GRP, H1])
        EDM = sb("EDM", [P, 2, 3, GRP, H1])
        FAC = sb("FAC", [P, 2, GRP, H1])
        FEX = sb("FEX", [P, 2, GRP, H1])
        SE = sb("SE", [P, GRP, H1])
        SE2 = sb("SE2", [P, GRP, H1])

        accf = ACC[:, :, :].rearrange("p b w -> p (b w)")
        xf = X[:, :, :].rearrange("p b w -> p (b w)")
        src_i = accf[:, 0 * C:1 * C].bitcast(I32)
        dst_i = accf[:, 1 * C:2 * C].bitcast(I32)
        typ_i = accf[:, 2 * C:3 * C].bitcast(I32)
        bkt = accf[:, 3 * C:4 * C]
        tmp_a = accf[:, 4 * C:5 * C]
        tmp_b = accf[:, 5 * C:6 * C]
        m_sel = accf[:, 6 * C:6 * C + T]
        attr = HT[:, 4 * C:8 * C].rearrange("p (c f) -> p c f", f=4)
        rec1 = HT[:, 0:4 * C].bitcast(I32).rearrange("p (c f) -> p c f", f=4)
        rec2 = HT[:, 5 * C:8 * C].bitcast(I32).rearrange("p (c f) -> p c f", f=3)
        DIST = HT[:, 0:GRP * P]
        GA = HT[:, GRP * P:GRP * P + AR * GRP * WROW].rearrange("p (a b) -> p a b", b=WROW)
        assert GRP * P + AR * GRP * WROW <= 5 * C and 8 * C <= NPAD and 6 * C + T <= NBLK * WROW
        iota_t = xf[:, 0:T]
        iota_ti = xf[:, T:2 * T].bitcast(I32)
        trash = xf[:, 2 * T:2 * T + C].bitcast(I32)
        zeros = xf[:, 2 * T + C:2 * T + 2 * C]
        eq = xf[:, 2 * T + 2 * C:2 * T + 3 * C]
        pre = xf[:, 2 * T + 3 * C:2 * T + 4 * C]
        emp = xf[:, 2 * T + 4 * C:2 * T + 4 * C + 3 * MW].bitcast(I32).rearrange("p (c f) -> p c f", f=3)
        small = xf[:, 2 * T + 4 * C + 3 * MW:]
        CNT, BAS = small[:, 0:NBLK], small[:, NBLK:2 * NBLK]
        TOT = small[:, 2 * NBLK:5 * NBLK].rearrange("p (k b) -> p k b", k=3)
        TIL = small[:, 5 * NBLK:6 * NBLK].bitcast(I32)
        ENDC = small[:, 6 * NBLK:6 * NBLK + 1]
        STGS = sb("STGS", [P, 2, SCOL, 4], I32)
        STG2 = sb("STG2", [P, 2, SCOL, 3], I32)

        PS = [ctx.enter_context(nc.psum_tensor(f"PS{i}", [P, 512], F32)) for i in range(8)]

        s_ints = sem("s_ints")
        s_const = sem("s_const")
        s_key = sem("s_key")
        s_empty = sem("s_empty")
        s_emp0 = sem("s_emp0")
        s_cnt = sem("s_cnt")
        s_pre = sem("s_pre")
        s_end = sem("s_end")
        s_endt = sem("s_endt")
        s_sel = sem("s_sel")
        s_blk = sem("s_blk")
        s_blkc = sem("s_blkc")
        s_pos = sem("s_pos")
        s_stage = [sem(f"s_stage{i}") for i in range(2)]
        s_scat = [sem(f"s_scat{i}") for i in range(2)]
        s_x = sem("s_x")
        s_xz = sem("s_xz")
        s_w = sem("s_w")
        s_wp = sem("s_wp")
        s_wa = sem("s_wa")
        s_wv = sem("s_wv")
        s_acc0 = sem("s_acc0")
        s_rec = [sem(f"s_rec{i}") for i in range(RING)]
        s_gath = [sem(f"s_gath{i}") for i in range(RING)]
        s_rec_a = [sem(f"s_rec_a{i}") for i in range(AR)]
        s_gath_a = [sem(f"s_gath_a{i}") for i in range(AR)]
        s_hot = sem("s_hot")
        s_neg = sem("s_neg")
        s_dt = sem("s_dt")
        s_dts = sem("s_dts")
        s_v = sem("s_v")
        s_red = sem("s_red")
        s_m = sem("s_m")
        s_fe = sem("s_fe")
        s_eb = sem("s_eb")
        s_se = sem("s_se")
        s_pe = sem("s_pe")
        s_msg = sem("s_msg")
        s_sum = sem("s_sum")
        s_add = sem("s_add")
        s_turn = sem("s_turn")
        s_xs = sem("s_xs")
        s_t = sem("s_t")
        s_xt = sem("s_xt")
        s_mm = sem("s_mm")
        s_ev = sem("s_ev")
        s_tab = [sem(f"s_tab{i}") for i in range(2)]
        s_np = sem("s_np")
        s_na = sem("s_na")
        s_hr = sem("s_hr")
        s_hru = sem("s_hru")
        s_xr = sem("s_xr")
        s_g = sem("s_g")
        s_gr = sem("s_gr")
        s_gt = sem("s_gt")
        s_gn = sem("s_gn")
        s_gh = sem("s_gh")
        s_on = sem("s_on")
        s_out = sem("s_out")
        s_cv = sem("s_cv")
        s_ca = sem("s_ca")
        s_cp = sem("s_cp")
        s_tb_all = sem("s_tb_all")
        s_ht = sem("s_ht")
        s_xa = sem("s_xa")

        block = ctx.enter_context(nc.Block())


        def bcast(ap, n):
            return ap.unsqueeze(2).to_broadcast([ap.shape[0], ap.shape[1], n])

        def row_of(vec):
            return vec.rearrange("(a n) -> a n", a=1).to_broadcast([P, vec.shape[0]])

        W0 = 4 * 16
        W1 = W0 + (4 + 2 * H1) * 16
        W2M = W1 + (NET + 6) * 16
        W2 = W2M + (6 + NET) * 16
        W3 = W2 + (NBASE + 5) * 16
        full = (P - 1) * ECOL
        full_b = N // P

        @block.sync
        def _(sp):
            sp.wait_ge(s_key, 1)
            for vec, tile in ((dst, dst_i), (src, src_i), (edge_type_8, typ_i)):
                sp.dma_start(tile[0:P - 1, 0:ECOL], vec[0:full].rearrange("(p c) -> p c", p=P - 1)).then_inc(s_ints, 16)
                sp.dma_start(tile[P - 1:P, 0:ELAST], vec[full:E].rearrange("(p c) -> p c", p=1)).then_inc(s_ints, 16)
            sp.dma_start(attr[0:P - 1, 0:ECOL, :],
                         edge_attr_4[0:full, :].rearrange("(p c) f -> p c f", p=P - 1)).then_inc(s_ints, 16)
            sp.dma_start(attr[P - 1:P, 0:ELAST, :],
                         edge_attr_4[full:E, :].rearrange("(p c) f -> p c f", p=1)).then_inc(s_ints, 16)

            def prefill(recs, words, ready):
                sp.wait_ge(s_emp0, ready)
                view = recs[0:P * T, :].rearrange("(p t) f -> p t f", p=P)
                for k in range(4):
                    sp.dma_start(view[:, k * MW:(k + 1) * MW, :], emp[:, :, words]).then_inc(s_empty, 16)

            prefill(rec_dst, slice(0, 3), 1)
            prefill(rec_src, slice(1, 3), 2)

            def load_w(pairs):
                for tile, ap in pairs:
                    sp.dma_start(tile, ap).then_inc(s_w, 16)

            load_w([(w_t[:, :], L0_gnn_W), (att[:, 0:1], L0_gnn_a_src.rearrange("(n a) -> n a", a=1)),
                    (att[:, 1:2], L0_gnn_a_dst.rearrange("(n a) -> n a", a=1)), (bias_b[:, :], row_of(L0_gnn_bias))])

            def stage_columns(key, s, i, first=0):
                recs, stage, width = ((rec1, STGS, 4), (rec2, STG2, 3))[key]
                wait(sp, s_scat[s], (i + (key * SCI + first)) * (16 * SCOL))
                sp.dma_start(stage[:, s, :, :].rearrange("p c f -> p (c f)"),
                             recs.rearrange("p c f -> p (c f)")[:, bass.ds((i * 2 + (first * 2 + s)) * (SCOL * width),
                                                                          SCOL * width)]).then_inc(s_stage[s], 16)

            def stage_steps(key, first, count):
                def body(i):
                    for s in range(2):
                        stage_columns(key, s, i, first)
                steps(sp, count, body, peel=(key == 0 and first == 0))

            for k in range(ECH):
                sp.wait_ge(s_pos, k + 1)
                stage_steps(0, k * SCK, SCK)
            sp.wait_ge(s_pos, ECH + 1)
            stage_steps(1, 0, SC_A)

            def store_table(n, table, rows):
                width = table.shape[1] * rows

                def body(i):
                    for q in range(2):
                        sp.wait_ge(s_ev, i * 2 + (n * NBLK + (q + 1)))
                        sp.dma_start(table[bass.ds((i * 2 + q) * (P * rows), P * rows), :]
                                     .rearrange("(p r) f -> p (r f)", p=P), STG[:, q, 0:width]).then_inc(s_tab[q], 16)
                steps(sp, TBI, body)
                for q in range(2):
                    sp.wait_ge(s_tab[q], (n + 1) * (16 * TBI))
                    sp.sem_inc(s_turn, 1)
                sp.sem_inc(s_tb_all, 1)

            def load_group(n, i, q, ring, base, view, width, recs_ready, gathered):
                wait(sp, gathered[q], (base * (NG // ring) + i) * (16 * GRP))
                sp.sem_inc(s_turn, 1)
                wait(sp, s_hot, i * ring + (n * NG + (q + 1 - ring)))
                sp.dma_start(REC[:, q, :, 3 - width:3],
                             view[:, bass.ds(i * (ring * GRP) + q * GRP, GRP), :]).then_inc(recs_ready[q], 16)

            def load_records(n, recs, width):
                view = recs[0:P * T, :].rearrange("(p t) f -> p t f", p=P)

                def body(i):
                    for q in range(RING):
                        load_group(n, i, q, RING, n - 2, view, width, s_rec, s_gath)
                steps(sp, NI, body, peel=(isinstance(n, int) and n == 2))

            def load_records_attention(n, staging=False):
                view = rec_dst[0:P * T, :].rearrange("(p t) f -> p t f", p=P)

                def body(i):
                    for q in range(AR):
                        load_group(n, i, q, AR, n, view, 3, s_rec_a, s_gath_a)
                        if staging and q % 2:
                            stage_columns(1, (q // 2) % 2, i * 2 + q // RING, SC_A + SC_B)
                steps(sp, NIA, body, peel=(n == 0))

            store_table(0, tab0, 1)
            for s in range(2):
                sp.wait_ge(s_scat[s], (SCI + SC_A) * SCOL * 16)
            load_records_attention(0)
            sp.wait_ge(s_pos, ECH + 1)
            stage_steps(1, SC_A, SC_B)
            sp.wait_ge(s_xr, 1)
            load_w([(w_t[:, :], L1_gnn_W), (bias_b[:, :], row_of(L1_gnn_bias)),
                    (gamma_b[:, :], row_of(L1_gnn_gamma)), (beta_b[:, :], row_of(L1_gnn_beta))] +
                   [(att[h * HD:(h + 1) * HD, o + h:o + h + 1], a[h, :].rearrange("(n a) -> n a", a=1))
                    for o, a in ((0, L1_gnn_att_src), (H1, L1_gnn_att_dst)) for h in range(H1)])
            store_table(1, tab1, 1)
            load_records_attention(1, staging=True)
            rows1 = tab1.rearrange("(b p) w -> p b w", p=P)

            def own_rows(i):
                sp.wait_ge(s_hru, i + 1)
                sp.dma_start(T2[:, :, :], rows1[:, bass.ds(i * NPB, NPB), :]).then_inc(s_hr, 16)
                for k in range(SC_C // NPI):
                    for s in range(2):
                        stage_columns(1, s, i * (SC_C // NPI) + k, SC_A + SC_B + SC_L1)
            steps(sp, NPI, own_rows)
            sp.wait_ge(s_xr, 2)
            raws = [L2_gnn_W_edge[t, :, :] for t in range(NET)] + \
                   [m[g * D:(g + 1) * D, :] for m in (L2_gnn_W_ih, L2_gnn_W_hh) for g in range(3)]
            for k, m in enumerate(raws):
                load_w([(raw_w[:, 0:D], m)])
                sp.wait_ge(s_wp, 2 + k + 1)
            load_w([(b_gru[:, 3 * k + g:3 * k + g + 1], b[g * D:(g + 1) * D].rearrange("(n a) -> n a", a=1))
                    for k, b in enumerate((L2_gnn_b_ih, L2_gnn_b_hh)) for g in range(3)] +
                   [(wide_b[:, t * D:(t + 1) * D], row_of(L2_gnn_b_edge[t, :])) for t in range(NET)])
            store_table(2, tab2, NET)
            load_records(2, rec_dst, 3)
            store_table(3, tab2, NET)
            with sp.Fori(1, STEPS - 1) as st:
                load_records(st + 2, rec_dst, 3)
                store_table(st + 3, tab2, NET)
            load_records(STEPS + 1, rec_dst, 3)
            sp.wait_ge(s_xr, 3)
            load_w([(raw_w[:, b * D:(b + 1) * D], L3_gnn_weight[b, :, :]) for b in range(NBASE)] +
                   [(alpha_b[:, :], row_of(L3_gnn_alpha.rearrange("r b -> (r b)"))),
                    (wide_w[:, NREL * D:(NREL + 1) * D], L3_gnn_weight_self_loop),
                    (bias_b[:, :], row_of(L3_gnn_bias)), (gamma_b[:, :], row_of(L3_gnn_ln_gamma)),
                    (beta_b[:, :], row_of(L3_gnn_ln_beta))])
            store_table(6, tab3, NREL)
            for s in range(2):
                sp.wait_ge(s_scat[s], 2 * SCI * SCOL * 16)
            load_records(6, rec_src, 2)
            sp.wait_ge(s_on, 1)
            sp.dma_start(out[0:full_b * P, :].rearrange("(b p) f -> p b f", p=P), X[:, 0:full_b, :]).then_inc(s_out, 16)
            sp.dma_start(out[full_b * P:N, :], X[0:N - full_b * P, full_b, :]).then_inc(s_out, 16)
            sp.wait_ge(s_out, 32)

        @block.gpsimd
        def _(pool):
            ch = Chain(pool, s_cp)
            ch.done(pool.memset(ident[:, :], 0.0))
            ch.done(pool.memset(lower[:, :], 1.0))
            ch.done(pool.memset(maskc[:, :], 1.0))
            ch.done(pool.memset(ones[:, :], 1.0))
            ch.wait()
            ch.done(pool.affine_select(out=ident[:, :], in_=ident[:, :], compare_op=ALU.not_equal, fill=1.0,
                                       base=0, pattern=[[-1, P]], channel_multiplier=1))
            ch.done(pool.affine_select(out=lower[:, :], in_=lower[:, :], compare_op=ALU.is_gt, fill=0.0,
                                       base=0, pattern=[[1, P]], channel_multiplier=-1))
            ch.done(pool.affine_select(out=maskc[:, :], in_=maskc[:, :], compare_op=ALU.is_gt, fill=0.0,
                                       base=N - (NBLK - 1) * P, pattern=[[0, 1]], channel_multiplier=-1))
            ch.done(pool.iota(iotai[:, :], pattern=[[1, P]], base=0, channel_multiplier=0))
            ch.done(pool.iota(iota_ti, pattern=[[1, T]], base=0, channel_multiplier=0))
            ch.done(pool.iota(trash, pattern=[[1, C]], base=P * T, channel_multiplier=C))
            ch.wait()
            pool.sem_inc(s_const, 1)

            def scatter_columns(key, s, i, first=0):
                recs, stage, width = ((rec_dst, STGS, 4), (rec_src, STG2, 3))[key]
                pool.wait_ge(s_stage[s], (i + (key * SCI + first + 1)) * 16)
                pool.sem_inc(s_turn, 1)
                for c in range(SCOL):
                    pool.indirect_dma_start(recs, bass.IndirectOffsetOnAxis(stage[:, s, c, 0:1], 0),
                                            stage[:, s, c, 1:width], None).then_inc(s_scat[s], 16)

            def scatter_steps(key, first, count):
                def body(i):
                    for s in range(2):
                        scatter_columns(key, s, i, first)
                steps(pool, count, body)

            pool.wait_ge(s_empty, 8 * 16)
            scatter_steps(0, 0, SCI)
            scatter_steps(1, 0, SC_A)

            def gather_group(n, i, q, ring, base, table, word, dest, recs_ready, gathered):
                pool.wait_ge(recs_ready[q], (base * (NG // ring) + i + 1) * 16)
                pool.sem_inc(s_turn, 1)
                wait(pool, s_sum, i * ring + (n * NG + (q + 1 - ring)))
                pool.sem_inc(s_turn, 1)
                for j in range(GRP):
                    pool.indirect_dma_start(
                        dest[:, q * GRP + j, 0:table.shape[1]], None, table,
                        bass.IndirectOffsetOnAxis(REC[:, q, j, word:word + 1], 0)).then_inc(gathered[q], 16)

            def gather_attention(n, table, scattering=False):
                pool.wait_ge(s_tb_all, n + 1)
                pool.sem_inc(s_turn, 1)

                def body(i):
                    for q in range(AR):
                        gather_group(n, i, q, AR, n, table, 0, GA, s_rec_a, s_gath_a)
                        if scattering and q % 2:
                            scatter_columns(1, (q // 2) % 2, i * 2 + q // RING, SC_A + SC_B)
                steps(pool, NIA, body, peel=(n == 0))

            def gather(n, table):
                pool.wait_ge(s_tb_all, n + 1)
                pool.sem_inc(s_turn, 1)

                def body(i):
                    for q in range(RING):
                        gather_group(n, i, q, RING, n - 2, table, 1, G, s_rec, s_gath)
                steps(pool, NI, body)

            gather_attention(0, tab0)
            scatter_steps(1, SC_A, SC_B)
            gather_attention(1, tab1, scattering=True)
            scatter_steps(1, SC_A + SC_B + SC_L1, SC_C)
            with pool.Fori(0, STEPS) as st:
                gather(st + 2, tab2)
            gather(6, tab3)

        @block.tensor
        def _(pe):
            mm, tr = nc.tensor.matmul, nc.tensor.transpose
            pe.wait_ge(s_const, 1)
            for key in range(2):
                pe.wait_ge(s_cnt, key + 1)
                mm(PS[0][:, 0:NBLK], lower[:, :], CNT[:, :], start=True, stop=True)
                mm(PS[0][:, P:P + NBLK], ones[:, :], CNT[:, :], start=True, stop=True).then_inc(s_pre, 1)
                pe.wait_ge(s_end, key + 1)
                tr(PS[1][0:NBLK, 0:P], TOT[:, 1, :], ident[:, :]).then_inc(s_endt, 1)
                pe.wait_ge(s_sel, key + 1)
                for k in range(4):
                    wait(pe, s_blkc, key * 4 + k)
                    mm(PS[2][:, 0:MW], ones[0:NBLK, :], m_sel[0:NBLK, k * MW:(k + 1) * MW],
                       start=True, stop=True).then_inc(s_blk, 1)

            def attention_weights(n, heads, loaded):
                pe.wait_ge(s_w, loaded)
                tr(PS[3][:, 0:D], w_t[:, :], ident[:, :]).then_inc(s_wp, 1)
                pe.wait_ge(s_wv, 2 * n + 1)
                mm(PS[3][:, P:P + 2 * heads], w_t[:, :], att[:, 0:2 * heads], start=True, stop=True).then_inc(s_wa, 1)
                pe.wait_ge(s_wv, 2 * n + 2)

            def turn_block(turn, i, q):
                pe.wait_ge(s_xs, i * 2 + (turn * NBLK + q + 1))
                tr(PS[q][:, 0:D], XS[:, q, :], ident[:, :]).then_inc(s_t, 1)

            def table(n, turn, rhs, width):
                def body(i):
                    for q in range(2):
                        if turn is not None:
                            turn_block(turn, i, q)
                        pe.wait_ge(s_xt, i * 2 + (n * NBLK + (q + 1)))
                        wait(pe, s_ev, i * 2 + (n * NBLK + (q - 1)))
                        for k in range(-(-width // 512)):
                            w = min(512, width - 512 * k)
                            last = mm(PS[2 + 3 * q + k][:, 0:w], XT[:, q, :], rhs[:, 512 * k:512 * k + w],
                                      start=True, stop=True)
                        last.then_inc(s_mm, 1)
                steps(pe, TBI, body, peel=(isinstance(n, int) and n == 0))

            def attention(n, heads):
                def turn(i, q):
                    wait(pe, s_hot, i * AR + (n * NG + (q + 1)))
                    wait(pe, s_dts, i * AR + (n * NG + q))
                    for j in range(GRP):
                        last = tr(PS[4][:, j * P:(j + 1) * P], DOH[:, (q % RING) * GRP + j, :], ident[:, :])
                    last.then_inc(s_dt, 1)

                def scores(i, q):
                    wait(pe, s_neg, i * AR + (n * NG + (q + 1)))
                    wait(pe, s_red, i * AR + (n * NG + q))
                    for j in range(GRP):
                        o = PS[j][:, 0:heads * P] if heads > 1 else PS[0][:, j * P:(j + 1) * P]
                        if heads > 1:
                            mm(o, NEG[:, q % 2, j, :], identb[:, :].unsqueeze(1).to_broadcast([P, heads, P]),
                               start=True, stop=False)
                        else:
                            mm(o, NEG[:, q % 2, j, :], identb[:, :], start=True, stop=False)
                        for h in range(heads):
                            last = mm(o[:, h * P:(h + 1) * P], ESB[:, q % 2, j, h:h + 1].to_broadcast([P, P]),
                                      identb[:, :], start=False, stop=(h == heads - 1))
                    last.then_inc(s_v, 1)

                def by_edge(i, q):
                    wait(pe, s_m, i * AR + (n * NG + (q + 1)))
                    wait(pe, s_dts, i * AR + (n * NG + (q + 1)))
                    for j in range(GRP):
                        c = (q % 2) * 64 + j * 2 * heads
                        last = mm(PS[5][:, c:c + 2 * heads], DTS[:, q % 2, j * P:(j + 1) * P],
                                  EDM[:, q % 2, 0:2, j, 0:heads], start=True, stop=True)
                    last.then_inc(s_eb, 1)

                def sums(i, q):
                    wait(pe, s_msg, i * AR + (n * NG + (q + 1)))
                    wait(pe, s_add, i * AR + (n * NG + q))
                    for j in range(GRP):
                        c = (j % 2) * 256
                        last = mm(PS[6 + j // 2][:, c:c + D + heads], DOH[:, (q % RING) * GRP + j, :],
                                  GA[:, q * GRP + j, 0:D + heads], start=True, stop=True)
                    last.then_inc(s_sum, 1)

                def body(i, first=False, last=False):
                    for q in range(AR):
                        if not (last and q == AR - 1):
                            turn(*off(i, q, AR, 1))
                            scores(*off(i, q, AR, 1))
                        by_edge(i, q)
                        if not (first and q == 0):
                            sums(*off(i, q, AR, -1))

                turn(0, 0)
                scores(0, 0)
                body(0, first=True)
                with pe.Fori(1, NIA - 1) as i:
                    body(i)
                body(NIA - 1, last=True)
                sums(NIA - 1, AR - 1)

            def plain(n, turned):
                def body(i):
                    for q in range(RING):
                        pe.wait_ge(s_hot, i * RING + (n * NG + (q + 1)))
                        pe.wait_ge(s_gath[q], ((n - 2) * NI + i + 1) * (16 * GRP))
                        pe.wait_ge(s_add, i * RING + (n * NG + (q - 1)))
                        for j in range(GRP):
                            rows, hot = G[:, q * GRP + j, :], DOH[:, q * GRP + j, :]
                            if turned:
                                last = mm(PS[q % 2][:, j * P:(j + 1) * P], rows[:, 0:D], hot, start=True, stop=True)
                            else:
                                c = (j % 2) * 256
                                last = mm(PS[2 * (q % 2) + j // 2][:, c:c + D + 1], hot, rows[:, 0:D + 1],
                                          start=True, stop=True)
                        last.then_inc(s_sum, 1)
                steps(pe, NI, body)

            attention_weights(0, 1, W0)
            table(0, 0, w_ext, D + 2)
            attention(0, 1)
            attention_weights(1, H1, W1)
            table(1, 1, w_ext, D + 2 * H1)
            attention(1, H1)
            for k in range(NET + 6):
                pe.wait_ge(s_w, W1 + 16 * (k + 1))
                pe.wait_ge(s_wv, 4 + k)
                tr(PS[0][:, 0:D], raw_w[:, 0:D], ident[:, :]).then_inc(s_wp, 1)
            pe.wait_ge(s_wv, 4 + NET + 6 + 1)
            table(2, 2, wide_w, NET * D)
            pe.wait_ge(s_ht, NBLK)

            def gates(step, i, q):
                if not (isinstance(i, int) and i < 2):
                    pe.wait_ge(s_gt, step * GI + (i - 1))
                a, h = ACCT[:, bass.ds(i * GW, GW)], HT[:, bass.ds(i * GW, GW)]
                for g in range(2):
                    o = PS[2 * q][:, g * GW:(g + 1) * GW]
                    mm(o, w_ih[:, g * D:(g + 1) * D], a, start=True, stop=False)
                    mm(o, w_hh[:, g * D:(g + 1) * D], h, start=False, stop=True)
                mm(PS[2 * q + 1][:, 0:GW], w_ih[:, 2 * D:3 * D], a, start=True, stop=True)
                mm(PS[2 * q + 1][:, GW:2 * GW], w_hh[:, 2 * D:3 * D], h, start=True, stop=True).then_inc(s_g, 1)

            def next_rows(n, i):
                for u in range(2):
                    pe.wait_ge(s_xt, i * 2 + (n * NBLK + (u + 1)))
                    pe.wait_ge(s_ev, i * 2 + (n * NBLK + (u - 1)))
                    mm(PS[4 + u][:, :], XT[:, u, :], wide_w[:, 0:NET * D], start=True, stop=True).then_inc(s_mm, 1)

            def state_step(step, with_table):
                pe.wait_ge(s_add, (step + 3) * NG)
                pe.sem_inc(s_turn, 1)

                def body(i, q):
                    gates(step, i, q)
                    if with_table and not (isinstance(i, int) and i < 3):
                        next_rows(step + 3, i - 3)
                for i in range(3):
                    body(i, i % 2)
                with pe.Fori(0, GI // 2 - 1) as k:
                    for u in range(2):
                        body(k * 2 + (3 + u), (3 + u) % 2)
                if with_table:
                    for i in range(GI - 3, GI):
                        next_rows(step + 3, i)

            with pe.Fori(0, STEPS - 1) as st:
                plain(st + 2, True)
                state_step(st, True)
            plain(STEPS + 1, True)
            state_step(STEPS - 1, False)

            def out_of_state(i):
                for q in range(2):
                    turn_block(3, i, q)
            steps(pe, TBI, out_of_state)
            pe.wait_ge(s_wv, 4 + NET + 6 + 2)
            table(6, 4, wide_w, (NREL + 1) * D)
            plain(6, False)

        @block.scalar
        def _(act):
            def x_block(b):
                return X[:, bass.ds(b, 1), :].rearrange("p a f -> p (a f)")

            def h_block(b):
                return HT[:, bass.ds(b * P, P)]

            def turn_blocks(n, turn, state=False):
                def body(i):
                    for q in range(2):
                        wait(act, s_t, i * 2 + (turn * NBLK + (q - 1)))
                        act.sem_inc(s_turn, 1)
                        act.copy(XS[:, q, :], x_block(i * 2 + q)).then_inc(s_xs, 1)
                        act.wait_ge(s_t, i * 2 + (turn * NBLK + (q + 1)))
                        wait(act, s_mm, i * 2 + (n * NBLK + (q - 1)))
                        if state:
                            act.sem_inc(s_turn, 1)
                            act.copy(h_block(i * 2 + q), PS[q][:, 0:D]).then_inc(s_ht, 1)
                        act.copy(XT[:, q, :], PS[q][:, 0:D]).then_inc(s_xt, 1)
                steps(act, TBI, body, peel=(n == 0))

            def attention(n, heads):
                own = D // heads + 1

                def hot_rows(i, q):
                    act.wait_ge(s_rec_a[q], (i + (n * NIA + 1)) * 16)
                    act.sem_inc(s_turn, 1)
                    for j in range(GRP):
                        ch.done(act.activation(DIST[:, j * P:(j + 1) * P], iota[:, :], ACT.Square, scale=-1.0,
                                               bias=REC[:, q, j, 2:3].bitcast(F32)))
                    ch.wait()
                    wait(act, s_sum, i * AR + (n * NG + (q + 1 - RING)))
                    act.sem_inc(s_turn, 1)
                    act.activation(DOH[:, (q % RING) * GRP:(q % RING + 1) * GRP, :].rearrange("p a b -> p (a b)"), DIST, ACT.Relu,
                                   scale=-1.0, bias=ones[:, 0:1]).then_inc(s_hot, 1)
                    wait(act, s_v, i * AR + (n * NG + (q - 1)))
                    ch.done(act.activation(NEG[:, q % 2, :, :].rearrange("p a b -> p (a b)"), DIST, ACT.Copy,
                                           scale=-BIG))
                    act.wait_ge(s_gath_a[q], (i + (n * NIA + 1)) * (16 * GRP))
                    act.copy(ESB[:, q % 2, :, 0:heads], GA[:, q * GRP:(q + 1) * GRP, own - 1:D + heads:own]
                             ).then_inc(s_neg, 1)
                    ch.restart()

                def turned(i, q):
                    wait(act, s_dt, i * AR + (n * NG + (q + 1)))
                    wait(act, s_eb, i * AR + (n * NG + (q - 1)))
                    act.copy(DTS[:, q % 2, :], PS[4][:, :]).then_inc(s_dts, 1)

                def factors(i, q):
                    wait(act, s_m, i * AR + (n * NG + (q + 1)))
                    wait(act, s_add, i * AR + (n * NG + (q - 1)))
                    act.activation(FEX[:, q % 2, :, 0:heads], FAC[:, q % 2, :, 0:heads], ACT.Exp).then_inc(s_fe, 1)

                def weights(i, q):
                    wait(act, s_se, i * AR + (n * NG + (q + 1)))
                    act.activation(GA[:, q * GRP:(q + 1) * GRP, own - 1:D + heads:own], SE[:, :, 0:heads],
                                   ACT.Exp).then_inc(s_pe, 1)

                def body(i, first=False, last=False):
                    for q in range(AR):
                        if not (first and q == 0):
                            weights(*off(i, q, AR, -1))
                        if not (last and q >= AR - 2):
                            hot_rows(*off(i, q, AR, 2))
                        if not (last and q == AR - 1):
                            turned(*off(i, q, AR, 1))
                        factors(i, q)
                hot_rows(0, 0)
                turned(0, 0)
                hot_rows(0, 1)
                body(0, first=True)
                with act.Fori(1, NIA - 1) as i:
                    body(i)
                body(NIA - 1, last=True)
                weights(NIA - 1, AR - 1)

            t1d, t2d = T1[:, :, :], T2[:, :, 0:D]

            def node_phase(base, requests):
                def body(i):
                    for k, (func, o, a) in enumerate(requests):
                        act.wait_ge(s_np, i * len(requests) + (base + k + 1))
                        act.activation(o, a, func).then_inc(s_na, 1)
                steps(act, NPI, body)

            ch = Chain(act, s_ca)
            act.wait_ge(s_xz, 1)
            act.dma_start(X[:, 0:full_b, :], x[0:full_b * P, :].rearrange("(b p) f -> p b f", p=P)).then_inc(s_x, 16)
            act.dma_start(X[0:N - full_b * P, full_b, :], x[full_b * P:N, :]).then_inc(s_x, 16)
            act.wait_ge(s_x, 32)
            turn_blocks(0, 0)
            attention(0, 1)
            square, root = (ACT.Square, t2d, t1d), (ACT.Sqrt, SM[:, 1, :], SM[:, 1, :])
            node_phase(ASK[0], [(ACT.Exp, t2d, t2d), square, root])
            act.wait_ge(s_xr, 1)
            turn_blocks(1, 1)
            attention(1, H1)
            node_phase(ASK[1], [(ACT.Exp, SD[:, :, :], SD[:, :, :]), square, root, (ACT.Gelu, t2d, t1d),
                                  square, root])
            act.wait_ge(s_xr, 2)

            for s in range(2):
                act.wait_ge(s_scat[s], 2 * SCI * SCOL * 16)
            turn_blocks(2, 2, state=True)

            def next_blocks(step, i):
                for u in range(2):
                    act.wait_ge(s_gh, step * GI + (i + 1))
                    act.sem_inc(s_turn, 1)
                    act.wait_ge(s_mm, i * 2 + ((step + 3) * NBLK + (u - 1)))
                    act.sem_inc(s_turn, 1)
                    act.copy(XT[:, u, :], HT[:, bass.ds(i * GW + u * P, P)]).then_inc(s_xt, 1)

            def state_step(step, with_table):
                def body(i, q):
                    act.wait_ge(s_g, step * GI + (i + 1))
                    act.sem_inc(s_turn, 1)
                    if not (isinstance(i, int) and i < 2):
                        act.wait_ge(s_gh, step * GI + (i - 1))
                    for g in range(2):
                        last = act.activation(STG[:, q, 2 * GW + g * GW:2 * GW + (g + 1) * GW],
                                              PS[2 * q][:, g * GW:(g + 1) * GW], ACT.Sigmoid, bias=b_rz[:, g:g + 1])
                    last.then_inc(s_gr, 1)
                    act.wait_ge(s_gt, step * GI + (i + 1))
                    act.activation(GATE_T[:, q, GW:2 * GW], GATE_T[:, q, 0:GW], ACT.Tanh,
                                   bias=b_gru[:, 2:3]).then_inc(s_gn, 1)
                    if with_table and not (isinstance(i, int) and i < 2):
                        next_blocks(step, i - 2)
                for i in range(3):
                    body(i, i % 2)
                with act.Fori(0, GI // 2 - 1) as k:
                    for u in range(2):
                        body(k * 2 + (3 + u), (3 + u) % 2)
                if with_table:
                    next_blocks(step, GI - 2)
                    next_blocks(step, GI - 1)

            with act.Fori(0, STEPS - 1) as st:
                state_step(st, True)
            state_step(STEPS - 1, False)
            act.wait_ge(s_gh, STEPS * GI)

            def out_of_state(i):
                for q in range(2):
                    act.wait_ge(s_t, i * 2 + (3 * NBLK + q - 1))
                    act.sem_inc(s_turn, 1)
                    wait(act, s_xa, i * 2 + (q - 1))
                    act.sem_inc(s_turn, 1)
                    act.copy(XS[:, q, :], h_block(i * 2 + q)).then_inc(s_xs, 1)
            steps(act, TBI, out_of_state, peel=True)
            node_phase(ASK[2], [square, root])
            act.wait_ge(s_xr, 3)
            turn_blocks(6, 4)
            node_phase(ASK[3], [square, root, square, root])

        @block.vector
        def _(dve):
            v = nc.vector
            ch = Chain(dve, s_cv)
            ch.done(v.memset(accf[:, 0:3 * C].bitcast(I32), -1))
            ch.done(v.memset(HT[:, 4 * C:8 * C], 0.0))
            ch.wait()
            dve.sem_inc(s_key, 1)
            ch.done(v.memset(zeros, 0.0))
            ch.done(v.memset(emp[:, :, 0:1], DUMMY))
            ch.done(v.memset(emp[:, :, 1:2], DUMMY * NET))
            ch.done(v.memset(emp[:, :, 2:3].bitcast(F32), -1.0))
            ch.wait()
            dve.sem_inc(s_emp0, 1)
            dve.wait_ge(s_const, 1)
            ch.done(v.tensor_copy(iota[:, :], iotai[:, :]))
            ch.done(v.tensor_copy(identb[:, :], ident[:, :]))
            ch.done(v.tensor_copy(iota_t, iota_ti))
            dve.wait_ge(s_empty, 4 * 16)
            ch.done(v.memset(emp[:, :, 1:2], DUMMY * NREL))
            ch.wait()
            dve.sem_inc(s_emp0, 1)

            dve.wait_ge(s_ints, 8 * 16)
            top, et = tmp_b, tmp_a
            ch.done(v.tensor_reduce(top, attr, AX.X, ALU.max))
            ch.wait()
            ch.done(v.tensor_tensor(et, attr[:, :, 0], top, ALU.is_lt))
            ch.done(v.tensor_tensor(eq, attr[:, :, 1], top, ALU.is_lt))
            ch.done(v.tensor_tensor(pre, attr[:, :, 2], top, ALU.is_lt))
            ch.wait()
            ch.done(v.tensor_tensor(eq, eq, et, ALU.mult))
            ch.wait()
            ch.done(v.tensor_tensor(pre, pre, eq, ALU.mult))
            ch.done(v.tensor_tensor(et, et, eq, ALU.add))
            ch.wait()
            ch.done(v.tensor_tensor(et, et, pre, ALU.add))
            ch.wait()
            ch.done(v.tensor_copy(rec1[:, :, 1], src_i))
            ch.done(v.scalar_tensor_tensor(rec1[:, :, 2], src_i, float(NET), et, ALU.mult, ALU.add))
            ch.done(v.scalar_tensor_tensor(rec2[:, :, 1], dst_i, float(NREL), typ_i, ALU.mult, ALU.add))
            ch.wait()
            tmp_i = tmp_b.bitcast(I32)
            shift = P.bit_length() - 1
            tile_blk = xf[:, 2 * T + 2 * C:2 * T + 2 * C + T]

            def rank(key, key_i, recs, node_word):
                ch.done(v.tensor_scalar(tmp_i, key_i, P - 1, None, ALU.bitwise_and))
                ch.wait()
                ch.done(v.tensor_copy(recs[:, :, node_word].bitcast(F32), tmp_i))
                ch.wait()
                ch.done(v.tensor_scalar(tmp_i, key_i, shift, None, ALU.arith_shift_right))
                ch.wait()
                ch.done(v.tensor_copy(bkt, tmp_i))
                ch.restart()
                with dve.Fori(0, NBLK // 2) as b:
                    for u in range(2):
                        one = bass.ds(b * 2 + u, 1)
                        ch.done(v.tensor_scalar((eq, pre)[u], bkt, iota[:, one], 0.0, ALU.is_equal, ALU.add,
                                                accum_out=CNT[:, one]))
                    ch.restart()
                dve.sem_inc(s_cnt, 1)
                dve.wait_ge(s_pre, key + 1)
                ch.done(v.tensor_scalar(TIL[:, :], PS[0][:, P:P + NBLK], float(P - 1), None, ALU.add))
                ch.wait()
                ch.done(v.tensor_scalar(TIL[:, :], TIL[:, :], shift, None, ALU.arith_shift_right))
                ch.wait()
                ch.done(v.tensor_copy(TOT[:, 0, :], TIL[:, :]))
                ch.wait()
                ch.done(v.tensor_tensor_scan(TOT[:, 1, :], TOT[:, 0, :], zeros[:, 0:NBLK], 0.0, ALU.add, ALU.add))
                ch.wait()
                dve.sem_inc(s_end, 1)
                ch.done(v.tensor_tensor(TOT[:, 2, :], TOT[:, 1, :], TOT[:, 0, :], ALU.subtract))
                ch.wait()
                ch.done(v.scalar_tensor_tensor(BAS[:, :], TOT[:, 2, :], float(P), PS[0][:, 0:NBLK],
                                               ALU.mult, ALU.add))
                dve.wait_ge(s_endt, key + 1)
                ch.done(v.tensor_copy(ENDC[0:NBLK, :], PS[1][0:NBLK, 0:1]))
                ch.wait()
                ch.done(v.tensor_scalar(m_sel[0:NBLK, :], iota_t[0:NBLK, :], ENDC[0:NBLK, :], None, ALU.is_ge))
                ch.wait()
                dve.sem_inc(s_sel, 1)
                for k in range(4):
                    part = slice(k * MW, (k + 1) * MW)
                    dve.wait_ge(s_blk, key * 4 + k + 1)
                    ch.done(v.tensor_scalar((blk_d, blk_s)[key][:, part],
                                            PS[2][32 * key:32 * key + 1, 0:MW], float(NBLK - 1),
                                            None, ALU.min))
                    ch.done(v.tensor_scalar(tile_blk[:, part], PS[2][:, 0:MW], float(NBLK - 1), None, ALU.min))
                    ch.wait()
                    dve.sem_inc(s_blkc, 1)
                if key == 0:
                    ch.done(v.tensor_tensor(LIM[:, 1:T], tile_blk[:, 1:T], tile_blk[:, 0:T - 1], ALU.is_equal))
                    ch.done(v.memset(LIM[:, 0:1], 0.0))
                    ch.wait()
                    ch.done(v.tensor_scalar(LIM[:, :], LIM[:, :], 2 * BIG, -BIG, ALU.mult, ALU.add))
                    ch.wait()
                width = (CW, C)[key]
                for k in range(C // width):
                    cols = slice(k * width, (k + 1) * width)
                    if key == 0:
                        same = [eq[:, u * CW:(u + 1) * CW] for u in range(2)]
                        seen = [pre[:, u * CW:(u + 1) * CW] for u in range(2)]
                        pos = pre[:, 2 * CW:3 * CW]
                    else:
                        same, seen, pos = (tmp_a, tmp_b), (accf[:, 1 * C:2 * C], accf[:, 2 * C:3 * C]), pre
                    ch.done(v.memset(pos, 1.0))
                    ch.restart()
                    with dve.Fori(0, NBLK // 2) as b:
                        one = [bass.ds(b * 2 + u, 1) for u in range(2)]
                        is_same = [ch.done(v.tensor_scalar(same[u], bkt[:, cols], iota[:, one[u]], None,
                                                           ALU.is_equal)) for u in range(2)]
                        counted = []
                        for u in range(2):
                            ch.wait(is_same[u])
                            counted.append(ch.done(v.tensor_tensor_scan(seen[u], same[u], zeros[:, 0:width],
                                                                        BAS[:, one[u]], ALU.add, ALU.add)))
                        for u in range(2):
                            ch.wait(counted[u])
                            if u:
                                ch.wait(placed)
                            placed = ch.done(v.copy_predicated(pos, same[u].bitcast(U32), seen[u]))
                            ch.done(v.tensor_copy(BAS[:, one[u]], seen[u][:, width - 1:width]))
                        ch.restart()
                    pos_i, low, high = same[0].bitcast(I32), seen[0].bitcast(I32), pos.bitcast(I32)
                    ch.done(v.tensor_scalar(pos_i, pos, -1.0, None, ALU.add))
                    ch.wait()
                    ch.done(v.tensor_scalar(low, pos_i, P - 1, None, ALU.bitwise_and))
                    ch.done(v.tensor_scalar(high, pos_i, shift, None, ALU.arith_shift_right))
                    ch.wait()
                    ch.done(v.scalar_tensor_tensor(recs[:, cols, 0], low, float(T), high, ALU.mult, ALU.add))
                    ch.done(v.tensor_scalar(same[1], bkt[:, cols], 0.0, None, ALU.is_lt))
                    ch.wait()
                    ch.done(v.copy_predicated(recs[:, cols, 0], same[1].bitcast(U32), trash[:, cols]))
                    ch.wait()
                    dve.sem_inc(s_pos, 1)

            dve.wait_ge(s_empty, 8 * 16)
            rank(0, dst_i, rec1, 3)
            rank(1, src_i, rec2, 2)
            ch.done(v.memset(X[:, NBLK - 1, :], 0.0))
            ch.wait()
            dve.sem_inc(s_xz, 1)

            def attention_weights(n, heads):
                dve.wait_ge(s_wp, n + 1)
                by_head = w_ext[:, 0:D + heads].rearrange("p (h e) -> p h e", h=heads)
                ch.done(v.tensor_copy(by_head[:, :, 0:D // heads], w_t[:, :].rearrange("p (h d) -> p h d", h=heads)))
                ch.wait()
                ch.done(v.tensor_copy(w_t[:, :], PS[3][:, 0:D]))
                ch.wait()
                dve.sem_inc(s_wv, 1)
                dve.wait_ge(s_wa, n + 1)
                ch.done(v.tensor_copy(by_head[:, :, D // heads], PS[3][:, P:P + heads]))
                ch.done(v.tensor_copy(w_ext[:, D + heads:D + 2 * heads], PS[3][:, P + heads:P + 2 * heads]))
                ch.wait()
                dve.sem_inc(s_wv, 1)

            def x_block(b):
                return X[:, bass.ds(b, 1), :].rearrange("p a f -> p (a f)")

            def evacuate(n, width, heads=0, bias=None, self_loop=False):
                def body(i):
                    for q in range(2):
                        b = i * 2 + q
                        dve.wait_ge(s_mm, i * 2 + (n * NBLK + (q + 1)))
                        wait(dve, s_tab[q], (n * TBI + i) * 16)
                        for k in range(-(-width // 512)):
                            w = min(512, width - 512 * k)
                            o, p = STG[:, q, 512 * k:512 * k + w], PS[2 + 3 * q + k][:, 0:w]
                            last = v.tensor_copy(o, p) if bias is None else v.tensor_tensor(o, p, bias, ALU.add)
                        if heads:
                            ch.done(last)
                            last = v.tensor_copy(ED[:, bass.ds(b, 1), 0:heads].rearrange("p a f -> p (a f)"),
                                                 PS[2 + 3 * q][:, D + heads:D + 2 * heads])
                        if self_loop:
                            ch.done(last)
                            last = v.tensor_tensor(x_block(b), x_block(b), PS[4 + 3 * q][:, 0:D], ALU.add)
                        last.then_inc(s_ev, 1)
                    ch.restart()
                ch.restart()
                steps(dve, TBI, body, peel=(isinstance(n, int) and n == 0))

            def clear_sums():
                ch.done(v.memset(accf, 0.0))
                ch.restart()

            def hot_rows(n, i, q):
                dve.wait_ge(s_rec[q], (i + ((n - 2) * NI + 1)) * 16)
                v.tensor_tensor(DOH[:, q * GRP:(q + 1) * GRP, :],
                                iota[:, :].unsqueeze(1).to_broadcast([P, GRP, P]),
                                bcast(REC[:, q, :, 2].bitcast(F32), P), ALU.is_equal).then_inc(s_hot, 1)

            regs = [[dve.alloc_register(f"blk{k}_{j}") for j in range(GRP)] for k in range(2)]

            def blocks(tile_blocks, g, regs=regs[0]):
                dve.load(regs, tile_blocks[0:1, bass.ds(g * GRP, GRP)])
                return [dve.snap(r, min_val=0, max_val=NBLK - 1) for r in regs]

            def attention(n, heads):
                hs = slice(0, heads)
                own = D // heads + 1
                add_steps = 2 if heads > 1 else 1

                def scores_by_edge(q):
                    return (PS[5][:, (q % 2) * 64:(q % 2) * 64 + GRP * 2 * heads].rearrange(
                                "p (j k h) -> p j k h", j=GRP, k=2),
                            GA[:, q * GRP:(q + 1) * GRP, 0:D + heads].rearrange("p j (h e) -> p j h e", h=heads))

                def weigh(g, q):
                    _, rows = scores_by_edge(q)
                    dve.wait_ge(s_pe, g + (n * NG + 1))
                    v.tensor_tensor(rows[:, :, :, 0:own - 1], rows[:, :, :, 0:own - 1],
                                    rows[:, :, :, own - 1:own].to_broadcast([P, GRP, heads, own - 1]),
                                    ALU.mult).then_inc(s_msg, 1)

                def no_copies(part):
                    pass

                def shifted(g, i, q, copy_between=no_copies):
                    eb, rows = scores_by_edge(q)
                    dve.wait_ge(s_eb, g + (n * NG + 1))
                    dve.wait_ge(s_gath_a[q], (i + (n * NIA + 1)) * (16 * GRP))
                    last = ch.done(v.tensor_tensor(SE[:, :, hs], rows[:, :, :, own - 1], eb[:, :, 0, :], ALU.add))
                    copy_between(0)
                    ch.wait(last)
                    last = ch.done(v.scalar_tensor_tensor(SE2[:, :, hs], SE[:, :, hs], SLOPE, SE[:, :, hs],
                                                          ALU.mult, ALU.max))
                    copy_between(1)
                    ch.wait(last)
                    v.tensor_tensor(SE[:, :, hs], SE2[:, :, hs], eb[:, :, 1, :], ALU.subtract).then_inc(s_se, 1)

                def adder(g, q, regs):
                    blk = blocks(blk_d, g, regs)
                    dve.wait_ge(s_sum, g + (n * NG + 1))
                    dve.wait_ge(s_fe, g + (n * NG + 1))
                    wait(dve, s_add, g + n * NG)
                    added = []

                    def add_sums(count):
                        for _ in range(count):
                            j, k = divmod(len(added), add_steps)
                            if added:
                                ch.wait(added[-1])
                            a = ACC[:, bass.ds(blk[j], 1), 0:D + heads].rearrange("p a f -> p (a f)")
                            c = (j % 2) * 256
                            tile_sums = PS[6 + j // 2][:, c:c + D + heads]
                            if heads == 1:
                                last = v.scalar_tensor_tensor(a, a, FEX[:, q % 2, j, 0:1], tile_sums,
                                                              ALU.mult, ALU.add)
                            elif k == 0:
                                by_head = a.rearrange("p (h e) -> p h e", h=heads)
                                last = v.tensor_tensor(by_head, by_head, bcast(FEX[:, q % 2, j, 0:heads], own),
                                                       ALU.mult)
                            else:
                                last = v.tensor_tensor(a, a, tile_sums, ALU.add)
                            if len(added) < GRP * add_steps - 1:
                                added.append(ch.done(last))
                            else:
                                last.then_inc(s_add, 1)
                                added.append(None)
                    return add_sums

                share = [1] * 8 if heads > 1 else [0, 1, 0, 1, 0, 1, 1, 0]

                def step(i, q, lag1=True, lag2=True):
                    g = i * AR + q
                    i1, q1 = off(i, q, AR, -1)
                    dve.wait_ge(s_v, g + (n * NG + 1))
                    if heads == 1:
                        v.tensor_reduce(TMAX[:, :, 0], PS[0][:, :].rearrange("p (j e) -> p j e", j=GRP), AX.X,
                                        ALU.max).then_inc(s_red, 1)
                    else:
                        for j in range(GRP):
                            last = v.tensor_reduce(TMAX[:, j, :], PS[j][:, :].rearrange("p (h e) -> p h e", h=heads),
                                                   AX.X, ALU.max)
                            if j < GRP - 1:
                                ch.done(last)
                        last.then_inc(s_red, 1)
                    blk = blocks(blk_d, g, regs[0])
                    ed = EDM[:, q % 2, 0, :, hs]
                    if lag1:
                        wait(dve, s_eb, g + (n * NG - 1))

                    def copy_between(part):
                        for j in (range(2), range(2, GRP))[part]:
                            ch.done(v.tensor_copy(ed[:, j, :],
                                                  ED[:, bass.ds(blk[j], 1), hs].rearrange("p a h -> p (a h)")))
                        if part:
                            ch.done(v.tensor_copy(NEW[:, 0, hs], NEW[:, GRP, hs]))
                    if lag1:
                        shifted(g - 1, i1, q1, copy_between)
                    else:
                        copy_between(0)
                        copy_between(1)
                    copied = ch.n
                    if lag2:
                        _, q2 = off(i, q, AR, -2)
                        add_step = adder(g - 2, q2, regs[1])

                    def add_sums(count):
                        if lag2:
                            add_step(count)
                    dve.wait_ge(s_red, g + (n * NG + 1))
                    ch.wait(copied)
                    for j in range(GRP):
                        last = ch.done(v.scalar_tensor_tensor(NEW[:, j + 1, hs], NEW[:, j, hs],
                                                              LIM[:, bass.ds(g * GRP + j, 1)], TMAX[:, j, hs],
                                                              ALU.min, ALU.max))
                        add_sums(share[j])
                        if j == 2 and lag1:
                            weigh(g - 1, q1)
                        ch.wait(last)
                        if heads > 1:
                            ch.done(v.tensor_copy(ME[:, bass.ds(blk[j], 1), hs].rearrange("p a h -> p (a h)"),
                                                  NEW[:, j + 1, hs]))
                    last = ch.done(v.tensor_tensor(NEW[:, GRP + 1:2 * GRP + 1, hs], NEW[:, 0:GRP, hs],
                                                   bcast(LIM[:, bass.ds(g * GRP, GRP)], heads), ALU.min))
                    add_sums(share[4])
                    ch.wait(last)
                    last = ch.done(v.tensor_tensor(NO[:, :, :, hs],
                                                   NEW[:, 1:2 * GRP + 1, hs].rearrange("p (k j) h -> p k j h", k=2),
                                                   ed.unsqueeze(1).to_broadcast([P, 2, GRP, heads]), ALU.add))
                    add_sums(share[5])
                    ch.wait(last)
                    last = ch.done(v.scalar_tensor_tensor(EDM[:, q % 2, 1:3, :, hs].rearrange("p k j h -> p (k j) h"),
                                                          NO[:, :, :, hs].rearrange("p k j h -> p (k j) h"), SLOPE,
                                                          NO[:, :, :, hs].rearrange("p k j h -> p (k j) h"),
                                                          ALU.mult, ALU.max))
                    add_sums(share[6])
                    ch.wait(last)
                    v.tensor_tensor(FAC[:, q % 2, :, hs], EDM[:, q % 2, 2, :, hs], EDM[:, q % 2, 1, :, hs],
                                    ALU.subtract).then_inc(s_m, 1)
                    add_sums(share[7])

                def body(i, first=False):
                    for q in range(AR):
                        step(i, q, lag1=not (first and q == 0), lag2=not (first and q < 2))
                    ch.restart()

                ch.done(v.memset(NEW[:, GRP, :], -BIG))
                ch.done(v.memset(ME[:, :, :], -BIG))
                clear_sums()
                body(0, first=True)
                with dve.Fori(1, NIA) as i:
                    body(i)
                adder(NG - 2, AR - 2, regs[1])(GRP * add_steps)
                ch.wait()
                shifted(NG - 1, NIA - 1, AR - 1)
                weigh(NG - 1, AR - 1)
                adder(NG - 1, AR - 1, regs[0])(GRP * add_steps)
                ch.restart()
                dve.wait_ge(s_add, (n + 1) * NG)

            def plain(n, turned, tile_blocks):
                def add(i, q):
                    g = i * RING + q
                    blk = blocks(tile_blocks, g)
                    dve.wait_ge(s_sum, g + (n * NG + 1))
                    dve.wait_ge(s_add, g + n * NG)
                    for j in range(GRP):
                        if turned:
                            a = ACCT[:, bass.ds(blk[j] * P, P)]
                            s = PS[q % 2][:, j * P:(j + 1) * P]
                        else:
                            a = ACC[:, bass.ds(blk[j], 1), 0:D + 1].rearrange("p a f -> p (a f)")
                            s = PS[2 * (q % 2) + j // 2][:, (j % 2) * 256:(j % 2) * 256 + D + 1]
                        last = v.tensor_tensor(a, a, s, ALU.add)
                        if j < GRP - 1:
                            ch.done(last)
                            ch.wait()
                    last.then_inc(s_add, 1)

                def body(i, first=False):
                    for q in range(RING):
                        hot_rows(n, i, q)
                        if not (first and q == 0):
                            add(*off(i, q, RING, -1))
                    ch.restart()
                clear_sums()
                body(0, first=True)
                with dve.Fori(1, NI) as i:
                    body(i)
                add(NI - 1, RING - 1)
                ch.restart()
                dve.wait_ge(s_add, (n + 1) * NG)
                dve.sem_inc(s_turn, 1)

            sm = [SM[:, k, :] for k in range(3)]
            t1d, t2d = T1[:, :, :], T2[:, :, 0:D]

            def rows(tile):
                return tile[:, :].unsqueeze(1).to_broadcast([P, NPB, D])

            def tt(o, a, b, op):
                ch.done(v.tensor_tensor(o, a, b, op))
                ch.wait()

            def ts(o, a, s1, s2, op0, op1=ALU.bypass):
                if s2 is None:
                    ch.done(v.tensor_scalar(o, a, s1, None, op0))
                else:
                    ch.done(v.tensor_scalar(o, a, s1, s2, op0, op1))
                ch.wait()

            def stt(o, a, s, b, op0, op1):
                ch.done(v.scalar_tensor_tensor(o, a, s, b, op0, op1))
                ch.wait()

            def node_phase(base, per, body):
                def step(i):
                    asked = [0]

                    def ask():
                        asked[0] += 1
                        ch.wait()
                        dve.sem_inc(s_np, 1)
                        dve.wait_ge(s_na, i * per + (base + asked[0]))
                    body(i, ask)
                    assert asked[0] == per
                    ch.restart()
                ch.restart()
                steps(dve, NPI, step)

            def normalize(dest, ask):
                ch.done(v.tensor_reduce(sm[0], t1d, AX.X, ALU.add))
                ch.wait()
                ts(sm[0], sm[0], 1.0 / D, None, ALU.mult)
                tt(t1d, t1d, bcast(sm[0], D), ALU.subtract)
                ask()
                ch.done(v.tensor_reduce(sm[1], t2d, AX.X, ALU.add))
                ch.wait()
                ts(sm[1], sm[1], 1.0 / D, EPS, ALU.mult, ALU.add)
                ask()
                ch.done(v.reciprocal(sm[1], sm[1]))
                ch.wait()
                tt(dest, t1d, bcast(sm[1], D), ALU.mult)

            def new_x_complete():
                ch.done(v.tensor_scalar(X[:, NBLK - 1, :], X[:, NBLK - 1, :], maskc[:, :], None, ALU.mult))
                ch.wait()
                dve.sem_inc(s_xr, 1)

            dve.wait_ge(s_x, 32)
            attention_weights(0, 1)
            evacuate(0, D + 1, heads=1)
            attention(0, 1)

            def nodes0(i, ask):
                bs = bass.ds(i * NPB, NPB)
                ts(sm[2], ACC[:, bs, D], 1e-15, None, ALU.max)
                ch.done(v.reciprocal(sm[2], sm[2]))
                ch.wait()
                tt(t1d, ACC[:, bs, 0:D], bcast(sm[2], D), ALU.mult)
                tt(t1d, t1d, rows(bias_b), ALU.add)
                ts(t2d, t1d, 0.0, None, ALU.min)
                ask()
                stt(t1d, t1d, 0.0, t2d, ALU.max, ALU.add)
                stt(t1d, t1d, -1.0, X[:, bs, :], ALU.add, ALU.add)
                normalize(X[:, bs, :], ask)
            node_phase(ASK[0], 3, nodes0)
            ch.done(v.memset(att[:, :], 0.0))
            new_x_complete()

            attention_weights(1, H1)
            evacuate(1, D + H1, heads=H1)
            attention(1, H1)

            def nodes1(i, ask):
                bs = bass.ds(i * NPB, NPB)
                dve.sem_inc(s_hru, 1)
                dve.wait_ge(s_hr, (i + 1) * 16)

                def heads_of(ap):
                    return ap.rearrange("p b (h d) -> p b h d", h=H1)

                acc_h, own_h = heads_of(ACC[:, bs, :]), heads_of(T2[:, :, :])

                def per_row(ap):
                    return ap.rearrange("p (b h) -> p b h", h=H1).unsqueeze(3).to_broadcast([P, NPB, H1, HD])

                def small(ap):
                    return ap.rearrange("p (b h) -> p b h", h=H1)
                tt(small(SA[:, 0, :]), ME[:, bs, :], ED[:, bs, :], ALU.add)
                tt(small(SA[:, 2, :]), own_h[:, :, :, HD], ED[:, bs, :], ALU.add)
                tt(SA[:, 1, :], SA[:, 0, :], SA[:, 2, :], ALU.max)
                stt(SC[:, :, :], SA[:, :, :], SLOPE, SA[:, :, :], ALU.mult, ALU.max)
                tt(SD[:, 0, :], SC[:, 0, :], SC[:, 1, :], ALU.subtract)
                tt(SD[:, 1, :], SC[:, 2, :], SC[:, 1, :], ALU.subtract)
                ask()
                tt(heads_of(t1d), acc_h[:, :, :, 0:HD], per_row(SD[:, 0, :]), ALU.mult)
                tt(own_h[:, :, :, 0:HD], own_h[:, :, :, 0:HD], per_row(SD[:, 1, :]), ALU.mult)
                tt(heads_of(t1d), heads_of(t1d), own_h[:, :, :, 0:HD], ALU.add)
                tt(small(SA[:, 0, :]), acc_h[:, :, :, HD], small(SD[:, 0, :]), ALU.mult)
                stt(SA[:, 0, :], SA[:, 0, :], 1e-16, SD[:, 1, :], ALU.add, ALU.add)
                ch.done(v.reciprocal(SA[:, 1, :], SA[:, 0, :]))
                ch.wait()
                tt(heads_of(t1d), heads_of(t1d), per_row(SA[:, 1, :]), ALU.mult)
                tt(t1d, t1d, rows(bias_b), ALU.add)
                normalize(t1d, ask)
                tt(t1d, t1d, rows(gamma_b), ALU.mult)
                tt(t1d, t1d, rows(beta_b), ALU.add)
                ask()
                tt(t1d, t2d, X[:, bs, :], ALU.add)
                normalize(X[:, bs, :], ask)
            node_phase(ASK[1], 6, nodes1)
            new_x_complete()

            for k in range(NET + 6):
                dve.wait_ge(s_wp, 2 + k + 1)
                g = k - NET
                o = wide_w[:, k * D:(k + 1) * D] if k < NET else (w_ih, w_hh)[g // 3][:, (g % 3) * D:(g % 3 + 1) * D]
                ch.done(v.tensor_copy(o, PS[0][:, 0:D]))
                ch.wait()
                dve.sem_inc(s_wv, 1)
            dve.wait_ge(s_w, W2)
            tt(b_rz[:, :], b_gru[:, 0:2], b_gru[:, 3:5], ALU.add)
            dve.sem_inc(s_wv, 1)
            evacuate(2, NET * D, bias=wide_b[:, :])
            dve.wait_ge(s_ht, NBLK)
            ch.restart()

            def next_rows(n, i, u):
                dve.wait_ge(s_mm, i * 2 + (n * NBLK + (u + 1)))
                dve.sem_inc(s_turn, 1)
                dve.wait_ge(s_tab[u], (n * TBI + i) * 16)
                v.tensor_tensor(STG[:, u, 0:NET * D], PS[4 + u][:, :], wide_b[:, :], ALU.add).then_inc(s_ev, 1)

            def state_step(step, with_table):
                def body(i, q):
                    rows_too = with_table and not (isinstance(i, int) and i < 3)
                    h = HT[:, bass.ds(i * GW, GW)]
                    r, z = STG[:, q, 2 * GW:3 * GW], STG[:, q, 3 * GW:4 * GW]
                    t, n = GATE_T[:, q, 0:GW], GATE_T[:, q, GW:2 * GW]
                    dve.wait_ge(s_gr, step * GI + (i + 1))
                    ch.done(v.scalar_tensor_tensor(t, PS[2 * q + 1][:, GW:2 * GW], b_gru[:, 5:6], r, ALU.add, ALU.mult))
                    ch.wait()
                    v.tensor_tensor(t, t, PS[2 * q + 1][:, 0:GW], ALU.add).then_inc(s_gt, 1)
                    if rows_too:
                        next_rows(step + 3, i - 3, 0)
                    dve.wait_ge(s_gn, step * GI + (i + 1))
                    dve.sem_inc(s_turn, 1)
                    last = ch.done(v.tensor_tensor(h, h, n, ALU.subtract))
                    if rows_too:
                        next_rows(step + 3, i - 3, 1)
                    ch.wait(last)
                    ch.done(v.tensor_tensor(h, h, z, ALU.mult))
                    ch.wait()
                    v.tensor_tensor(h, h, n, ALU.add).then_inc(s_gh, 1)
                for i in range(3):
                    body(i, i % 2)
                ch.restart()
                with dve.Fori(0, GI // 2 - 1) as k:
                    for u in range(2):
                        body(k * 2 + (3 + u), (3 + u) % 2)
                    ch.restart()
                if with_table:
                    for i in range(GI - 3, GI):
                        for u in range(2):
                            next_rows(step + 3, i, u)
                dve.wait_ge(s_gh, (step + 1) * GI)
                dve.sem_inc(s_turn, 1)

            with dve.Fori(0, STEPS - 1) as st:
                plain(st + 2, True, blk_d)
                state_step(st, True)
            plain(STEPS + 1, True, blk_d)
            state_step(STEPS - 1, False)

            def add_state(i):
                for q in range(2):
                    dve.wait_ge(s_t, i * 2 + (3 * NBLK + q + 1))
                    b = i * 2 + q
                    v.tensor_tensor(x_block(b), x_block(b), PS[q][:, 0:D], ALU.add).then_inc(s_xa, 1)
            steps(dve, TBI, add_state)
            dve.wait_ge(s_xa, NBLK)

            def nodes2(i, ask):
                bs = bass.ds(i * NPB, NPB)
                ch.done(v.tensor_copy(t1d, X[:, bs, :]))
                ch.wait()
                normalize(X[:, bs, :], ask)
            node_phase(ASK[2], 2, nodes2)
            new_x_complete()

            dve.wait_ge(s_w, W3)
            for r in range(NREL):
                w_r = wide_w[:, r * D:(r + 1) * D]
                ts(w_r, raw_w[:, 0:D], alpha_b[:, r * NBASE:r * NBASE + 1], None, ALU.mult)
                for b in range(1, NBASE):
                    stt(w_r, raw_w[:, b * D:(b + 1) * D], alpha_b[:, r * NBASE + b:r * NBASE + b + 1], w_r,
                        ALU.mult, ALU.add)
            tt(beta_b[:, :], beta_b[:, :], bias_b[:, :], ALU.add)
            ch.done(v.memset(G[:, :, D:D + 1], 1.0))
            ch.wait()
            dve.sem_inc(s_wv, 1)
            evacuate(6, NREL * D, self_loop=True)
            plain(6, False, blk_s)

            def nodes3(i, ask):
                bs = bass.ds(i * NPB, NPB)
                ts(sm[2], ACC[:, bs, D], 1.0, None, ALU.max)
                ch.done(v.reciprocal(sm[2], sm[2]))
                ch.wait()
                tt(t1d, ACC[:, bs, 0:D], bcast(sm[2], D), ALU.mult)
                normalize(t1d, ask)
                tt(t1d, t1d, rows(gamma_b), ALU.mult)
                tt(t1d, t1d, rows(beta_b), ALU.add)
                tt(t1d, t1d, X[:, bs, :], ALU.add)
                normalize(X[:, bs, :], ask)
            node_phase(ASK[3], 4, nodes3)
            dve.sem_inc(s_on, 1)


_INS = ['x', 'src', 'dst', 'edge_attr_4', 'edge_type_8',
        'L0_gnn_W', 'L0_gnn_a_src', 'L0_gnn_a_dst', 'L0_gnn_bias',
        'L1_gnn_W', 'L1_gnn_att_src', 'L1_gnn_att_dst', 'L1_gnn_bias', 'L1_gnn_gamma', 'L1_gnn_beta',
        'L2_gnn_W_edge', 'L2_gnn_b_edge', 'L2_gnn_W_ih', 'L2_gnn_W_hh', 'L2_gnn_b_ih', 'L2_gnn_b_hh',
        'L3_gnn_weight', 'L3_gnn_alpha', 'L3_gnn_bias', 'L3_gnn_weight_self_loop', 'L3_gnn_ln_gamma',
        'L3_gnn_ln_beta']


def kernel(**inputs):
    import numpy as _np
    import concourse.bacc as _bacc
    from concourse import mybir as _mybir
    from concourse.bass_utils import run_bass_kernel_spmd as _run

    nc = _bacc.Bacc("TRN2", target_bir_lowering=False, num_devices=1)
    arrays, args = {}, []
    for name in _INS:
        a = _np.ascontiguousarray(inputs[name])
        arrays[f"in_{name}"] = a
        args.append(nc.dram_tensor(f"in_{name}", a.shape, _mybir.dt.from_np(a.dtype), kind="ExternalInput").ap())
    args.append(nc.dram_tensor("out_x", (N, D), F32, kind="ExternalOutput").ap())
    build(nc, *args)
    r = _run(nc, [arrays], core_ids=[0])
    return r.results[0]["out_x"]
```
